# Optimizing a Trainium2 kernel written in Bass

```python
import numpy as np
import jax
import jax.numpy as jnp

def _softmax(x, axis=-1):
    return jax.nn.softmax(x, axis=axis)

def _gelu(x):
    return jax.nn.gelu(x, approximate=True)

def _silu(x):
    return jax.nn.silu(x)

def _sigmoid(x):
    return jax.nn.sigmoid(x)

def _layernorm(x, axis=-1, eps=1e-05):
    m = jnp.mean(x, axis=axis, keepdims=True)
    v = jnp.var(x, axis=axis, keepdims=True)
    return (x - m) / jnp.sqrt(v + eps)

def _scatter_add(tgt, idx, src, axis=0):
    return tgt.at[idx].add(src)

def _segment_sum(src, seg, n):
    return jax.ops.segment_sum(src, seg, n)
kernel_name = 'mk_xattn_ffn_d1_seqx_r2_d04c1f'

def setup_inputs(seed: int=0):
    np.random.seed(seed)
    _w = jnp.asarray

    def _rec_inputs():
        import jax
        import jax.numpy as jnp
        _rk = jax.random.key(seed)
        x = 0.0002417 + 0.9998 * jax.random.normal(jax.random.fold_in(_rk, 1), (8, 512, 512), jnp.float32)
        _lenS = 512 - jax.random.randint(jax.random.fold_in(_rk, 7), (8,), 0, max(1, 512 // 4) + 1, jnp.int32)
        _lenS2 = 77 - jax.random.randint(jax.random.fold_in(_rk, 8), (8,), 0, max(1, 77 // 4) + 1, jnp.int32)
        _ctx_1024P = jax.random.normal(jax.random.fold_in(_rk, 11), (8, 16, 512), jnp.float32)
        _ctx_1024c = jax.random.dirichlet(jax.random.fold_in(_rk, 511), 0.3 * jnp.ones((16,), jnp.float32), (8, 77))
        _ctx_1024t = jnp.einsum('bsk,bkd->bsd', _ctx_1024c, _ctx_1024P)
        _ctx_1024t = _ctx_1024t * jax.lax.rsqrt(jnp.mean(jnp.square(_ctx_1024t)) + 1e-12) * 0.953939
        ctx_1024 = -0.000125008 + 0.999885 * (_ctx_1024t + 0.3 * jax.random.normal(jax.random.fold_in(_rk, 611), (8, 77, 512), jnp.float32))
        _validS = jnp.arange(512)[None, :] < _lenS[:, None]
        _validS2 = jnp.arange(77)[None, :] < _lenS2[:, None]
        _causal = jnp.tril(jnp.ones((512, 512), dtype=bool))
        mask_BxSxS2_bk1 = jnp.broadcast_to(_validS2[:, None, :], (8, 512, 77))
        return (x, ctx_1024, mask_BxSxS2_bk1)
    x, ctx_1024, mask_BxSxS2_bk1 = _rec_inputs()

    def _L0_xattn_setup():
        import jax, jax.numpy as jnp
        import numpy as np
        NEG_INF = -1000000000.0
        key = jax.random.key(seed)
        kv, kk, kq, km, kw, kb = jax.random.split(key, 6)
        B, Lq, Lk, D = (8, 512, 2048, 512)
        v = jax.random.normal(kv, (B, Lk, D), dtype=jnp.float32)
        k = jax.random.normal(kk, (B, Lk, D), dtype=jnp.float32)
        q = jax.random.normal(kq, (B, Lq, D), dtype=jnp.float32)
        mask = jax.random.randint(km, (B, Lq, Lk), 0, 2) > 0
        W_merge = jax.random.normal(kw, (D, D), dtype=jnp.float32) / np.sqrt(D)
        b_merge = jax.random.normal(kb, (D,), dtype=jnp.float32) * 0.02
        return {'v': v, 'k': k, 'q': q, 'mask': mask, 'W_merge': W_merge, 'b_merge': b_merge}
    _L0_xattn_all = _L0_xattn_setup()
    _L0_xattn_in = {k: v for k, v in _L0_xattn_all.items() if k in ('W_merge', 'b_merge')}
    del _L0_xattn_all

    def _L0_ffn_setup():
        import jax, jax.numpy as jnp
        import numpy as np
        HIDDEN = 512
        HEAD_DIM = 64
        N_EXPERTS = 16
        MIN_EXPERTS = 2
        B, T = (4, 1024)

        def _normalize(x, axis):
            n = jnp.sqrt(jnp.sum(x * x, axis=axis, keepdims=True))
            return x / jnp.maximum(n, 1e-12)

        def _ste(x):
            hard = jax.lax.stop_gradient((x > 0).astype(x.dtype))
            return hard + x - jax.lax.stop_gradient(x)

        def _gating(hidden_states, sim_matrix, gates):
            b, t, c = hidden_states.shape
            flat = hidden_states.reshape(b * t, c)
            logits = _normalize(flat, -1) @ _normalize(sim_matrix, 0) - jax.nn.sigmoid(gates)
            gated = jax.nn.relu(logits)
            mask = _ste(gated)
            inactive = jnp.sum(mask, axis=1) == 0
            _, fb_idx = jax.lax.top_k(logits, MIN_EXPERTS)
            fb = jnp.zeros_like(mask).at[jnp.arange(b * t)[:, None], fb_idx].set(1.0)
            fb_applied = inactive[:, None] & (fb > 0)
            mask = jnp.where(fb_applied, 1.0, mask)
            masked_logits = jnp.where(mask > 0, gated, -jnp.inf)
            return jax.nn.softmax(masked_logits, axis=-1).reshape(b, t, -1)
        key = jax.random.key(seed)
        ks = jax.random.split(key, 6)
        xav_qkv = float(np.sqrt(6.0 / (HIDDEN + HEAD_DIM)))
        return {'hidden_states': jax.random.normal(ks[0], (B, T, HIDDEN), dtype=jnp.float32), 'sim_matrix': jax.random.normal(ks[1], (HIDDEN, N_EXPERTS), dtype=jnp.float32), 'gates': jnp.zeros((N_EXPERTS,), dtype=jnp.float32), 'q_proj': jax.random.uniform(ks[2], (N_EXPERTS, HIDDEN, HEAD_DIM), jnp.float32, -xav_qkv, xav_qkv), 'k_proj': jax.random.uniform(ks[3], (N_EXPERTS, HIDDEN, HEAD_DIM), jnp.float32, -xav_qkv, xav_qkv), 'v_proj': jax.random.uniform(ks[4], (N_EXPERTS, HIDDEN, HEAD_DIM), jnp.float32, -xav_qkv, xav_qkv), 'o_proj': jax.random.uniform(ks[5], (N_EXPERTS, HEAD_DIM, HIDDEN), jnp.float32, -xav_qkv, xav_qkv)}
    _L0_ffn_all = _L0_ffn_setup()
    _L0_ffn_in = {k: v for k, v in _L0_ffn_all.items() if k in ('sim_matrix', 'gates', 'q_proj', 'k_proj', 'v_proj', 'o_proj')}
    del _L0_ffn_all
    return {'x': x, 'ctx_1024': ctx_1024, 'mask_BxSxS2_bk1': mask_BxSxS2_bk1, 'L0_xattn_W_merge': _L0_xattn_in['W_merge'], 'L0_xattn_b_merge': _L0_xattn_in['b_merge'], 'L0_ffn_sim_matrix': _L0_ffn_in['sim_matrix'], 'L0_ffn_gates': _L0_ffn_in['gates'], 'L0_ffn_q_proj': _L0_ffn_in['q_proj'], 'L0_ffn_k_proj': _L0_ffn_in['k_proj'], 'L0_ffn_v_proj': _L0_ffn_in['v_proj'], 'L0_ffn_o_proj': _L0_ffn_in['o_proj']}

def reference(x, ctx_1024, mask_BxSxS2_bk1, L0_xattn_W_merge, L0_xattn_b_merge, L0_ffn_sim_matrix, L0_ffn_gates, L0_ffn_q_proj, L0_ffn_k_proj, L0_ffn_v_proj, L0_ffn_o_proj):
    import jax
    import jax.numpy as jnp

    def _L0_xattn_ref(v, k, q, mask, W_merge, b_merge):
        import jax, jax.numpy as jnp
        import numpy as np
        NEG_INF = -1000000000.0
        d_k = q.shape[-1]
        scale = 1.0 / jnp.sqrt(jnp.asarray(d_k, dtype=q.dtype))
        scores = jnp.einsum('bqd,bkd->bqk', q, k) * scale
        scores = jnp.where(mask, jnp.asarray(NEG_INF, dtype=scores.dtype), scores)
        att_map = jax.nn.softmax(scores, axis=-1)
        atted = jnp.einsum('bqk,bkd->bqd', att_map, v)
        atted = jnp.swapaxes(atted, -1, -2)
        return jnp.einsum('bdl,ol->bdo', atted, W_merge) + b_merge

    def _L0_ffn_ref(hidden_states, sim_matrix, gates, q_proj, k_proj, v_proj, o_proj):
        import jax, jax.numpy as jnp
        import numpy as np
        HIDDEN = 512
        HEAD_DIM = 64
        N_EXPERTS = 16
        MIN_EXPERTS = 2
        B, T = (4, 1024)

        def _normalize(x, axis):
            n = jnp.sqrt(jnp.sum(x * x, axis=axis, keepdims=True))
            return x / jnp.maximum(n, 1e-12)

        def _ste(x):
            hard = jax.lax.stop_gradient((x > 0).astype(x.dtype))
            return hard + x - jax.lax.stop_gradient(x)

        def _gating(hidden_states, sim_matrix, gates):
            b, t, c = hidden_states.shape
            flat = hidden_states.reshape(b * t, c)
            logits = _normalize(flat, -1) @ _normalize(sim_matrix, 0) - jax.nn.sigmoid(gates)
            gated = jax.nn.relu(logits)
            mask = _ste(gated)
            inactive = jnp.sum(mask, axis=1) == 0
            _, fb_idx = jax.lax.top_k(logits, MIN_EXPERTS)
            fb = jnp.zeros_like(mask).at[jnp.arange(b * t)[:, None], fb_idx].set(1.0)
            fb_applied = inactive[:, None] & (fb > 0)
            mask = jnp.where(fb_applied, 1.0, mask)
            masked_logits = jnp.where(mask > 0, gated, -jnp.inf)
            return jax.nn.softmax(masked_logits, axis=-1).reshape(b, t, -1)
        b, t, c = hidden_states.shape
        rw = _gating(hidden_states, sim_matrix, gates)
        q = jnp.einsum('bte,bted->btd', rw, jnp.einsum('btc,ecd->bted', hidden_states, q_proj))
        k = jnp.einsum('bte,bted->btd', rw, jnp.einsum('btc,ecd->bted', hidden_states, k_proj))
        v = jnp.einsum('bte,bted->btd', rw, jnp.einsum('btc,ecd->bted', hidden_states, v_proj))
        scale = 1.0 / jnp.sqrt(jnp.asarray(HEAD_DIM, dtype=q.dtype))
        scores = jnp.einsum('bqd,bkd->bqk', q, k) * scale
        causal = jnp.tril(jnp.ones((t, t), dtype=bool))
        scores = jnp.where(causal, scores, -jnp.inf)
        attn = jnp.einsum('bqk,bkd->bqd', jax.nn.softmax(scores, axis=-1), v)
        mixed = attn[:, :, None, :] * rw[..., None]
        return jnp.einsum('bted,edc->btc', mixed, o_proj)
    x = x + _L0_xattn_ref(ctx_1024, ctx_1024, _layernorm(x, axis=-1), mask_BxSxS2_bk1, L0_xattn_W_merge, L0_xattn_b_merge)
    x = x + _L0_ffn_ref(_layernorm(x, axis=-1), L0_ffn_sim_matrix, L0_ffn_gates, L0_ffn_q_proj, L0_ffn_k_proj, L0_ffn_v_proj, L0_ffn_o_proj)
    return x

_drawn_inputs = setup_inputs


def setup_inputs(seed=0):
    import zlib

    import numpy as np

    out = dict(_drawn_inputs(seed))
    spreads = {'L0_ffn_gates': (0.0, 0.1)}
    factors = {'L0_xattn_b_merge': 2.856}
    for name, (base, spread) in spreads.items():
        noise = np.random.default_rng([zlib.crc32(name.encode()), seed]).standard_normal(out[name].shape)
        drawn = base * np.exp(spread * noise) if base else spread * noise
        out[name] = jnp.asarray(drawn.astype(out[name].dtype))
    for name, factor in factors.items():
        out[name] = (out[name] * factor).astype(out[name].dtype)
    return out
```

```python
from contextlib import ExitStack

import concourse.bass as bass
from concourse import mybir

ALU = mybir.AluOpType
ACT = mybir.ActivationFunctionType
AX = mybir.AxisListType
F32 = mybir.dt.float32
F32R = mybir.dt.float32r
U8 = mybir.dt.uint8

P = 128
NEG_INF = -1.0e9
CAUSAL_FILL = -1.0e30
LN_EPS = 1e-5
NORM_FLOOR = 1e-12
HEAD_SCALE = 0.125

SCORES_AT = {0: 0, 3: 1, 6: 2, 9: 3}
PROBS_T_AT = {3: 0, 6: 1, 9: 2, 12: 3}
VALUES_AT = {5: 0, 8: 1, 11: 2, 14: 3}
MIX_AT = {6: 0, 9: 1, 19: 2, 23: 3}
QK_T_AT = {1: 3, 14: 0, 21: 1, 30: 2}
MIXED_T_AT = {14: (0, 0), 16: (0, 1), 19: (1, 0), 20: (1, 1), 23: (2, 0), 24: (2, 1), 27: (3, 0), 28: (3, 1)}
PROJECT_AT = {16: (0, 0), 18: (0, 1), 21: (1, 0), 22: (1, 1), 25: (2, 0), 26: (2, 1), 29: (3, 0), 30: (3, 1)}
STATS_SLOT, NORM_SLOT, H_T_SLOT, LOGITS_SLOT = 0, 1, 2, 4


class Seq:

    def __init__(self):
        self.base, self.k, self.static = 0, 0, 0

    def step(self):
        self.k += 1
        return self.base + self.k

    def now(self):
        return self.base + self.k

    def bank(self):
        return (self.static + self.k - 1) % 2

    def enter(self, turn, per):
        assert per % 2 == 0
        self.first = self.base + self.k
        self.base, self.static, self.k = self.first + per * turn, self.first, 0

    def leave(self, per, turns):
        assert self.k == per, (self.k, per)
        self.base = self.static = self.first + per * turns
        self.k = 0


def products(a, b):
    return ((a[0], b[0]), (a[0], b[1]), (a[1], b[0]))


def cross_attention_then_experts_kernel(nc, x, ctx_in, mask, merge_t, bias, sim, gates, w_qkv, w_o, out):
    B, S, D = x.shape
    C = ctx_in.shape[1]
    E = sim.shape[1]
    DH = w_qkv.shape[2] // E // 3
    TILES = S // P
    KC = D // P
    Q3 = 3 * DH
    PAIRS = E // 2
    SLOTS = TILES * PAIRS
    OC = E * DH // P
    HALF = OC // 2
    CP = C + 1
    CE = CP + CP % 2
    assert TILES == 4 and KC == 4 and PAIRS == 8 and DH == 64 and SLOTS == 32 and B == 8
    W_COLS = w_qkv.shape[1] * w_qkv.shape[2]
    W_PIECE = W_COLS // B
    REV_TOP = float(E)

    x2_dram = nc.dram_tensor("x2_scratch", (B, S, D), F32, kind="Internal").ap()

    whole = ExitStack()
    with whole:
        def alloc(stack):
            def sb(name, shape, dt=F32):
                return stack.enter_context(nc.sbuf_tensor(name, shape, dt))

            def ps(name):
                return stack.enter_context(nc.psum_tensor(name, [P, 512], F32))

            def sem(name):
                return stack.enter_context(nc.semaphore(name))

            def pair(name, shape):
                return (sb(name + "_hi", shape, F32R), sb(name + "_lo", shape, F32R))
            return sb, ps, sem, pair

        sb, _, sem, pair = alloc(whole)
        Wqkv = pair("Wqkv", [P, W_COLS])
        simn = pair("simn", [P, KC, E])
        ident = sb("ident", [P, P])
        ident_r = sb("ident_r", [P, P], F32R)
        causal_r = sb("causal_r", [P, P], F32R)
        rev = sb("rev", [P, E])
        neg_sig = sb("neg_sig", [P, E])
        neg_half = sb("neg_half", [P, TILES])
        const_ready = sem("const_ready")

        first = ExitStack()
        with first:
            sb, ps, sem, pair = alloc(first)
            X = [sb(f"X{p}", [P, TILES, D]) for p in range(2)]
            CTX = [sb(f"CTX{p}", [C, D]) for p in range(2)]
            ctx = [pair(f"ctx{p}", [CP, D]) for p in range(2)]
            MASK = [sb(f"MASK{p}", [P, TILES, C], U8) for p in range(2)]
            ctx_centred = sb("ctx_centred", [C, D])
            ctxT = pair("ctxT", [P, KC, CE])
            xT = [pair(f"xT{p}", [P, S]) for p in range(2)]
            keep = sb("keep", [P, TILES, C])
            fill = sb("fill", [P, TILES, C])
            scores = sb("scores", [P, TILES, C])
            E_un = sb("E_un", [P, TILES, C])
            att = pair("att", [P, TILES, CE])
            G = pair("G", [CP, D])
            mergeT = pair("mergeT", [P, KC, D])
            stage = [sb(f"stage{p}", [P, W_PIECE]) for p in range(2)]
            sim_f = sb("sim_f", [P, KC, E])
            sim_sq = sb("sim_sq", [P, KC, E])
            sim_ss = sb("sim_ss", [P, E])
            sim_rn = sb("sim_rn", [P, E])
            half_e = sb("half_e", [P, E])
            ones_f = sb("ones_f", [P, P])
            gate_e = sb("gate_e", [P, E])
            bias_f = sb("bias_f", [1, D])
            bias_p = pair("bias_p", [1, D])
            causal_f = sb("causal_f", [P, P])
            stats = sb("stats", [P, TILES, 6])
            mv = sb("mv", [P, TILES, 2])
            var_in = sb("var_in", [P, TILES])
            row_scale = [sb(f"row_scale{p}", [P, TILES]) for p in range(2)]
            ctx_mean = sb("ctx_mean", [C, 2])
            neg_max = sb("neg_max", [P, TILES])
            row_sum = sb("row_sum", [P, TILES])
            row_inv = sb("row_inv", [P, TILES])

            psXT = [ps(f"psXT{p}") for p in range(2)]
            psCT = ps("psCT")
            psS = ps("psS")
            psG = ps("psG")
            psX2 = [ps(f"psX2{p}") for p in range(2)]
            psK = ps("psK")
            psCT_v = psCT[:, 0:KC * CE].rearrange("p (c k) -> p c k", c=KC)
            psS_v = psS[:, 0:TILES * CE].rearrange("p (t k) -> p t k", t=TILES)

            ld_x = [sem(f"ld_x{p}") for p in range(2)]
            ld_ctx = [sem(f"ld_ctx{p}") for p in range(2)]
            ld_mask = [sem(f"ld_mask{p}") for p in range(2)]
            ld_w = [sem(f"ld_w{p}") for p in range(2)]
            ld_merge = sem("ld_merge")
            ld_sim = sem("ld_sim")
            ld_gates = sem("ld_gates")
            ld_bias = sem("ld_bias")
            st_x2 = [sem(f"st_x2{p}") for p in range(2)]
            bias_placed = sem("bias_placed")
            pool_init = sem("pool_init")
            dve_init = sem("dve_init")
            act_init = sem("act_init")
            sim_normed = sem("sim_normed")
            sim_summed = sem("sim_summed")
            merge_hi = sem("merge_hi")
            merge_lo = sem("merge_lo")
            w_hi = sem("w_hi")
            w_lo = sem("w_lo")
            ctx_hi = sem("ctx_hi")
            ctx_lo = sem("ctx_lo")
            centred = sem("centred")
            ctxT_moved = sem("ctxT_moved")
            ctxT_hi = sem("ctxT_hi")
            ctxT_lo = sem("ctxT_lo")
            xT_moved = sem("xT_moved")
            xT_hi = sem("xT_hi")
            xT_lo = sem("xT_lo")
            xT_used = sem("xT_used")
            scores_read = sem("scores_read")
            mask_ready = sem("mask_ready")
            var_ready = sem("var_ready")
            scale_ready = sem("scale_ready")
            max_ready = sem("max_ready")
            exp_done = sem("exp_done")
            inv_ready = sem("inv_ready")
            att_hi = sem("att_hi")
            att_lo = sem("att_lo")
            G_summed = sem("G_summed")
            G_hi = sem("G_hi")
            G_lo = sem("G_lo")
            x2_summed = sem("x2_summed")
            x2_added = sem("x2_added")
            dve_own = sem("dve_own")

            def batches(eng, step):
                step(0, 0, True, False)
                step(1, 1, True, True)
                with eng.Fori(0, (B - 2) // 2) as n:
                    for p in range(2):
                        step(2 * n + 2 + p, p, True, True)
                step(B, B % 2, False, True)

            def turns(i, p):
                return i // 2 + 1 if isinstance(i, int) else (i - p) // 2 + 1

            with nc.Block() as block:
                @block.sync
                def _(sp):
                    sp.dma_start(X[0][:], x[0].rearrange("(t p) d -> p t d", p=P)).then_inc(ld_x[0], 16)
                    sp.dma_start(CTX[0][:], ctx_in[0]).then_inc(ld_ctx[0], 16)
                    sp.dma_start(MASK[0][:], mask[0].rearrange("(t p) c -> p t c", p=P)).then_inc(ld_mask[0], 16)
                    sp.dma_start(bias_f[:], bias).then_inc(ld_bias, 16)
                    sp.dma_start(stage[0][:], merge_t[:, 0:W_PIECE]).then_inc(ld_merge, 16)
                    sp.dma_start(stage[1][:, 0:KC * D - W_PIECE], merge_t[:, W_PIECE:KC * D]).then_inc(ld_merge, 16)
                    sp.dma_start(sim_f[:], sim.rearrange("(c p) e -> p c e", p=P)).then_inc(ld_sim, 16)
                    sp.dma_start(gate_e[:], gates.partition_broadcast(P)).then_inc(ld_gates, 16)
                    sp.dma_start(X[1][:], x[1].rearrange("(t p) d -> p t d", p=P)).then_inc(ld_x[1], 16)
                    sp.dma_start(CTX[1][:], ctx_in[1]).then_inc(ld_ctx[1], 16)
                    sp.dma_start(MASK[1][:], mask[1].rearrange("(t p) c -> p t c", p=P)).then_inc(ld_mask[1], 16)
                    sp.wait_ge(act_init, 1)
                    sp.dma_start(G[0][C:CP, :].bitcast(F32), bias_p[0][:].bitcast(F32)).then_inc(bias_placed, 16)
                    sp.wait_ge(dve_init, 1)
                    sp.dma_start(G[1][C:CP, :].bitcast(F32), bias_p[1][:].bitcast(F32)).then_inc(bias_placed, 16)
                    sp.wait_ge(merge_hi, 2)
                    sp.wait_ge(merge_lo, 2)

                    def step(i, p, front, back):
                        q = 1 - p
                        if front:
                            if not isinstance(i, int) or i >= 2:
                                sp.wait_ge(w_hi, i - 1)
                                sp.wait_ge(w_lo, i - 1)
                            sp.dma_start(stage[p][:], piece(w_qkv, i)).then_inc(ld_w[p], 16)
                        if back:
                            sp.wait_ge(x2_added, TILES * i)
                            dst = x2_dram[one(i - 1)].rearrange("b (t p) d -> p (b t) d", p=P)
                            sp.dma_start(dst, X[q][:]).then_inc(st_x2[q], 16)
                        if back and front and not (isinstance(i, int) and i + 1 >= B):
                            sp.wait_ge(st_x2[q], 16 * turns(i - 1, q))
                            sp.dma_start(X[q][:], x[one(i + 1)].rearrange("b (t p) d -> p (b t) d", p=P)
                                         ).then_inc(ld_x[q], 16)
                            sp.wait_ge(centred, i)
                            sp.wait_ge(ctx_lo, i)
                            sp.dma_start(CTX[q][:], ctx_in[one(i + 1)].rearrange("b c d -> (b c) d")
                                         ).then_inc(ld_ctx[q], 16)
                            sp.wait_ge(mask_ready, i)
                            sp.dma_start(MASK[q][:], mask[one(i + 1)].rearrange("b (t p) c -> p (b t) c", p=P)
                                         ).then_inc(ld_mask[q], 16)

                    def one(i):
                        return bass.ds(i, 1)

                    def piece(w, i):
                        flat = w.rearrange("p c n -> p (c n)")
                        return flat[:, bass.ds(i * W_PIECE, W_PIECE)]

                    step(0, 0, True, False)
                    step(1, 1, True, True)
                    with sp.Fori(0, (B - 4) // 2) as n:
                        for p in range(2):
                            step(2 * n + 2 + p, p, True, True)
                    step(B - 2, 0, True, True)
                    step(B - 1, 1, True, True)
                    step(B, 0, False, True)
                    for p in range(2):
                        sp.wait_ge(st_x2[p], 16 * (B // 2))

                @block.gpsimd
                def _(pool):
                    pool.memset(neg_half[:], -0.5).then_inc(pool_init, 1)
                    pool.memset(half_e[:], -0.5).then_inc(pool_init, 1)
                    pool.memset(ones_f[:], 1.0).then_inc(pool_init, 1)
                    pool.wait_ge(pool_init, 3)
                    pool.affine_select(out=ident[:], in_=ones_f[:], compare_op=ALU.is_equal, fill=0.0, base=0,
                                       pattern=[[-1, P]], channel_multiplier=1).then_inc(pool_init, 1)
                    pool.memset(causal_f[:], 0.0).then_inc(pool_init, 1)
                    pool.wait_ge(pool_init, 5)
                    pool.affine_select(out=causal_f[:], in_=causal_f[:], compare_op=ALU.is_ge, fill=CAUSAL_FILL,
                                       base=0, pattern=[[-1, P]], channel_multiplier=1).then_inc(pool_init, 1)
                    pool.iota(rev[:], pattern=[[-1, E]], base=E, channel_multiplier=0,
                              allow_small_or_imprecise_dtypes=True).then_inc(pool_init, 1)

                    def step(i, p, front, back):
                        if not front:
                            return
                        pool.wait_ge(ld_mask[p], 16 * turns(i, p))
                        if not isinstance(i, int) or i >= 1:
                            pool.wait_ge(max_ready, i)
                        pool.wait_ge(var_ready, i + 1)
                        pool.tensor_tensor(row_scale[p][:], var_in[:], neg_half[:], ALU.pow).then_inc(scale_ready, 1)
                        pool.tensor_scalar(keep[:], MASK[p][:], -1.0, 1.0, ALU.mult, ALU.add)
                        pool.tensor_scalar(fill[:], MASK[p][:], NEG_INF, None, ALU.mult).then_inc(mask_ready, 1)
                        pool.wait_ge(ctx_hi, i + 1)
                        pool.tensor_tensor(ctx[p][1][0:C, :], CTX[p][:], ctx[p][0][0:C, :].bitcast(F32),
                                           ALU.subtract).then_inc(ctx_lo, 1)
                        pool.wait_ge(w_hi, i + 1)
                        dst = bass.ds(i * W_PIECE, W_PIECE)
                        pool.tensor_tensor(Wqkv[1][:, dst], stage[p][:], Wqkv[0][:, dst].bitcast(F32),
                                           ALU.subtract).then_inc(w_lo, 1)

                    pool.wait_ge(sim_summed, 2)
                    pool.tensor_tensor(sim_rn[:], sim_ss[:], half_e[:], ALU.pow).then_inc(sim_normed, 1)
                    step(0, 0, True, False)
                    step(1, 1, True, True)
                    with pool.Fori(0, (B - 2) // 2) as n:
                        for p in range(2):
                            step(2 * n + 2 + p, p, True, True)

                @block.scalar
                def _(act):
                    act.wait_ge(ld_bias, 16)
                    act.activation(bias_p[0][:], bias_f[:], ACT.Copy).then_inc(act_init, 1)
                    act.wait_ge(ld_merge, 32)
                    m = mergeT[0][:].rearrange("p c n -> p (c n)")
                    act.activation(m[:, 0:W_PIECE], stage[0][:], ACT.Copy).then_inc(merge_hi, 1)
                    act.activation(m[:, W_PIECE:KC * D], stage[1][:, 0:KC * D - W_PIECE], ACT.Copy
                                   ).then_inc(merge_hi, 1)
                    act.wait_ge(ld_gates, 16)
                    act.activation(gate_e[:], gate_e[:], ACT.Exp, scale=-1.0).then_inc(act_init, 1)
                    act.wait_ge(pool_init, 6)
                    act.activation(ident_r[:], ident[:], ACT.Copy).then_inc(const_ready, 1)
                    act.activation(causal_r[:], causal_f[:], ACT.Copy).then_inc(const_ready, 1)
                    act.wait_ge(sim_normed, 2)
                    act.activation(simn[0][:], sim_f[:], ACT.Copy).then_inc(sim_normed, 1)

                    def step(i, p, front, back):
                        q = 1 - p
                        if back:
                            act.wait_ge(max_ready, i)
                            for t in range(TILES):
                                act.activation(E_un[:, t, :], scores[:, t, :], ACT.Exp, bias=neg_max[:, t:t + 1],
                                               accum_out=row_sum[:, t:t + 1]).then_inc(exp_done, 1)
                            act.wait_ge(inv_ready, i)
                            if not isinstance(i, int) or i >= 2:
                                act.wait_ge(G_summed, i - 1)
                            for t in range(TILES):
                                act.activation(att[0][:, t, 0:C], E_un[:, t, :], ACT.Copy,
                                               scale=row_inv[:, t:t + 1]).then_inc(att_hi, 1)
                        if front:
                            act.wait_ge(ld_ctx[p], 16 * turns(i, p))
                            if not isinstance(i, int) or i >= 2:
                                act.wait_ge(x2_summed, TILES * (i - 1))
                            else:
                                act.wait_ge(dve_init, 2)
                            act.activation(ctx[p][0][0:C, :], CTX[p][:], ACT.Copy).then_inc(ctx_hi, 1)
                            act.wait_ge(ctxT_moved, i + 1)
                            if not isinstance(i, int) or i >= 1:
                                act.wait_ge(xT_used, KC * i)
                            act.activation(ctxT[0][:, :, 0:C], psCT_v[:, :, 0:C], ACT.Copy).then_inc(ctxT_hi, 1)
                            for c in range(KC):
                                act.wait_ge(xT_moved, KC * i + c + 1)
                                if not isinstance(i, int) or KC * i + c >= 2:
                                    act.wait_ge(xT_used, KC * i + c - 1)
                                act.activation(xT[c % 2][0][:], psXT[c % 2][:], ACT.Copy).then_inc(xT_hi, 1)
                            act.wait_ge(ld_w[p], 16 * turns(i, p))
                            dst = bass.ds(i * W_PIECE, W_PIECE)
                            act.activation(Wqkv[0][:, dst], stage[p][:], ACT.Copy).then_inc(w_hi, 1)
                        if back:
                            act.wait_ge(G_summed, i)
                            if not isinstance(i, int) or i >= 2:
                                act.wait_ge(x2_summed, TILES * (i - 1))
                            act.activation(G[0][0:C, :], psG[0:C, :], ACT.Copy).then_inc(G_hi, 1)

                    batches(act, step)

                @block.vector
                def _(dve):
                    own = Seq()

                    def link(ins):
                        ins.then_inc(dve_own, 1)
                        dve.wait_ge(dve_own, own.step())

                    def lo(dst, src, hi, signal):
                        dve.tensor_tensor(dst, src, hi.bitcast(F32), ALU.subtract).then_inc(signal, 1)

                    dve.wait_ge(act_init, 1)
                    lo(bias_p[1][:], bias_f[:], bias_p[0][:], dve_init)
                    for p in range(2):
                        dve.memset(ctx[p][0][:].bitcast(F32), 1.0)
                        dve.memset(ctx[p][1][:].bitcast(F32), 0.0)
                    for part in range(2):
                        dve.memset(att[part][:].bitcast(F32), 0.0)
                        last = dve.memset(ctxT[part][:].bitcast(F32), 0.0)
                    last.then_inc(dve_init, 1)
                    m = [t[:].rearrange("p c n -> p (c n)") for t in mergeT]
                    dve.wait_ge(merge_hi, 1)
                    lo(m[1][:, 0:W_PIECE], stage[0][:], m[0][:, 0:W_PIECE], merge_lo)
                    dve.wait_ge(merge_hi, 2)
                    lo(m[1][:, W_PIECE:KC * D], stage[1][:, 0:KC * D - W_PIECE], m[0][:, W_PIECE:KC * D], merge_lo)

                    def gate_constants():
                        dve.wait_ge(act_init, 2)
                        link(dve.tensor_scalar(gate_e[:], gate_e[:], 1.0, None, ALU.add))
                        link(dve.reciprocal(gate_e[:], gate_e[:]))
                        dve.tensor_scalar(neg_sig[:], gate_e[:], -1.0, None, ALU.mult).then_inc(const_ready, 1)
                        dve.wait_ge(ld_sim, 16)
                        dve.tensor_tensor(sim_sq[:], sim_f[:], sim_f[:], ALU.mult).then_inc(dve_init, 1)
                        dve.wait_ge(sim_summed, 1)
                        dve.tensor_scalar(sim_ss[:], psK[:, 0:E], NORM_FLOOR ** 2, None, ALU.max
                                          ).then_inc(sim_summed, 1)
                        dve.wait_ge(sim_normed, 1)
                        for c in range(KC):
                            last = dve.tensor_tensor(sim_f[:, c, :], sim_f[:, c, :], sim_rn[:], ALU.mult)
                        last.then_inc(sim_normed, 1)
                        dve.wait_ge(sim_normed, 3)
                        lo(simn[1][:], sim_f[:], simn[0][:], const_ready)

                    def step(i, p, front, back):
                        q = 1 - p
                        j = i - 1
                        if back:
                            dve.wait_ge(xT_used, KC * i)
                            dve.wait_ge(scale_ready, i)
                            dve.wait_ge(mask_ready, i)
                            for t in range(TILES):
                                last = dve.scalar_tensor_tensor(
                                    out=scores[:, t, :], in0=psS_v[:, t, 0:C], scalar=row_scale[q][:, t:t + 1],
                                    in1=keep[:, t, :], op0=ALU.mult, op1=ALU.mult)
                            last.then_inc(scores_read, 1)
                            dve.wait_ge(scores_read, i)
                            link(dve.tensor_tensor(scores[:], scores[:], fill[:], ALU.add))
                            dve.tensor_reduce(neg_max[:], scores[:], AX.X, ALU.max, negate=True).then_inc(max_ready, 1)
                        if front:
                            dve.wait_ge(ld_ctx[p], 16 * turns(i, p))
                            link(dve.tensor_reduce(ctx_mean[:, 0:1], CTX[p][:], AX.X, ALU.add))
                            link(dve.tensor_scalar(ctx_mean[:, 1:2], ctx_mean[:, 0:1], -1.0 / D, None, ALU.mult))
                            if not isinstance(i, int) or i >= 1:
                                dve.wait_ge(ctxT_moved, i)
                            dve.tensor_scalar(ctx_centred[:], CTX[p][:], ctx_mean[:, 1:2], None, ALU.add
                                              ).then_inc(centred, 1)
                            dve.wait_ge(ld_x[p], 16 * turns(i, p))
                            for t in range(TILES):
                                dve.bn_stats(stats[:, t, :], X[p][:, t, :])
                            dve.drain()
                            for t in range(TILES):
                                last = dve.bn_aggr(mv[:, t, :], stats[:, t, :])
                            link(last)
                            if not isinstance(i, int) or i >= 1:
                                dve.wait_ge(scale_ready, i)
                            dve.tensor_scalar(var_in[:], mv[:, :, 1], LN_EPS, float(D), ALU.add, ALU.mult
                                              ).then_inc(var_ready, 1)
                        if back:
                            dve.wait_ge(exp_done, TILES * i)
                            dve.reciprocal(row_inv[:], row_sum[:]).then_inc(inv_ready, 1)
                            for t in range(TILES):
                                dve.wait_ge(att_hi, TILES * j + t + 1)
                                last = dve.scalar_tensor_tensor(
                                    out=att[1][:, t, 0:C], in0=E_un[:, t, :], scalar=row_inv[:, t:t + 1],
                                    in1=att[0][:, t, 0:C].bitcast(F32), op0=ALU.mult, op1=ALU.subtract)
                            last.then_inc(att_lo, 1)
                        if front:
                            dve.wait_ge(ctxT_hi, i + 1)
                            lo(ctxT[1][:, :, 0:C], psCT_v[:, :, 0:C], ctxT[0][:, :, 0:C], ctxT_lo)
                            for c in range(KC):
                                dve.wait_ge(xT_hi, KC * i + c + 1)
                                lo(xT[c % 2][1][:], psXT[c % 2][:], xT[c % 2][0][:], xT_lo)
                        if back:
                            dve.wait_ge(G_hi, i)
                            lo(G[1][0:C, :], psG[0:C, :], G[0][0:C, :], G_lo)
                            for t in range(TILES):
                                dve.wait_ge(x2_summed, TILES * j + t + 1)
                                dve.tensor_tensor(X[q][:, t, :], psX2[t % 2][:], X[q][:, t, :], ALU.add
                                                  ).then_inc(x2_added, 1)

                    gate_constants()
                    step(0, 0, True, False)
                    step(1, 1, True, True)
                    per = 2 * 4
                    with dve.Fori(0, (B - 2) // 2) as n:
                        own.enter(n, per)
                        for p in range(2):
                            step(2 * n + 2 + p, p, True, True)
                        own.leave(per, (B - 2) // 2)
                    step(B, B % 2, False, True)

                @block.tensor
                def _(pe):
                    pe.wait_ge(dve_init, 3)
                    pe.wait_ge(pool_init, 3)
                    for c in range(KC):
                        last = pe.matmul(psK[:, 0:E], ones_f[:], sim_sq[:, c, :], start=(c == 0), stop=(c == KC - 1))
                    last.then_inc(sim_summed, 1)
                    pe.wait_ge(pool_init, 4)

                    def move_x(i, p, c):
                        n = KC * i + c
                        if not isinstance(i, int) or n >= 2:
                            pe.wait_ge(xT_lo, n - 1)
                        for t in range(TILES):
                            last = pe.transpose(psXT[c % 2][:, t * P:(t + 1) * P], X[p][:, t, c * P:(c + 1) * P],
                                                ident[:])
                        last.then_inc(xT_moved, 1)

                    def sum_scores(i, c):
                        pe.wait_ge(xT_lo, KC * i + c + 1)
                        if c == 0:
                            pe.wait_ge(ctxT_lo, i + 1)
                            if not isinstance(i, int) or i >= 1:
                                pe.wait_ge(scores_read, i)
                        for t in range(TILES):
                            for n, (a, b) in enumerate(products(xT[c % 2], ctxT)):
                                last = pe.matmul(psS_v[:, t, :], a[:, t * P:(t + 1) * P], b[:, c, :],
                                                 start=(c == 0 and t == 0 and n == 0), stop=(c == KC - 1 and n == 2),
                                                 skip_group_check=True)
                        last.then_inc(xT_used, 1)

                    def step(i, p, front, back):
                        q = 1 - p
                        j = i - 1
                        if front:
                            pe.wait_ge(centred, i + 1)
                            if not isinstance(i, int) or i >= 1:
                                pe.wait_ge(ctxT_lo, i)
                            for c in range(KC):
                                last = pe.transpose(psCT_v[:, c, 0:C], ctx_centred[:, c * P:(c + 1) * P],
                                                    ident[0:C, 0:C])
                            last.then_inc(ctxT_moved, 1)
                            pe.wait_ge(ld_x[p], 16 * turns(i, p))
                            move_x(i, p, 0)
                            move_x(i, p, 1)
                            sum_scores(i, 0)
                            move_x(i, p, 2)
                            sum_scores(i, 1)
                            move_x(i, p, 3)
                            sum_scores(i, 2)
                            sum_scores(i, 3)
                        if back:
                            pe.wait_ge(att_lo, i)
                            if isinstance(i, int) and i == 1:
                                pe.wait_ge(merge_lo, 2)
                                pe.wait_ge(bias_placed, 32)
                            else:
                                pe.wait_ge(G_lo, j)
                            for t in range(TILES):
                                for n, (a, b) in enumerate(products(att, mergeT)):
                                    last = pe.matmul(psG[0:CE, :], a[:, t, :], b[:, t, :],
                                                     start=(t == 0 and n == 0), stop=(t == TILES - 1 and n == 2))
                            last.then_inc(G_summed, 1)
                            pe.wait_ge(G_lo, i)
                            pe.wait_ge(ctx_lo, i)
                            for t in range(TILES):
                                n = TILES * j + t
                                if not isinstance(i, int) or n >= 2:
                                    pe.wait_ge(x2_added, n - 1)
                                for k, (a, b) in enumerate(products(ctx[q], G)):
                                    last = pe.matmul(psX2[t % 2][:], a[:, t * P:(t + 1) * P], b[:],
                                                     start=(k == 0), stop=(k == 2))
                                last.then_inc(x2_summed, 1)

                    batches(pe, step)

        experts_block(nc, whole, alloc, x2_dram, w_o, out, Wqkv, simn, ident, ident_r, causal_r, rev, neg_sig,
                      neg_half, const_ready, (B, S, D, E, DH, TILES, KC, Q3, PAIRS, SLOTS, OC, HALF))


def experts_block(nc, whole, alloc, x2_dram, w_o, out, Wqkv, simn, ident, ident_r, causal_r, rev, neg_sig,
                  neg_half, const_ready, sizes):
    B, S, D, E, DH, TILES, KC, Q3, PAIRS, SLOTS, OC, HALF = sizes
    N_TILES = B * TILES
    PW = 2 * Q3
    sb, ps, sem, pair = alloc(whole)
    Wo = pair("Wo", [P, OC, D])
    wo_stage = [sb(f"wo_stage{p}", [P, D * 2]) for p in range(2)]
    X2 = [sb(f"X2_{p}", [P, D]) for p in range(2)]
    H = [sb(f"H{p}", [P, D]) for p in range(2)]
    hT = [pair(f"hT{p}", [P, D]) for p in range(2)]
    acc = [sb(f"acc{k}", [P, Q3]) for k in range(2)]
    nat = [sb(f"nat{p}", [P, Q3]) for p in range(2)]
    qkT = pair("qkT", [DH, 2, S])
    V = pair("V", [P, TILES, DH])
    probs = [sb(f"probs{p}", [P, S]) for p in range(2)]
    probsT = pair("probsT", [P, S])
    attended = [sb(f"attended{p}", [P, DH]) for p in range(2)]
    mixed = [sb(f"mixed{p}", [P, E, DH]) for p in range(2)]
    mixedT = [pair(f"mixedT{p}", [P, HALF * P]) for p in range(2)]
    resid = [sb(f"resid{p}", [P, D]) for p in range(2)]
    RW = [sb(f"RW{p}", [P, E]) for p in range(2)]
    RW_all = sb("RW_all", [P, N_TILES * E])
    stats = sb("b_stats", [P, 6])
    mv = sb("b_mv", [P, 2])
    pow_in = sb("pow_in", [P, 2])
    pow_tmp = sb("pow_tmp", [P, 2])
    pow_out = [sb(f"pow_out{p}", [P, 2]) for p in range(2)]
    neg_mx = [sb(f"neg_mx{p}", [P, 2]) for p in range(2)]
    p_sum = [sb(f"p_sum{p}", [P, 1]) for p in range(2)]
    p_inv = sb("p_inv", [P, 1])
    logit = sb("logit", [P, E])
    rank = sb("rank", [P, E])
    pick1 = sb("pick1", [P, E])
    picks = sb("picks", [P, E])
    other = sb("other", [P, E])
    active = sb("active", [P, E])
    chosen = sb("chosen", [P, E])
    gate_in = sb("gate_in", [P, E])
    gate_exp = sb("gate_exp", [P, E])
    g1 = sb("g1", [P, 8])

    psQ = [ps(f"psQ{k}") for k in range(4)]
    psT = [ps(f"psT{k}") for k in range(2)]
    psM = ps("psM")
    psO = ps("psO")

    ld_wo = [sem(f"ld_wo{p}") for p in range(2)]
    wo_hi, wo_lo = sem("wo_hi"), sem("wo_lo")
    x2_in = [sem(f"x2_in{p}") for p in range(2)]
    res_in = [sem(f"res_in{p}") for p in range(2)]
    y_out = [sem(f"y_out{p}") for p in range(2)]
    pow_asked, pow_done = sem("pow_asked"), sem("pow_done")
    h_ready = sem("h_ready")
    moved = sem("moved")
    moved_hi = sem("moved_hi")
    moved_lo = sem("moved_lo")
    logits_summed = sem("logits_summed")
    qkv_summed = sem("qkv_summed")
    expert_added = sem("expert_added")
    nat_ready = sem("nat_ready")
    v_hi, v_lo = sem("v_hi"), sem("v_lo")
    scored = sem("scored")
    neg_max_ready = sem("neg_max_ready")
    m_free = sem("m_free")
    valued = sem("valued")
    mixed_ready = sem("mixed_ready")
    projected = sem("projected")
    y_ready = sem("y_ready")
    gate_in_ready, gate_exp_ready = sem("gate_in_ready"), sem("gate_exp_ready")
    rw_ready, rw_kept = sem("rw_ready"), sem("rw_kept")
    own2 = sem("own2")

    MOVES, M_JOBS = 20, 12
    LOOP = B - 3

    def bodies(eng, body, seqs):
        body(0, True, False, True)
        body(1, True, True, True)
        with eng.Fori(0, LOOP) as n:
            for s, per in seqs:
                s.enter(n, per)
            body(n + 2, True, True, True)
            for s, per in seqs:
                s.leave(per, LOOP)
        body(B - 1, True, True, False)
        body(B, False, True, False)

    def job_lists(k, b, qkv, attn, last_prep):
        j, g = divmod(k, PAIRS)
        prepare = qkv and (last_prep or j < TILES - 1)
        return j, g, prepare

    def tile_copies(k, qkv, attn):
        if k in QK_T_AT and (attn if k == 1 else qkv):
            return QK_T_AT[k]
        return None

    with nc.Block() as block:
        @block.sync
        def _(sp):
            for n in range(2):
                sp.dma_start(X2[n][:], x2_dram[0, n * P:(n + 1) * P, :]).then_inc(x2_in[n], 16)
            wo_flat = w_o.rearrange("p c n -> p (c n)")
            piece = 2 * D
            for n in range(OC // 2):
                if n >= 2:
                    sp.wait_ge(wo_lo, n - 1)
                    sp.wait_ge(wo_hi, n - 1)
                sp.dma_start(wo_stage[n % 2][:], wo_flat[:, n * piece:(n + 1) * piece]).then_inc(ld_wo[n % 2], 16)

            def row(dram, b, t):
                return dram.rearrange("b (t p) d -> (b t) p d", p=P)[bass.ds(TILES * b + t, 1)].rearrange(
                    "a p d -> p (a d)")

            def store_y(b, i):
                sp.wait_ge(y_ready, TILES * (b - 1) + i + 1)
                sp.dma_start(row(out, b - 1, i), resid[i % 2][:]).then_inc(y_out[i % 2], 16)

            def load_resid(b, i):
                if not isinstance(b, int) or TILES * (b - 1) + i >= 2:
                    sp.wait_ge(y_out[i % 2], 16 * (2 * (b - 1) + i // 2))
                sp.dma_start(resid[i % 2][:], row(x2_dram, b - 1, i)).then_inc(res_in[i % 2], 16)

            def body(b, qkv, attn, prep):
                for j in range(TILES):
                    if qkv and (prep or j < 2):
                        sp.wait_ge(h_ready, TILES * b + j + 1)
                        sp.dma_start(X2[j % 2][:], row(x2_dram, b, j + 2)).then_inc(x2_in[j % 2], 16)
                    if attn and j == 0:
                        load_resid(b, 0)
                        load_resid(b, 1)
                    if attn and j == 2:
                        store_y(b, 0)
                        load_resid(b, 2)
                        store_y(b, 1)
                        load_resid(b, 3)
                    if attn and j == 3:
                        store_y(b, 2)
                        store_y(b, 3)

            bodies(sp, body, [])
            for p in range(2):
                sp.wait_ge(y_out[p], 16 * (N_TILES // 2))

        @block.gpsimd
        def _(pool):
            def powers(t, p):
                pool.wait_ge(pow_asked, t + 1)
                pool.tensor_tensor(pow_out[p][:], pow_in[:], neg_half[:, 0:2], ALU.pow).then_inc(pow_done, 1)

            def keep_gates(t, p):
                pool.wait_ge(rw_ready, t + 1)
                pool.tensor_copy(RW_all[:, bass.ds(t * E, E)], RW[p][:]).then_inc(rw_kept, 1)

            powers(0, 0)
            wo_hi_f = Wo[0][:].rearrange("p c n -> p (c n)")
            wo_lo_f = Wo[1][:].rearrange("p c n -> p (c n)")
            for n in range(OC // 2):
                pool.wait_ge(wo_hi, n + 1)
                cols = slice(n * 2 * D, (n + 1) * 2 * D)
                pool.tensor_tensor(wo_lo_f[:, cols], wo_stage[n % 2][:], wo_hi_f[:, cols].bitcast(F32),
                                   ALU.subtract).then_inc(wo_lo, 1)
            keep_gates(0, 0)
            jobs = Seq()
            jobs.step()

            def body(b, qkv, attn, prep):
                values_job = {}
                for k in range(SLOTS):
                    j, g, prepare = job_lists(k, b, qkv, attn, prep)
                    t = TILES * b + j
                    if prepare and g == STATS_SLOT:
                        powers(t + 1, (j + 1) % 2)
                    if prepare and g == LOGITS_SLOT:
                        jobs.step()
                    if attn and k in SCORES_AT:
                        jobs.step()
                    if attn and k in VALUES_AT:
                        values_job[VALUES_AT[k]] = jobs.step()
                    if attn and k in MIX_AT:
                        i = MIX_AT[k]
                        a = TILES * (b - 1) + i
                        pool.wait_ge(m_free, values_job[i])
                        pool.wait_ge(rw_kept, a + 1)
                        if not isinstance(b, int) or a >= 2:
                            pool.wait_ge(projected, 2 * (a - 1))
                        rw = RW_all[:, bass.ds(a * E, E)].unsqueeze(2).broadcast_to([P, E, DH])
                        at = attended[i % 2][:].unsqueeze(1).broadcast_to([P, E, DH])
                        pool.tensor_tensor(mixed[i % 2][:], at, rw, ALU.mult).then_inc(mixed_ready, 1)
                    if prepare and g == PAIRS - 1:
                        keep_gates(t + 1, (j + 1) % 2)

            bodies(pool, body, [(jobs, M_JOBS)])

        @block.scalar
        def _(act):
            moves, jobs = Seq(), Seq()

            def copy_h(t, p):
                if not isinstance(t, int) or t >= 2:
                    act.wait_ge(qkv_summed, PAIRS * (t - 1))
                act.wait_ge(moved, moves.step())
                act.activation(hT[p][0][:], psT[moves.bank()][:], ACT.Copy).then_inc(moved_hi, 1)

            def gate(t):
                act.wait_ge(gate_in_ready, t + 1)
                act.activation(gate_exp[:], gate_in[:], ACT.Exp).then_inc(gate_exp_ready, 1)

            copy_h(0, 0)
            jobs.step()
            gate(0)
            wo_hi_f = Wo[0][:].rearrange("p c n -> p (c n)")
            for n in range(OC // 2):
                act.wait_ge(ld_wo[n % 2], 16 * (n // 2 + 1))
                act.activation(wo_hi_f[:, n * 2 * D:(n + 1) * 2 * D], wo_stage[n % 2][:], ACT.Copy
                               ).then_inc(wo_hi, 1)

            def body(b, qkv, attn, prep):
                for k in range(SLOTS):
                    j, g, prepare = job_lists(k, b, qkv, attn, prep)
                    t = TILES * b + j
                    if prepare and g == H_T_SLOT:
                        copy_h(t + 1, (j + 1) % 2)
                    if prepare and g == LOGITS_SLOT:
                        jobs.step()
                    if attn and k in PROBS_T_AT:
                        i = PROBS_T_AT[k]
                        a = TILES * (b - 1) + i
                        n = moves.step()
                        act.wait_ge(moved, n)
                        if not isinstance(b, int) or a >= 1:
                            act.wait_ge(valued, a)
                        act.activation(probsT[0][:, 0:(i + 1) * P], psT[moves.bank()][:, 0:(i + 1) * P],
                                       ACT.Copy).then_inc(moved_hi, 1)
                    if attn and k in SCORES_AT:
                        i = SCORES_AT[k]
                        jobs.step()
                        act.wait_ge(neg_max_ready, TILES * (b - 1) + i + 1)
                        act.activation(probs[i % 2][:, 0:(i + 1) * P], psM[:, 0:(i + 1) * P], ACT.Exp,
                                       bias=neg_mx[i % 2][:, 1:2], scale=HEAD_SCALE,
                                       accum_out=p_sum[i % 2][:]).then_inc(m_free, 1)
                    if attn and k in VALUES_AT:
                        jobs.step()
                    i = tile_copies(k, qkv, attn)
                    if i is not None:
                        bt = b - 1 if k == 1 else b
                        n = moves.step()
                        act.wait_ge(moved, n)
                        if not isinstance(b, int) or bt >= 1:
                            act.wait_ge(scored, TILES * bt)
                            act.wait_ge(valued, TILES * bt)
                        src = psT[moves.bank()][0:DH, 0:2 * P].rearrange("p (a s) -> p a s", a=2)
                        act.activation(qkT[0][:, :, i * P:(i + 1) * P], src, ACT.Copy).then_inc(moved_hi, 1)
                        act.activation(V[0][:, i, :], nat[i % 2][:, 2 * DH:Q3], ACT.Copy).then_inc(v_hi, 1)
                    if attn and k in MIXED_T_AT:
                        i, h = MIXED_T_AT[k]
                        a = TILES * (b - 1) + i
                        n = moves.step()
                        act.wait_ge(moved, n)
                        if not isinstance(b, int) or a >= 1:
                            act.wait_ge(projected, 2 * (a - 1) + h + 1)
                        act.activation(mixedT[h][0][:], psT[moves.bank()][:], ACT.Copy).then_inc(moved_hi, 1)
                    if prepare and g == LOGITS_SLOT + 2:
                        gate(t + 1)

            bodies(act, body, [(moves, MOVES), (jobs, M_JOBS)])

        @block.vector
        def _(dve):
            own, moves, jobs = Seq(), Seq(), Seq()

            def link(ins):
                ins.then_inc(own2, 1)
                dve.wait_ge(own2, own.step())

            def lo(dst, cols, dst_hi, view=None):
                n = moves.step()
                bank = psT[moves.bank()]
                src = bank[:, cols] if view is None else view(bank)
                dve.wait_ge(moved_hi, n)
                dve.tensor_tensor(dst, src, dst_hi.bitcast(F32), ALU.subtract).then_inc(moved_lo, 1)

            def row_stats(t, p):
                dve.wait_ge(x2_in[p], 16 * turns(t, p))
                dve.bn_stats(stats[:], X2[p][:])
                dve.drain()
                link(dve.bn_aggr(mv[:], stats[:]))
                link(dve.tensor_scalar(pow_tmp[:, 0:1], mv[:, 1:2], LN_EPS, None, ALU.add))
                link(dve.reciprocal(pow_tmp[:, 1:2], pow_tmp[:, 0:1]))
                link(dve.scalar_tensor_tensor(out=pow_tmp[:, 1:2], in0=mv[:, 1:2], scalar=float(D),
                                              in1=pow_tmp[:, 1:2], op0=ALU.mult, op1=ALU.mult))
                dve.tensor_copy(pow_in[:, 0:1], pow_tmp[:, 0:1])
                dve.tensor_scalar(pow_in[:, 1:2], pow_tmp[:, 1:2], NORM_FLOOR ** 2, None, ALU.max
                                  ).then_inc(pow_asked, 1)

            def turns(t, p):
                return t // 2 + 1 if isinstance(t, int) else (t - p) // 2 + 1

            def normalise(t, p):
                dve.wait_ge(pow_done, t + 1)
                dve.tensor_scalar(H[p][:], X2[p][:], mv[:, 0:1], pow_out[p][:, 0:1], ALU.subtract, ALU.mult
                                  ).then_inc(h_ready, 1)

            def gates_1(t, p):
                dve.wait_ge(logits_summed, t + 1)
                dve.scalar_tensor_tensor(out=logit[:], in0=psM[:, 0:E], scalar=pow_out[p][:, 1:2], in1=neg_sig[:],
                                         op0=ALU.mult, op1=ALU.add).then_inc(m_free, 1)
                dve.wait_ge(m_free, jobs.step())
                link(dve.tensor_reduce(g1[:, 0:1], logit[:], AX.X, ALU.max))
                link(dve.scalar_tensor_tensor(out=rank[:], in0=logit[:], scalar=g1[:, 0:1], in1=rev[:],
                                              op0=ALU.is_equal, op1=ALU.mult))
                link(dve.tensor_reduce(g1[:, 1:2], rank[:], AX.X, ALU.max))
                link(dve.tensor_scalar(pick1[:], rev[:], g1[:, 1:2], None, ALU.is_equal))
                link(dve.scalar_tensor_tensor(out=other[:], in0=pick1[:], scalar=CAUSAL_FILL, in1=logit[:],
                                              op0=ALU.mult, op1=ALU.add))
                link(dve.tensor_reduce(g1[:, 2:3], other[:], AX.X, ALU.max))

            def gates_2(t, p):
                link(dve.scalar_tensor_tensor(out=rank[:], in0=other[:], scalar=g1[:, 2:3], in1=rev[:],
                                              op0=ALU.is_equal, op1=ALU.mult))
                link(dve.tensor_reduce(g1[:, 3:4], rank[:], AX.X, ALU.max))
                dve.tensor_scalar(active[:], logit[:], 0.0, None, ALU.is_gt)
                dve.tensor_scalar(g1[:, 4:5], g1[:, 0:1], 0.0, None, ALU.is_le)
                dve.tensor_scalar(g1[:, 5:6], g1[:, 0:1], -1.0, 0.0, ALU.mult, ALU.min)
                link(dve.scalar_tensor_tensor(out=picks[:], in0=rev[:], scalar=g1[:, 3:4], in1=pick1[:],
                                              op0=ALU.is_equal, op1=ALU.add))
                dve.tensor_scalar(gate_in[:], logit[:], 0.0, g1[:, 5:6], ALU.max, ALU.add).then_inc(gate_in_ready, 1)
                link(dve.scalar_tensor_tensor(out=chosen[:], in0=picks[:], scalar=g1[:, 4:5], in1=active[:],
                                              op0=ALU.mult, op1=ALU.add))

            def gates_3(t, p):
                dve.wait_ge(gate_exp_ready, t + 1)
                link(dve.tensor_tensor(chosen[:], chosen[:], gate_exp[:], ALU.mult))
                link(dve.tensor_reduce(g1[:, 6:7], chosen[:], AX.X, ALU.add))
                link(dve.reciprocal(g1[:, 7:8], g1[:, 6:7]))
                if not isinstance(t, int) or t >= 2:
                    dve.wait_ge(rw_kept, t - 1)
                dve.tensor_scalar(RW[p][:], chosen[:], g1[:, 7:8], None, ALU.mult).then_inc(rw_ready, 1)

            row_stats(0, 0)
            normalise(0, 0)
            lo(hT[0][1][:], slice(0, D), hT[0][0][:])
            gates_1(0, 0)
            gates_2(0, 0)
            gates_3(0, 0)

            def body(b, qkv, attn, prep):
                for k in range(SLOTS):
                    j, g, prepare = job_lists(k, b, qkv, attn, prep)
                    t = TILES * b + j
                    tp = j % 2
                    if qkv:
                        dve.wait_ge(qkv_summed, SLOTS * b + k + 1)
                        if g == 0:
                            dve.wait_ge(rw_ready, t + 1)
                        for e in range(2):
                            src = psQ[g % 4][:, e * Q3:(e + 1) * Q3]
                            w = RW[tp][:, 2 * g + e:2 * g + e + 1]
                            if g == 0:
                                dve.tensor_scalar(acc[e][:], src, w, None, ALU.mult).then_inc(expert_added, 1)
                            else:
                                dve.wait_ge(expert_added, 2 * (SLOTS * b + k) + e - 1)
                                dve.scalar_tensor_tensor(out=acc[e][:], in0=src, scalar=w, in1=acc[e][:],
                                                         op0=ALU.mult, op1=ALU.add).then_inc(expert_added, 1)
                    if qkv and g == PAIRS - 1:
                        dve.wait_ge(expert_added, 2 * (SLOTS * b + k + 1))
                        dve.tensor_tensor(nat[tp][:], acc[0][:], acc[1][:], ALU.add).then_inc(nat_ready, 1)
                    if prepare and g == STATS_SLOT:
                        row_stats(t + 1, 1 - tp)
                    if prepare and g == NORM_SLOT:
                        normalise(t + 1, 1 - tp)
                    if prepare and g == H_T_SLOT + 1:
                        lo(hT[1 - tp][1][:], slice(0, D), hT[1 - tp][0][:])
                    if attn and k - 1 in PROBS_T_AT:
                        cols = slice(0, (PROBS_T_AT[k - 1] + 1) * P)
                        lo(probsT[1][:, cols], cols, probsT[0][:, cols])
                    i = tile_copies(k - 1, qkv, attn)
                    if i is not None:
                        bt = b - 1 if k == 2 else b
                        lo(qkT[1][:, :, i * P:(i + 1) * P], None, qkT[0][:, :, i * P:(i + 1) * P],
                           lambda bank: bank[0:DH, 0:2 * P].rearrange("p (a s) -> p a s", a=2))
                        dve.wait_ge(v_hi, TILES * bt + i + 1)
                        dve.tensor_tensor(V[1][:, i, :], nat[i % 2][:, 2 * DH:Q3], V[0][:, i, :].bitcast(F32),
                                          ALU.subtract).then_inc(v_lo, 1)
                    if attn and k - 1 in MIXED_T_AT:
                        h = MIXED_T_AT[k - 1][1]
                        lo(mixedT[h][1][:], slice(0, HALF * P), mixedT[h][0][:])
                    if prepare and g == LOGITS_SLOT + 1:
                        gates_1(t + 1, 1 - tp)
                    if prepare and g == LOGITS_SLOT + 2:
                        gates_2(t + 1, 1 - tp)
                    if prepare and g == LOGITS_SLOT + 3:
                        gates_3(t + 1, 1 - tp)
                    if attn and k in SCORES_AT:
                        i = SCORES_AT[k]
                        jobs.step()
                        dve.wait_ge(scored, TILES * (b - 1) + i + 1)
                        link(dve.tensor_reduce(neg_mx[i % 2][:, 0:1], psM[:, 0:(i + 1) * P], AX.X, ALU.max,
                                               negate=True))
                        dve.tensor_scalar(neg_mx[i % 2][:, 1:2], neg_mx[i % 2][:, 0:1], HEAD_SCALE, None, ALU.mult
                                          ).then_inc(neg_max_ready, 1)
                    if attn and k in VALUES_AT:
                        i = VALUES_AT[k]
                        a = TILES * (b - 1) + i
                        dve.wait_ge(valued, a + 1)
                        link(dve.reciprocal(p_inv[:], p_sum[i % 2][:]))
                        if not isinstance(b, int) or a >= 2:
                            dve.wait_ge(mixed_ready, a - 1)
                        jobs.step()
                        dve.tensor_scalar(attended[i % 2][:], psM[:, 0:DH], p_inv[:], None, ALU.mult
                                          ).then_inc(m_free, 1)
                    if attn and k - 1 in PROJECT_AT and PROJECT_AT[k - 1][1] == 1:
                        i = PROJECT_AT[k - 1][0]
                        a = TILES * (b - 1) + i
                        dve.wait_ge(projected, 2 * a + 2)
                        dve.wait_ge(res_in[i % 2], 16 * (2 * (b - 1) + i // 2 + 1))
                        dve.tensor_tensor(resid[i % 2][:], psO[:], resid[i % 2][:], ALU.add).then_inc(y_ready, 1)

            bodies(dve, body, [(own, OWN_STEPS), (moves, MOVES), (jobs, M_JOBS)])

        @block.tensor
        def _(pe):
            moves, jobs = Seq(), Seq()

            def next_bank(ready, value):
                n = moves.step()
                if not isinstance(n, int) or n >= 3:
                    pe.wait_ge(moved_lo, n - 2)
                pe.wait_ge(ready, value)
                return psT[moves.bank()]

            def next_job():
                n = jobs.step()
                if not isinstance(n, int) or n >= 2:
                    pe.wait_ge(m_free, n - 1)
                return n

            def move_h(t, p):
                bank = next_bank(h_ready, t + 1)
                for c in range(KC):
                    last = pe.transpose(bank[:, c * P:(c + 1) * P], H[p][:, c * P:(c + 1) * P], ident[:])
                last.then_inc(moved, 1)

            def sum_logits(t, p, h_moved):
                next_job()
                pe.wait_ge(moved_lo, h_moved)
                for c in range(KC):
                    for n, (a, b) in enumerate(products(hT[p], simn)):
                        last = pe.matmul(psM[:, 0:E], a[:, c * P:(c + 1) * P], b[:, c, :],
                                         start=(c == 0 and n == 0), stop=(c == KC - 1 and n == 2))
                last.then_inc(logits_summed, 1)

            move_h(0, 0)
            sum_logits(0, 0, moves.now())
            Wv = [w[:].rearrange("p (c n) -> p c n", c=KC) for w in Wqkv]

            def body(b, qkv, attn, prep):
                before = moves.now()
                h_moved = qk3_moved = None
                probs_moved, scores_job, mixed_moved = {}, {}, {}
                for k in range(SLOTS):
                    j, g, prepare = job_lists(k, b, qkv, attn, prep)
                    t = TILES * b + j
                    tp = j % 2
                    if qkv:
                        n = SLOTS * b + k
                        if not isinstance(b, int) or n >= 4:
                            pe.wait_ge(expert_added, 2 * (n - 3))
                        for c in range(KC):
                            for m, (x, w) in enumerate(products(hT[tp], Wv)):
                                last = pe.matmul(psQ[g % 4][:, 0:PW], x[:, c * P:(c + 1) * P],
                                                 w[:, c, g * PW:(g + 1) * PW],
                                                 start=(c == 0 and m == 0), stop=(c == KC - 1 and m == 2))
                        last.then_inc(qkv_summed, 1)
                    if prepare and g == H_T_SLOT:
                        move_h(t + 1, 1 - tp)
                        h_moved = moves.now()
                    if prepare and g == LOGITS_SLOT:
                        sum_logits(t + 1, 1 - tp, h_moved)
                    if attn and k in PROBS_T_AT:
                        i = PROBS_T_AT[k]
                        bank = next_bank(m_free, scores_job[i])
                        for s in range(i + 1):
                            last = pe.transpose(bank[:, s * P:(s + 1) * P], probs[i % 2][:, s * P:(s + 1) * P],
                                                ident[:])
                        last.then_inc(moved, 1)
                        probs_moved[i] = moves.now()
                    if attn and k in SCORES_AT:
                        i = SCORES_AT[k]
                        scores_job[i] = next_job()
                        if i == 0:
                            pe.wait_ge(moved_lo, before)
                        if i == TILES - 1:
                            pe.wait_ge(moved_lo, qk3_moved)
                        cols = slice(0, (i + 1) * P)
                        for n, (q, kk) in enumerate(products(qkT, qkT)):
                            last = pe.matmul(psM[:, cols], q[:, 0, i * P:(i + 1) * P], kk[:, 1, cols],
                                             start=(n == 0), stop=(n == 2), skip_group_check=True)
                            if n == 0:
                                pe.matmul(psM[:, i * P:(i + 1) * P], ident_r[:], causal_r[:], start=False,
                                          stop=False, skip_group_check=True)
                        last.then_inc(scored, 1)
                    if attn and k in VALUES_AT:
                        i = VALUES_AT[k]
                        next_job()
                        pe.wait_ge(moved_lo, probs_moved[i])
                        pe.wait_ge(v_lo, TILES * (b - 1) + i + 1)
                        for s in range(i + 1):
                            for n, (x, v) in enumerate(products(probsT, V)):
                                last = pe.matmul(psM[:, 0:DH], x[:, s * P:(s + 1) * P], v[:, s, :],
                                                 start=(s == 0 and n == 0), stop=(s == i and n == 2))
                        last.then_inc(valued, 1)
                    i = tile_copies(k, qkv, attn)
                    if i is not None:
                        bank = next_bank(nat_ready, TILES * (b - 1 if k == 1 else b) + i + 1)
                        for s in range(2):
                            last = pe.transpose(bank[:, s * P:(s + 1) * P], nat[i % 2][:, s * DH:s * DH + P],
                                                ident[:])
                        last.then_inc(moved, 1)
                        if k == 1:
                            qk3_moved = moves.now()
                    if attn and k in MIXED_T_AT:
                        i, h = MIXED_T_AT[k]
                        bank = next_bank(mixed_ready, TILES * (b - 1) + i + 1)
                        flat = mixed[i % 2][:].rearrange("p e d -> p (e d)")
                        for c in range(HALF):
                            last = pe.transpose(bank[:, c * P:(c + 1) * P],
                                                flat[:, (h * HALF + c) * P:(h * HALF + c + 1) * P], ident[:])
                        last.then_inc(moved, 1)
                        mixed_moved[i, h] = moves.now()
                    if attn and k in PROJECT_AT:
                        i, h = PROJECT_AT[k]
                        a = TILES * (b - 1) + i
                        pe.wait_ge(moved_lo, mixed_moved[i, h])
                        if h == 0:
                            if isinstance(b, int) and a == 0:
                                pass
                            else:
                                pe.wait_ge(y_ready, a)
                        pe.wait_ge(wo_lo, OC // 2)
                        for c in range(HALF):
                            for n, (x, w) in enumerate(products(mixedT[h], Wo)):
                                last = pe.matmul(psO[:], x[:, c * P:(c + 1) * P], w[:, h * HALF + c, :],
                                                 start=(h == 0 and c == 0 and n == 0),
                                                 stop=(h == 1 and c == HALF - 1 and n == 2))
                        last.then_inc(projected, 1)

            bodies(pe, body, [(moves, MOVES), (jobs, M_JOBS)])


OWN_STEPS = 4 * (4 + 6 + 4 + 3) + 4 + 4

_OUTS = [((8, 512, 512), 'float32')]


def kernel(x, ctx_1024, mask_BxSxS2_bk1, L0_xattn_W_merge, L0_xattn_b_merge, L0_ffn_sim_matrix, L0_ffn_gates,
           L0_ffn_q_proj, L0_ffn_k_proj, L0_ffn_v_proj, L0_ffn_o_proj):
    import numpy as _np
    import concourse.bacc as _bacc
    from concourse import mybir as _mybir
    from concourse.bass_utils import run_bass_kernel_spmd as _run

    E, D, DH = L0_ffn_q_proj.shape

    def rows_on_partitions(w):
        return w.reshape(-1, 128, w.shape[-1]).transpose(1, 0, 2)

    merge = _np.asarray(L0_xattn_W_merge)
    qkv = _np.stack([_np.asarray(w) for w in (L0_ffn_q_proj, L0_ffn_k_proj, L0_ffn_v_proj)], 2)
    laid = {
        "x": _np.asarray(x),
        "ctx_in": _np.asarray(ctx_1024),
        "mask": _np.asarray(mask_BxSxS2_bk1),
        "merge_t": rows_on_partitions(merge.T).reshape(128, -1),
        "bias": _np.asarray(L0_xattn_b_merge).reshape(1, -1),
        "sim": _np.asarray(L0_ffn_sim_matrix),
        "gates": _np.asarray(L0_ffn_gates),
        "w_qkv": rows_on_partitions(qkv.transpose(1, 0, 2, 3).reshape(D, E * 3 * DH)),
        "w_o": rows_on_partitions(_np.asarray(L0_ffn_o_proj).reshape(E * DH, D)),
    }
    nc = _bacc.Bacc("TRN2", target_bir_lowering=False, num_devices=1)
    arrays, args = {}, []
    for name, a in laid.items():
        a = _np.ascontiguousarray(a)
        arrays[f"in_{name}"] = a
        args.append(nc.dram_tensor(f"in_{name}", a.shape, _mybir.dt.from_np(a.dtype), kind="ExternalInput").ap())
    for i, (shape, dtype) in enumerate(_OUTS):
        dt = _mybir.dt.from_np(_np.dtype(dtype))
        args.append(nc.dram_tensor(f"out_{i}", shape, dt, kind="ExternalOutput").ap())
    cross_attention_then_experts_kernel(nc, *args)
    r = _run(nc, [arrays], core_ids=[0])
    return r.results[0]["out_0"]
```

```python
from contextlib import ExitStack

import concourse.bass as bass
from concourse import mybir

ALU = mybir.AluOpType
ACT = mybir.ActivationFunctionType
AX = mybir.AxisListType
F32 = mybir.dt.float32
F32R = mybir.dt.float32r
U8 = mybir.dt.uint8

P = 128
NEG_INF = -1.0e9
CAUSAL_FILL = -1.0e30
LN_EPS = 1e-5
NORM_FLOOR = 1e-12
HEAD_SCALE = 0.125

SCORES_AT = {0: 0, 2: 1, 4: 2, 6: 3}
PROBS_T_AT = {2: 0, 4: 1, 6: 2, 8: 3}
GATES_AT = {1: 0, 3: 1, 5: 2, 7: 3}
GATES_T_AT = {5: 0, 9: 1}
VALUES_AT = {8: 0, 11: 1}
QK_T_AT = {1: 3, 14: 0, 22: 1, 30: 2}
MIX_AT = {10: (0, 0), 11: (0, 1), 12: (0, 2), 13: (0, 3),
          18: (1, 0), 19: (1, 1), 20: (1, 2), 21: (1, 3)}
PROJECT_AT = {13: (0, 0), 15: (0, 1), 17: (1, 0), 18: (1, 1), 21: (2, 0), 23: (2, 1), 25: (3, 0), 26: (3, 1)}
STATS_SLOT, NORM_SLOT, H_T_SLOT, LOGITS_SLOT = 0, 1, 3, 4
LOGITS_T_SLOT = 5


class Seq:

    def __init__(self):
        self.base, self.k, self.static = 0, 0, 0

    def step(self):
        self.k += 1
        return self.base + self.k

    def now(self):
        return self.base + self.k

    def bank(self):
        return (self.static + self.k - 1) % 2

    def enter(self, turn, per):
        assert per % 2 == 0
        self.first = self.base + self.k
        self.base, self.static, self.k = self.first + per * turn, self.first, 0

    def leave(self, per, turns):
        assert self.k == per, (self.k, per)
        self.base = self.static = self.first + per * turns
        self.k = 0


def products(a, b):
    return ((a[0], b[0]), (a[0], b[1]), (a[1], b[0]))


def cross_attention_then_experts_kernel(nc, x, ctx_in, mask, merge_t, bias, sim, gates, w_qkv, w_o, out):
    B, S, D = x.shape
    C = ctx_in.shape[1]
    E = sim.shape[1]
    DH = w_qkv.shape[2] // E // 3
    TILES = S // P
    KC = D // P
    Q3 = 3 * DH
    PAIRS = E // 2
    SLOTS = TILES * PAIRS
    OC = E * DH // P
    HALF = OC // 2
    CP = C + 1
    CE = CP + CP % 2
    assert TILES == 4 and KC == 4 and PAIRS == 8 and DH == 64 and SLOTS == 32 and B == 8
    W_COLS = w_qkv.shape[1] * w_qkv.shape[2]
    W_PIECE = W_COLS // B
    REV_TOP = float(E)

    x2_dram = nc.dram_tensor("x2_scratch", (B, S, D), F32, kind="Internal").ap()

    whole = ExitStack()
    with whole:
        def alloc(stack):
            def sb(name, shape, dt=F32):
                return stack.enter_context(nc.sbuf_tensor(name, shape, dt))

            def ps(name):
                return stack.enter_context(nc.psum_tensor(name, [P, 512], F32))

            def sem(name):
                return stack.enter_context(nc.semaphore(name))

            def pair(name, shape):
                return (sb(name + "_hi", shape, F32R), sb(name + "_lo", shape, F32R))
            return sb, ps, sem, pair

        sb, _, sem, pair = alloc(whole)
        Wqkv = pair("Wqkv", [P, W_COLS])
        simn = pair("simn", [P, KC, E])
        ident = sb("ident", [P, P])
        ident_r = sb("ident_r", [P, P], F32R)
        causal_r = sb("causal_r", [P, P], F32R)
        rev = sb("rev", [P, E])
        neg_sig = sb("neg_sig", [P, E])
        neg_half = sb("neg_half", [P, TILES])
        const_ready = sem("const_ready")

        first = ExitStack()
        with first:
            sb, ps, sem, pair = alloc(first)
            X = [sb(f"X{p}", [P, TILES, D]) for p in range(2)]
            XR = [sb(f"XR{p}", [P, TILES, D]) for p in range(2)]
            CTX = [sb(f"CTX{p}", [C, D]) for p in range(2)]
            ctx = [pair(f"ctx{p}", [CP, D]) for p in range(2)]
            MASK = [sb(f"MASK{p}", [P, TILES, C], U8) for p in range(2)]
            ctx_centred = sb("ctx_centred", [C, D])
            ctxT = pair("ctxT", [P, KC, CE])
            xT = [pair(f"xT{p}", [P, S]) for p in range(2)]
            scoresT = sb("scoresT", [CE, S])
            keep = sb("keep", [P, TILES, C])
            fill = sb("fill", [P, TILES, C])
            scores = sb("scores", [P, TILES, C])
            E_un = sb("E_un", [P, TILES, C])
            att_f = sb("att_f", [P, TILES, CE])
            att = pair("att", [P, TILES, CE])
            G = pair("G", [CP, D])
            mergeT = pair("mergeT", [P, KC, D])
            stage = sb("stage", [P, W_PIECE])
            sim_f = sb("sim_f", [P, KC, E])
            sim_sq = sb("sim_sq", [P, KC, E])
            sim_ss = sb("sim_ss", [P, E])
            sim_rn = sb("sim_rn", [P, E])
            half_e = sb("half_e", [P, E])
            ones_f = sb("ones_f", [P, P])
            gate_e = sb("gate_e", [P, E])
            bias_f = sb("bias_f", [1, D])
            bias_p = pair("bias_p", [1, D])
            causal_f = sb("causal_f", [P, P])
            stats = sb("stats", [P, TILES, 6])
            mv = sb("mv", [P, TILES, 2])
            var_in = sb("var_in", [P, TILES])
            row_scale = [sb(f"row_scale{p}", [P, TILES]) for p in range(2)]
            ctx_mean = sb("ctx_mean", [C, 2])
            neg_max = sb("neg_max", [P, TILES])
            row_sum = sb("row_sum", [P, TILES])
            row_inv = sb("row_inv", [P, TILES])

            psXT = [ps(f"psXT{p}") for p in range(2)]
            psCT = ps("psCT")
            psST = ps("psST")
            psS = ps("psS")
            psG = ps("psG")
            psX2 = [ps(f"psX2{p}") for p in range(2)]
            psCT_v = psCT[:, 0:KC * CE].rearrange("p (c k) -> p c k", c=KC)
            psS_v = psS[:, 0:TILES * CE].rearrange("p (t k) -> p t k", t=TILES)

            ld_x = [sem(f"ld_x{p}") for p in range(2)]
            ld_ctx = [sem(f"ld_ctx{p}") for p in range(2)]
            ld_mask = [sem(f"ld_mask{p}") for p in range(2)]
            ld_w = sem("ld_w")
            ld_merge = sem("ld_merge")
            ld_sim = sem("ld_sim")
            ld_gates = sem("ld_gates")
            ld_bias = sem("ld_bias")
            st_x2 = [sem(f"st_x2{p}") for p in range(2)]
            bias_placed = sem("bias_placed")
            pool_init = sem("pool_init")
            dve_init = sem("dve_init")
            act_init = sem("act_init")
            sim_normed = sem("sim_normed")
            sim_summed = sem("sim_summed")
            merge_hi = sem("merge_hi")
            merge_lo = sem("merge_lo")
            w_hi = sem("w_hi")
            w_lo = sem("w_lo")
            ctx_hi = sem("ctx_hi")
            ctx_lo = sem("ctx_lo")
            centred = sem("centred")
            ctx_summed = sem("ctx_summed")
            ctxT_moved = sem("ctxT_moved")
            ctxT_hi = sem("ctxT_hi")
            ctxT_lo = sem("ctxT_lo")
            xT_moved = sem("xT_moved")
            xT_hi = sem("xT_hi")
            xT_lo = sem("xT_lo")
            xT_used = sem("xT_used")
            scoresT_out = sem("scoresT_out")
            scores_moved = sem("scores_moved")
            scores_read = sem("scores_read")
            mask_ready = sem("mask_ready")
            var_ready = sem("var_ready")
            scale_ready = sem("scale_ready")
            max_ready = sem("max_ready")
            exp_done = sem("exp_done")
            inv_ready = sem("inv_ready")
            att_scaled = sem("att_scaled")
            att_hi = sem("att_hi")
            att_lo = sem("att_lo")
            G_summed = sem("G_summed")
            G_hi = sem("G_hi")
            G_lo = sem("G_lo")
            resid_kept = sem("resid_kept")
            x2_summed = sem("x2_summed")
            x2_added = sem("x2_added")
            dve_own = sem("dve_own")

            def steps(eng, step, own=None, per=0):
                step(0, 0, True, True, False, False)
                step(1, 1, True, True, True, False)
                with eng.Fori(0, (B - 4) // 2) as n:
                    if own:
                        own.enter(n, per)
                    for p in range(2):
                        step(2 * n + 2 + p, p, True, True, True, True)
                    if own:
                        own.leave(per, (B - 4) // 2)
                step(B - 2, 0, True, True, True, True)
                step(B - 1, 1, True, False, True, True)
                step(B, 0, False, False, True, True)
                step(B + 1, 1, False, False, False, True)

            def turns(i, p):
                return i // 2 + 1 if isinstance(i, int) else (i - p) // 2 + 1

            FREE = 2

            def from_batch(i, least):
                return not isinstance(i, int) or i >= least

            with nc.Block() as block:
                @block.sync
                def _(sp):
                    def tiles_of(dram, i):
                        return dram[bass.ds(i, 1)].rearrange("b (t p) d -> p (b t) d", p=P)

                    sp.dma_start(CTX[0][:], ctx_in[0]).then_inc(ld_ctx[0], 16)
                    sp.dma_start(X[0][:], tiles_of(x, 0)).then_inc(ld_x[0], 16)
                    sp.dma_start(sim_f[:], sim.rearrange("(c p) e -> p c e", p=P)).then_inc(ld_sim, 16)
                    sp.dma_start(MASK[0][:], tiles_of(mask, 0)).then_inc(ld_mask[0], 16)
                    sp.dma_start(gate_e[:], gates.partition_broadcast(P)).then_inc(ld_gates, 16)
                    sp.dma_start(bias_f[:], bias).then_inc(ld_bias, 16)
                    sp.dma_start(CTX[1][:], ctx_in[1]).then_inc(ld_ctx[1], 16)
                    sp.dma_start(X[1][:], tiles_of(x, 1)).then_inc(ld_x[1], 16)
                    sp.dma_start(MASK[1][:], tiles_of(mask, 1)).then_inc(ld_mask[1], 16)
                    sp.dma_start(XR[1][:].rearrange("p t d -> p (t d)"), merge_t).then_inc(ld_merge, 16)
                    w_flat = w_qkv.rearrange("p c n -> p (c n)")
                    sp.dma_start(stage[:], w_flat[:, 0:W_PIECE]).then_inc(ld_w, 16)
                    sp.wait_ge(act_init, 1)
                    sp.dma_start(G[0][C:CP, :].bitcast(F32), bias_p[0][:].bitcast(F32)).then_inc(bias_placed, 16)
                    sp.wait_ge(dve_init, 2)
                    sp.dma_start(G[1][C:CP, :].bitcast(F32), bias_p[1][:].bitcast(F32)).then_inc(bias_placed, 16)

                    def step(i, p, score, ahead, back, tail):
                        if score and from_batch(i, 1):
                            sp.wait_ge(w_hi, i)
                            sp.wait_ge(w_lo, i)
                            sp.dma_start(stage[:], w_flat[:, bass.ds(i * W_PIECE, W_PIECE)]).then_inc(ld_w, 16)
                        if tail:
                            for h in range(2):
                                sp.wait_ge(x2_added, FREE + TILES * (i - 2) + 2 * h + 2)
                                dst = x2_dram.rearrange("b (h t p) d -> (b h) p t d", p=P, h=2)
                                sp.dma_start(dst[bass.ds(2 * (i - 2) + h, 1)].rearrange("a p t d -> p (a t) d"),
                                             XR[p][:, 2 * h:2 * h + 2, :]).then_inc(st_x2[p], 16)
                        if ahead and not (isinstance(i, int) and i + 2 >= B):
                            sp.wait_ge(xT_moved, KC * (i + 1))
                            sp.wait_ge(resid_kept, i + 1)
                            sp.wait_ge(var_ready, i + 1)
                            sp.wait_ge(mask_ready, i + 1)
                            sp.wait_ge(centred, i + 1)
                            sp.wait_ge(ctx_lo, i + 1)
                            sp.dma_start(X[p][:], tiles_of(x, i + 2)).then_inc(ld_x[p], 16)
                            sp.dma_start(MASK[p][:], tiles_of(mask, i + 2)).then_inc(ld_mask[p], 16)
                            sp.dma_start(CTX[p][:], ctx_in[bass.ds(i + 2, 1)].rearrange("b c d -> (b c) d")
                                         ).then_inc(ld_ctx[p], 16)

                    steps(sp, step)
                    for p in range(2):
                        sp.wait_ge(st_x2[p], 16 * B)

                @block.gpsimd
                def _(pool):
                    pool.memset(neg_half[:], -0.5).then_inc(pool_init, 1)
                    pool.memset(half_e[:], -0.5).then_inc(pool_init, 1)
                    pool.memset(ones_f[:], 1.0).then_inc(pool_init, 1)
                    pool.wait_ge(pool_init, 3)
                    pool.affine_select(out=ident[:], in_=ones_f[:], compare_op=ALU.is_equal, fill=0.0, base=0,
                                       pattern=[[-1, P]], channel_multiplier=1).then_inc(pool_init, 1)
                    pool.memset(causal_f[:], 0.0).then_inc(pool_init, 1)
                    pool.wait_ge(pool_init, 5)
                    pool.affine_select(out=causal_f[:], in_=causal_f[:], compare_op=ALU.is_ge, fill=CAUSAL_FILL,
                                       base=0, pattern=[[-1, P]], channel_multiplier=1).then_inc(pool_init, 1)
                    pool.iota(rev[:], pattern=[[-1, E]], base=E, channel_multiplier=0,
                              allow_small_or_imprecise_dtypes=True).then_inc(pool_init, 1)

                    def power(m, p):
                        pool.wait_ge(var_ready, m + 1)
                        pool.tensor_tensor(row_scale[p][:], var_in[:], neg_half[:], ALU.pow).then_inc(scale_ready, 1)

                    def masks(i, p):
                        pool.tensor_scalar(keep[:], MASK[p][:], -1.0, 1.0, ALU.mult, ALU.add)
                        pool.tensor_scalar(fill[:], MASK[p][:], NEG_INF, None, ALU.mult).then_inc(mask_ready, 1)

                    def step(i, p, score, ahead, back, tail):
                        if score:
                            pool.wait_ge(ld_mask[p], 16 * turns(i, p))
                        if back:
                            pool.wait_ge(att_hi, i)
                            pool.tensor_tensor(att[1][:], att_f[:], att[0][:].bitcast(F32), ALU.subtract
                                               ).then_inc(att_lo, 1)
                        if score:
                            masks(i, p)
                            pool.wait_ge(ctx_hi, i + 1)
                            pool.tensor_tensor(ctx[p][1][0:C, :], CTX[p][:], ctx[p][0][0:C, :].bitcast(F32),
                                               ALU.subtract).then_inc(ctx_lo, 1)
                        if ahead:
                            power(i + 1, 1 - p)
                        if score:
                            pool.wait_ge(w_hi, i + 1)
                            dst = bass.ds(i * W_PIECE, W_PIECE)
                            pool.tensor_tensor(Wqkv[1][:, dst], stage[:], Wqkv[0][:, dst].bitcast(F32),
                                               ALU.subtract).then_inc(w_lo, 1)
                        if isinstance(i, int) and i == 0:
                            pool.wait_ge(sim_summed, 2)
                            pool.tensor_tensor(sim_rn[:], sim_ss[:], half_e[:], ALU.pow).then_inc(sim_normed, 1)

                    power(0, 0)
                    steps(pool, step)

                @block.scalar
                def _(act):
                    def split_x(i, c):
                        act.wait_ge(xT_moved, KC * i + c + 1)
                        if from_batch(i, 1) or c >= 2:
                            act.wait_ge(xT_used, KC * i + c - 1)
                        act.activation(xT[c % 2][0][:], psXT[c % 2][:], ACT.Copy).then_inc(xT_hi, 1)

                    def split_ahead(m):
                        act.wait_ge(ctxT_moved, m + 1)
                        if from_batch(m, 1):
                            act.wait_ge(xT_used, KC * m)
                        act.activation(ctxT[0][:, :, 0:C], psCT_v[:, :, 0:C], ACT.Copy).then_inc(ctxT_hi, 1)
                        split_x(m, 0)
                        split_x(m, 1)

                    def centre(m, p):
                        act.wait_ge(ld_ctx[p], 16 * turns(m, p))
                        if from_batch(m, 1):
                            act.wait_ge(ctxT_moved, m)
                        act.activation(ctx_centred[:], CTX[p][:], ACT.Copy, scale=-1.0 / D, accum_out=ctx_mean[:, 0:1]
                                       ).then_inc(ctx_summed, 1)
                        act.wait_ge(ctx_summed, m + 1)
                        act.activation(ctx_centred[:], CTX[p][:], ACT.Identity, bias=ctx_mean[:, 0:1]
                                       ).then_inc(centred, 1)

                    def step(i, p, score, ahead, back, tail):
                        if score:
                            split_x(i, 2)
                        if back:
                            act.wait_ge(max_ready, i)
                            for t in range(TILES):
                                act.activation(E_un[:, t, :], scores[:, t, :], ACT.Exp, bias=neg_max[:, t:t + 1],
                                               accum_out=row_sum[:, t:t + 1]).then_inc(exp_done, 1)
                        if score:
                            split_x(i, 3)
                        if back:
                            act.wait_ge(inv_ready, i)
                            if from_batch(i, 2):
                                act.wait_ge(att_lo, i - 1)
                                act.wait_ge(G_summed, i - 1)
                            for t in range(TILES):
                                last = act.activation(att_f[:, t, 0:C], E_un[:, t, :], ACT.Copy,
                                                      scale=row_inv[:, t:t + 1])
                            last.then_inc(att_scaled, 1)
                            act.wait_ge(att_scaled, i)
                            act.activation(att[0][:], att_f[:], ACT.Copy).then_inc(att_hi, 1)
                        if score:
                            act.wait_ge(xT_used, KC * (i + 1))
                            if from_batch(i, 1):
                                act.wait_ge(scores_moved, i)
                            act.activation(scoresT[:], psST[0:CE, :], ACT.Copy).then_inc(scoresT_out, 1)
                            if from_batch(i, 2):
                                act.wait_ge(x2_summed, TILES * (i - 1))
                            else:
                                act.wait_ge(dve_init, 1)
                            act.activation(ctx[p][0][0:C, :], CTX[p][:], ACT.Copy).then_inc(ctx_hi, 1)
                        if ahead:
                            centre(i + 1, 1 - p)
                        if back:
                            act.wait_ge(G_summed, i)
                            if from_batch(i, 2):
                                act.wait_ge(x2_summed, TILES * (i - 1))
                            act.activation(G[0][0:C, :], psG[0:C, :], ACT.Copy).then_inc(G_hi, 1)
                        if ahead:
                            split_ahead(i + 1)
                        if isinstance(i, int) and i == 0:
                            act.wait_ge(ld_merge, 16)
                            act.activation(mergeT[0][:], XR[1][:], ACT.Copy).then_inc(merge_hi, 1)
                        if score:
                            act.wait_ge(ld_w, 16 * (i + 1))
                            dst = bass.ds(i * W_PIECE, W_PIECE)
                            act.activation(Wqkv[0][:, dst], stage[:], ACT.Copy).then_inc(w_hi, 1)
                            if from_batch(i, 2):
                                act.wait_ge(st_x2[p], 32 * (turns(i, p) - 1))
                            elif i == 1:
                                act.wait_ge(merge_lo, 1)
                            act.activation(XR[p][:], X[p][:], ACT.Copy).then_inc(resid_kept, 1)
                        if isinstance(i, int) and i == 1:
                            act.wait_ge(sim_normed, 2)
                            act.activation(simn[0][:], sim_f[:], ACT.Copy).then_inc(sim_normed, 1)

                    centre(0, 0)
                    act.wait_ge(dve_init, 1)
                    split_ahead(0)
                    act.wait_ge(ld_bias, 16)
                    act.activation(bias_p[0][:], bias_f[:], ACT.Copy).then_inc(act_init, 1)
                    act.wait_ge(ld_gates, 16)
                    act.activation(gate_e[:], gate_e[:], ACT.Exp, scale=-1.0).then_inc(act_init, 1)
                    act.wait_ge(pool_init, 6)
                    act.activation(ident_r[:], ident[:], ACT.Copy).then_inc(const_ready, 1)
                    act.activation(causal_r[:], causal_f[:], ACT.Copy).then_inc(const_ready, 1)

                    steps(act, step)

                @block.vector
                def _(dve):
                    own = Seq()

                    def link(ins):
                        ins.then_inc(dve_own, 1)
                        dve.wait_ge(dve_own, own.step())

                    def lo(dst, src, hi, signal):
                        dve.tensor_tensor(dst, src, hi.bitcast(F32), ALU.subtract).then_inc(signal, 1)

                    def row_stats(m, p):
                        dve.wait_ge(ld_x[p], 16 * turns(m, p))
                        for t in range(TILES):
                            dve.bn_stats(stats[:, t, :], X[p][:, t, :])
                        dve.drain()
                        for t in range(TILES):
                            last = dve.bn_aggr(mv[:, t, :], stats[:, t, :])
                        link(last)
                        if from_batch(m, 1):
                            dve.wait_ge(scale_ready, m)
                        dve.tensor_scalar(var_in[:], mv[:, :, 1], LN_EPS, float(D), ALU.add, ALU.mult
                                          ).then_inc(var_ready, 1)

                    def split_x(i, c):
                        dve.wait_ge(xT_hi, KC * i + c + 1)
                        lo(xT[c % 2][1][:], psXT[c % 2][:], xT[c % 2][0][:], xT_lo)

                    def split_ahead(m):
                        dve.wait_ge(ctxT_hi, m + 1)
                        lo(ctxT[1][:, :, 0:C], psCT_v[:, :, 0:C], ctxT[0][:, :, 0:C], ctxT_lo)
                        split_x(m, 0)
                        split_x(m, 1)

                    def mask_scores(i, p):
                        dve.wait_ge(scores_moved, i + 1)
                        dve.wait_ge(scale_ready, i + 1)
                        dve.wait_ge(mask_ready, i + 1)
                        if from_batch(i, 1):
                            dve.wait_ge(exp_done, TILES * i)
                        for t in range(TILES):
                            last = dve.scalar_tensor_tensor(
                                out=scores[:, t, :], in0=psS_v[:, t, 0:C], scalar=row_scale[p][:, t:t + 1],
                                in1=keep[:, t, :], op0=ALU.mult, op1=ALU.mult)
                        last.then_inc(scores_read, 1)
                        dve.wait_ge(scores_read, i + 1)
                        link(dve.tensor_tensor(scores[:], scores[:], fill[:], ALU.add))
                        dve.tensor_reduce(neg_max[:], scores[:], AX.X, ALU.max, negate=True).then_inc(max_ready, 1)

                    def add_residual(i, p, t):
                        dve.wait_ge(x2_summed, TILES * (i - 2) + t + 1)
                        dve.wait_ge(resid_kept, i - 1)
                        dve.tensor_tensor(XR[p][:, t, :], psX2[t % 2][:], XR[p][:, t, :], ALU.add
                                          ).then_inc(x2_added, 1)

                    def step(i, p, score, ahead, back, tail):
                        if score:
                            split_x(i, 2)
                        if tail:
                            add_residual(i, p, 0)
                        if back:
                            dve.wait_ge(exp_done, TILES * i)
                            dve.reciprocal(row_inv[:], row_sum[:]).then_inc(inv_ready, 1)
                        if score:
                            split_x(i, 3)
                        if tail:
                            for t in range(1, TILES):
                                add_residual(i, p, t)
                        if isinstance(i, int) and i == 0:
                            dve.wait_ge(ld_sim, 16)
                            dve.tensor_tensor(sim_sq[:], sim_f[:], sim_f[:], ALU.mult).then_inc(dve_init, 1)
                            dve.wait_ge(sim_summed, 1)
                            dve.tensor_scalar(sim_ss[:], psG[:, 0:E], NORM_FLOOR ** 2, None, ALU.max
                                              ).then_inc(sim_summed, 1)
                        if ahead:
                            row_stats(i + 1, 1 - p)
                        if back:
                            dve.wait_ge(G_hi, i)
                            lo(G[1][0:C, :], psG[0:C, :], G[0][0:C, :], G_lo)
                        if ahead:
                            split_ahead(i + 1)
                        if score:
                            mask_scores(i, p)
                        if isinstance(i, int) and i == 0:
                            dve.wait_ge(merge_hi, 1)
                            lo(mergeT[1][:], XR[1][:], mergeT[0][:], merge_lo)
                        if isinstance(i, int) and i == 1:
                            link(dve.tensor_scalar(gate_e[:], gate_e[:], 1.0, None, ALU.add))
                            link(dve.reciprocal(gate_e[:], gate_e[:]))
                            dve.tensor_scalar(neg_sig[:], gate_e[:], -1.0, None, ALU.mult).then_inc(const_ready, 1)
                            dve.wait_ge(sim_normed, 1)
                            for c in range(KC):
                                last = dve.tensor_tensor(sim_f[:, c, :], sim_f[:, c, :], sim_rn[:], ALU.mult)
                            last.then_inc(sim_normed, 1)
                            dve.wait_ge(sim_normed, 3)
                            lo(simn[1][:], sim_f[:], simn[0][:], const_ready)

                    for part in range(2):
                        dve.memset(ctxT[part][:].bitcast(F32), 0.0)
                    for p in range(2):
                        dve.memset(ctx[p][0][:].bitcast(F32), 1.0)
                        dve.memset(ctx[p][1][:].bitcast(F32), 0.0)
                    dve.memset(att_f[:], 0.0).then_inc(dve_init, 1)
                    dve.memset(row_sum[:], 1.0).then_inc(x2_added, FREE)
                    split_ahead(0)
                    row_stats(0, 0)
                    dve.wait_ge(act_init, 2)
                    lo(bias_p[1][:], bias_f[:], bias_p[0][:], dve_init)
                    steps(dve, step, own, 2 * 2)

                @block.tensor
                def _(pe):
                    def move_ctx(m):
                        pe.wait_ge(centred, m + 1)
                        if from_batch(m, 1):
                            pe.wait_ge(ctxT_lo, m)
                        for c in range(KC):
                            last = pe.transpose(psCT_v[:, c, 0:C], ctx_centred[:, c * P:(c + 1) * P],
                                                ident[0:C, 0:C])
                        last.then_inc(ctxT_moved, 1)

                    def move_x(m, p, c):
                        if c == 0:
                            pe.wait_ge(ld_x[p], 16 * turns(m, p))
                        if from_batch(m, 1) or c >= 2:
                            pe.wait_ge(xT_lo, KC * m + c - 1)
                        for t in range(TILES):
                            last = pe.transpose(psXT[c % 2][:, t * P:(t + 1) * P], X[p][:, t, c * P:(c + 1) * P],
                                                ident[:])
                        last.then_inc(xT_moved, 1)

                    def sum_scores(i, c):
                        pe.wait_ge(xT_lo, KC * i + c + 1)
                        if c == 0:
                            pe.wait_ge(ctxT_lo, i + 1)
                            if from_batch(i, 1):
                                pe.wait_ge(scoresT_out, i)
                        for n, (a, b) in enumerate(products(ctxT, xT[c % 2])):
                            last = pe.matmul(psST[0:CE, :], a[:, c, :], b[:],
                                             start=(c == 0 and n == 0), stop=(c == KC - 1 and n == 2))
                        last.then_inc(xT_used, 1)

                    def sum_x2(i, p, t):
                        if t == 0:
                            pe.wait_ge(G_lo, i - 1)
                            pe.wait_ge(ctx_lo, i - 1)
                        pe.wait_ge(x2_added, FREE + TILES * (i - 2) + t - 1)
                        for k, (a, b) in enumerate(products(ctx[p], G)):
                            last = pe.matmul(psX2[t % 2][:], a[:, t * P:(t + 1) * P], b[:], start=(k == 0), stop=(k == 2))
                        last.then_inc(x2_summed, 1)

                    def step(i, p, score, ahead, back, tail):
                        if score:
                            sum_scores(i, 0)
                            move_x(i, p, 2)
                        if tail:
                            sum_x2(i, p, 0)
                        if score:
                            sum_scores(i, 1)
                            move_x(i, p, 3)
                        if tail:
                            sum_x2(i, p, 1)
                        if score:
                            sum_scores(i, 2)
                        if tail:
                            sum_x2(i, p, 2)
                        if score:
                            sum_scores(i, 3)
                        if tail:
                            sum_x2(i, p, 3)
                        if isinstance(i, int) and i == 0:
                            pe.wait_ge(dve_init, 3)
                            for c in range(KC):
                                last = pe.matmul(psG[:, 0:E], ones_f[:], sim_sq[:, c, :], start=(c == 0),
                                                 stop=(c == KC - 1))
                            last.then_inc(sim_summed, 1)
                        if back:
                            pe.wait_ge(att_lo, i)
                            if isinstance(i, int) and i == 1:
                                pe.wait_ge(merge_lo, 1)
                                pe.wait_ge(bias_placed, 32)
                                pe.wait_ge(sim_summed, 2)
                            else:
                                pe.wait_ge(G_lo, i - 1)
                            for t in range(TILES):
                                for n, (a, b) in enumerate(products(att, mergeT)):
                                    last = pe.matmul(psG[0:CE, :], a[:, t, :], b[:, t, :],
                                                     start=(t == 0 and n == 0), stop=(t == TILES - 1 and n == 2))
                            last.then_inc(G_summed, 1)
                        if score:
                            pe.wait_ge(scoresT_out, i + 1)
                            if from_batch(i, 1):
                                pe.wait_ge(scores_read, i)
                            for t in range(TILES):
                                last = pe.transpose(psS_v[:, t, 0:C], scoresT[0:C, t * P:(t + 1) * P],
                                                    ident[0:C, 0:C])
                            last.then_inc(scores_moved, 1)
                        if ahead:
                            move_ctx(i + 1)
                            move_x(i + 1, 1 - p, 0)
                            move_x(i + 1, 1 - p, 1)

                    pe.wait_ge(pool_init, 4)
                    move_ctx(0)
                    move_x(0, 0, 0)
                    move_x(0, 0, 1)
                    steps(pe, step)

        experts_block(nc, whole, alloc, x2_dram, w_o, out, Wqkv, simn, ident, ident_r, causal_r, rev, neg_sig,
                      neg_half, const_ready, (B, S, D, E, DH, TILES, KC, Q3, PAIRS, SLOTS, OC, HALF))


def experts_block(nc, whole, alloc, x2_dram, w_o, out, Wqkv, simn, ident, ident_r, causal_r, rev, neg_sig,
                  neg_half, const_ready, sizes):
    B, S, D, E, DH, TILES, KC, Q3, PAIRS, SLOTS, OC, HALF = sizes
    N_TILES = B * TILES
    PW = 2 * Q3
    GK = 32 + E
    sb, ps, sem, pair = alloc(whole)
    Wo = pair("Wo", [P, OC, D])
    X2 = sb("X2", [P, D])
    H = sb("H", [P, D])
    hT = [pair(f"hT{p}", [P, D]) for p in range(2)]
    acc = [sb(f"acc{k}", [P, Q3]) for k in range(2)]
    nat = [sb(f"nat{p}", [P, Q3]) for p in range(2)]
    qkT = pair("qkT", [DH, 2, S])
    V = pair("V", [P, TILES, 2, DH])
    probs = [sb(f"probs{p}", [P, S]) for p in range(2)]
    probsT = [pair(f"probsT{h}", [P, (4 * h + 3) * P]) for h in range(2)]
    attT = [sb(f"attT{h}", [P, 2 * P]) for h in range(2)]
    gates_q = sb("gates_q", [P, (TILES + 1) * 64])
    gatesT = sb("gatesT", [GK, S], F32R)
    spread = sb("spread", [GK, OC, P], F32R)
    mixed_f = [sb(f"mixed_f{p}", [P, 2, 2 * P]) for p in range(2)]
    mixedT = pair("mixedT", [P, OC, 2 * P])
    resid = [sb(f"resid{p}", [P, D]) for p in range(2)]
    RW = [sb(f"RW{p}", [P, E]) for p in range(2)]
    RW_all = sb("RW_all", [P, N_TILES * E])
    stats = sb("b_stats", [P, 6])
    mv = sb("b_mv", [P, 2])
    pow_in = sb("pow_in", [P, 2])
    pow_tmp = sb("pow_tmp", [P, 2])
    pow_out = [sb(f"pow_out{p}", [P, 2]) for p in range(2)]
    neg_mx = [sb(f"neg_mx{p}", [P, 2]) for p in range(2)]
    p_sum = [sb(f"p_sum{p}", [P, 1]) for p in range(2)]
    p_inv = [sb(f"p_inv{p}", [P, 1]) for p in range(2)]
    logitT = sb("logitT", [P, P])
    logit = sb("logit", [P, E])
    rank = sb("rank", [P, E])
    pick1 = sb("pick1", [P, E])
    picks = sb("picks", [P, E])
    other = sb("other", [P, E])
    active = sb("active", [P, E])
    chosen = picks
    gate_in, gate_exp = other, rank
    g1 = sb("g1", [P, 8])

    psQ = [ps(f"psQ{k}") for k in range(4)]
    psT = [ps(f"psT{k}") for k in range(2)]
    psM = ps("psM")
    psO = ps("psO")

    ld_wo = [sem(f"ld_wo{p}") for p in range(2)]
    wo_hi, wo_lo = sem("wo_hi"), sem("wo_lo")
    x2_in = sem("x2_in")
    res_in = [sem(f"res_in{p}") for p in range(2)]
    y_out = [sem(f"y_out{p}") for p in range(2)]
    pow_asked, pow_done = sem("pow_asked"), sem("pow_done")
    h_ready = sem("h_ready")
    moved = sem("moved")
    moved_hi = sem("moved_hi")
    moved_lo = sem("moved_lo")
    logits_moved, logitT_zero = sem("logits_moved"), sem("logitT_zero")
    qkv_summed = sem("qkv_summed")
    expert_added = sem("expert_added")
    nat_ready = sem("nat_ready")
    v_hi, v_lo = sem("v_hi"), sem("v_lo")
    scored = sem("scored")
    neg_max_ready = sem("neg_max_ready")
    exp_done = sem("b_exp_done")
    valued = sem("valued")
    inv_made = sem("inv_made")
    gates_divided = sem("gates_divided")
    attT_out = sem("attT_out")
    mix_hi, mix_lo = sem("mix_hi"), sem("mix_lo")
    spread_made = sem("spread_made")
    projected = sem("projected")
    y_ready = sem("y_ready")
    gate_in_ready, gate_exp_ready = sem("gate_in_ready"), sem("gate_exp_ready")
    rw_ready, rw_kept = sem("rw_ready"), sem("rw_kept")
    own2 = sem("own2")

    MOVES, HIS = 26, 18
    WO_EVERY = SLOTS // OC
    LOOP = B - 3

    def bodies(eng, body, seqs):
        body(0, True, False, True)
        body(1, True, True, True)
        with eng.Fori(0, LOOP) as n:
            for s, per in seqs:
                s.enter(n, per)
            body(n + 2, True, True, True)
            for s, per in seqs:
                s.leave(per, LOOP)
        body(B - 1, True, True, False)
        body(B, False, True, False)

    def job_lists(k, b, qkv, attn, last_prep):
        j, g = divmod(k, PAIRS)
        prepare = qkv and (last_prep or j < TILES - 1)
        return j, g, prepare

    def tile_copies(k, qkv, attn):
        if k in QK_T_AT and (attn if k == 1 else qkv):
            return QK_T_AT[k]
        return None

    def place(i):
        return slice((1 - i % 2) * P, (2 - i % 2) * P)

    def keys_of(half, i):
        blocks = 2 * (i - i % 2) + 3
        return half[:].rearrange("p (s l) -> p s l", l=P)[:, 1 - i % 2:blocks:2, :]

    def v_twice(i):
        return nat[i % 2][:, 2 * DH:Q3].unsqueeze(1).broadcast_to([P, 2, DH])

    with nc.Block() as block:
        @block.sync
        def _(sp):
            sp.dma_start(X2[:], x2_dram[0, 0:P, :]).then_inc(x2_in, 16)

            def load_wo(n):
                if n >= 2:
                    sp.wait_ge(wo_lo, n - 1)
                sp.dma_start(mixed_f[n % 2][:].rearrange("p a l -> p (a l)"), w_o[:, n, :]).then_inc(ld_wo[n % 2], 16)

            def row(dram, b, t):
                return dram.rearrange("b (t p) d -> (b t) p d", p=P)[bass.ds(TILES * b + t, 1)].rearrange(
                    "a p d -> p (a d)")

            def store_y(b, i):
                sp.wait_ge(y_ready, TILES * (b - 1) + i + 1)
                sp.dma_start(row(out, b - 1, i), resid[i % 2][:]).then_inc(y_out[i % 2], 16)

            def load_resid(b, i):
                if not isinstance(b, int) or TILES * (b - 1) + i >= 2:
                    sp.wait_ge(y_out[i % 2], 16 * (2 * (b - 1) + i // 2))
                sp.dma_start(resid[i % 2][:], row(x2_dram, b - 1, i)).then_inc(res_in[i % 2], 16)

            def body(b, qkv, attn, prep):
                for j in range(TILES):
                    if qkv and (prep or j < TILES - 1):
                        sp.wait_ge(h_ready, TILES * b + j + 1)
                        sp.dma_start(X2[:], row(x2_dram, b, j + 1)).then_inc(x2_in, 16)
                    if not attn:
                        for n in range(OC // TILES):
                            load_wo(j * OC // TILES + n)
                    if attn and j == 0:
                        load_resid(b, 0)
                        load_resid(b, 1)
                    if attn and j == 2:
                        store_y(b, 0)
                        load_resid(b, 2)
                        store_y(b, 1)
                        load_resid(b, 3)
                    if attn and j == 3:
                        store_y(b, 2)
                        store_y(b, 3)

            bodies(sp, body, [])
            for p in range(2):
                sp.wait_ge(y_out[p], 16 * (N_TILES // 2))

        @block.gpsimd
        def _(pool):
            def powers(t, p):
                pool.wait_ge(pow_asked, t + 1)
                pool.tensor_tensor(pow_out[p][:], pow_in[:], neg_half[:, 0:2], ALU.pow).then_inc(pow_done, 1)

            def keep_gates(t, p):
                pool.wait_ge(rw_ready, t + 1)
                pool.tensor_copy(RW_all[:, bass.ds(t * E, E)], RW[p][:]).then_inc(rw_kept, 1)

            pool.memset(gates_q[:], 0.0).then_inc(spread_made, 1)
            pool.memset(logitT[:], 0.0).then_inc(logitT_zero, 1)
            powers(0, 0)
            done = 1
            for p in range(2):
                pool.memset(probs[p][:], 0.0).then_inc(spread_made, 1)
                done += 1
            pool.wait_ge(spread_made, done)
            for sign, base in (None, None), (1, 0), (-1, DH - 1):
                for p in range(2):
                    for row in (0, 32):
                        rows = probs[p][row:row + E, :].rearrange("k (c m) -> k c m", m=P)
                        if sign is None:
                            pool.memset(rows, 1.0).then_inc(spread_made, 1)
                        else:
                            shift = sign * 2 * DH * p * OC // 2
                            pool.affine_select(out=rows, in_=rows, compare_op=ALU.is_ge, fill=0.0, base=base + shift,
                                               pattern=[[sign * 2 * DH, OC // 2], [sign, P]],
                                               channel_multiplier=-sign * DH).then_inc(spread_made, 1)
                        done += 1
                pool.wait_ge(spread_made, done)
            for p in range(2):
                pool.tensor_copy(spread[:, p * OC // 2:(p + 1) * OC // 2, :],
                                 probs[p][0:GK, :].rearrange("k (c m) -> k c m", m=P)).then_inc(spread_made, 1)
            keep_gates(0, 0)

            def body(b, qkv, attn, prep):
                for k in range(SLOTS):
                    j, g, prepare = job_lists(k, b, qkv, attn, prep)
                    t = TILES * b + j
                    if prepare and g == STATS_SLOT:
                        powers(t + 1, (j + 1) % 2)
                    if not attn and k % WO_EVERY == 0:
                        n = k // WO_EVERY
                        pool.wait_ge(wo_hi, n + 1)
                        pool.tensor_tensor(Wo[1][:, n, :], mixed_f[n % 2][:].rearrange("p a l -> p (a l)"),
                                           Wo[0][:, n, :].bitcast(F32), ALU.subtract).then_inc(wo_lo, 1)
                    if attn and k in GATES_AT:
                        i = GATES_AT[k]
                        a = TILES * (b - 1) + i
                        pool.wait_ge(inv_made, a + 1)
                        pool.wait_ge(rw_kept, a + 1)
                        twice = gates_q[:, i * 64:(i + 1) * 64].rearrange("p (r e) -> p r e", r=2)[:, :, 0:E]
                        rw = RW_all[:, bass.ds(a * E, E)].unsqueeze(1).broadcast_to([P, 2, E])
                        inv = p_inv[i % 2][:].unsqueeze(2).broadcast_to([P, 2, E])
                        pool.tensor_tensor(twice, rw, inv, ALU.mult).then_inc(gates_divided, 1)
                    if attn and k in MIX_AT:
                        h, u = MIX_AT[k]
                        pool.wait_ge(mix_hi, 2 * TILES * (b - 1) + 4 * h + u + 1)
                        pair_of = slice(2 * u, 2 * u + 2)
                        pool.tensor_tensor(mixedT[1][:, pair_of, :], mixed_f[u % 2][:],
                                           mixedT[0][:, pair_of, :].bitcast(F32), ALU.subtract).then_inc(mix_lo, 1)
                    if prepare and g == PAIRS - 1:
                        keep_gates(t + 1, (j + 1) % 2)

            bodies(pool, body, [])

        @block.scalar
        def _(act):
            moves = Seq()

            def copy_h(t, p):
                if not isinstance(t, int) or t >= 2:
                    act.wait_ge(qkv_summed, PAIRS * (t - 1))
                act.wait_ge(moved, moves.step())
                act.activation(hT[p][0][:], psT[moves.bank()][:], ACT.Copy).then_inc(moved_hi, 1)

            def gate(t):
                act.wait_ge(gate_in_ready, t + 1)
                act.activation(gate_exp[:], gate_in[:], ACT.Exp).then_inc(gate_exp_ready, 1)

            def copy_logits():
                act.wait_ge(moved, moves.step())
                act.activation(logitT[0:E, :], psT[moves.bank()][0:E, 0:P], ACT.Copy).then_inc(moved_hi, 1)

            copy_h(0, 0)
            act.wait_ge(logitT_zero, 1)
            copy_logits()
            gate(0)
            def body(b, qkv, attn, prep):
                for k in range(SLOTS):
                    j, g, prepare = job_lists(k, b, qkv, attn, prep)
                    t = TILES * b + j
                    if prepare and g == H_T_SLOT:
                        copy_h(t + 1, (j + 1) % 2)
                    if not attn and k % WO_EVERY == 0:
                        n = k // WO_EVERY
                        act.wait_ge(ld_wo[n % 2], 16 * (n // 2 + 1))
                        act.activation(Wo[0][:, n, :], mixed_f[n % 2][:].rearrange("p a l -> p (a l)"), ACT.Copy
                                       ).then_inc(wo_hi, 1)
                    if attn and k in PROBS_T_AT:
                        i = PROBS_T_AT[k]
                        n = moves.step()
                        act.wait_ge(moved, n)
                        if not isinstance(b, int) or b >= 2:
                            act.wait_ge(valued, 2 * (b - 2) + i // 2 + 1)
                        act.activation(keys_of(probsT[i // 2][0], i),
                                       psT[moves.bank()][:, 0:(i + 1) * P].rearrange("p (s l) -> p s l", l=P),
                                       ACT.Copy).then_inc(moved_hi, 1)
                    i = tile_copies(k, qkv, attn)
                    if i is not None:
                        bt = b - 1 if k == 1 else b
                        n = moves.step()
                        act.wait_ge(moved, n)
                        if not isinstance(b, int) or bt >= 1:
                            act.wait_ge(scored, TILES * bt)
                            act.wait_ge(valued, 2 * bt)
                        src = psT[moves.bank()][0:DH, 0:2 * P].rearrange("p (a s) -> p a s", a=2)
                        act.activation(qkT[0][:, :, i * P:(i + 1) * P], src, ACT.Copy).then_inc(moved_hi, 1)
                        act.activation(V[0][:, i, :, :], v_twice(i), ACT.Copy).then_inc(v_hi, 1)
                    if attn and k in GATES_T_AT:
                        h = GATES_T_AT[k]
                        n = moves.step()
                        act.wait_ge(moved, n)
                        act.activation(gatesT[:, h * 2 * P:(h + 1) * 2 * P], psT[moves.bank()][0:GK, 0:2 * P], ACT.Copy
                                       ).then_inc(moved_hi, 1)
                    if attn and k in MIX_AT:
                        h, u = MIX_AT[k]
                        act.wait_ge(moved_lo, moves.step())
                        if h == 1:
                            act.wait_ge(projected, 8 * (b - 1) + 3 + u // 2)
                        elif not isinstance(b, int) or b >= 2:
                            act.wait_ge(projected, 8 * (b - 2) + 7 + u // 2)
                        act.activation(mixedT[0][:, 2 * u:2 * u + 2, :], mixed_f[u % 2][:], ACT.Copy).then_inc(mix_hi, 1)
                    if prepare and g == LOGITS_SLOT:
                        copy_logits()
                    if attn and k in SCORES_AT:
                        i = SCORES_AT[k]
                        act.wait_ge(neg_max_ready, TILES * (b - 1) + i + 1)
                        if isinstance(b, int) and b == 1 and i < 2:
                            act.wait_ge(spread_made, 17)
                        act.activation(probs[i % 2][:, 0:(i + 1) * P], psM[:, 0:(i + 1) * P], ACT.Exp,
                                       bias=neg_mx[i % 2][:, 1:2], scale=HEAD_SCALE,
                                       accum_out=p_sum[i % 2][:]).then_inc(exp_done, 1)
                    if attn and k in VALUES_AT:
                        h = VALUES_AT[k]
                        act.wait_ge(valued, 2 * (b - 1) + h + 1)
                        act.activation(attT[h][:], psM[:, 0:2 * P], ACT.Copy).then_inc(attT_out, 1)
                    if prepare and g == LOGITS_SLOT + 2:
                        gate(t + 1)

            bodies(act, body, [(moves, MOVES)])

        @block.vector
        def _(dve):
            own, moves, his = Seq(), Seq(), Seq()

            def link(ins):
                ins.then_inc(own2, 1)
                dve.wait_ge(own2, own.step())

            def lo(dst, cols, dst_hi, view=None):
                moves.step()
                bank = psT[moves.bank()]
                src = bank[:, cols] if view is None else view(bank)
                dve.wait_ge(moved_hi, his.step())
                dve.tensor_tensor(dst, src, dst_hi.bitcast(F32), ALU.subtract).then_inc(moved_lo, 1)

            def row_stats(t):
                dve.wait_ge(x2_in, 16 * (t + 1))
                dve.bn_stats(stats[:], X2[:])
                dve.drain()
                link(dve.bn_aggr(mv[:], stats[:]))
                link(dve.tensor_scalar(pow_tmp[:, 0:1], mv[:, 1:2], LN_EPS, None, ALU.add))
                link(dve.reciprocal(pow_tmp[:, 1:2], pow_tmp[:, 0:1]))
                link(dve.scalar_tensor_tensor(out=pow_tmp[:, 1:2], in0=mv[:, 1:2], scalar=float(D),
                                              in1=pow_tmp[:, 1:2], op0=ALU.mult, op1=ALU.mult))
                dve.tensor_copy(pow_in[:, 0:1], pow_tmp[:, 0:1])
                dve.tensor_scalar(pow_in[:, 1:2], pow_tmp[:, 1:2], NORM_FLOOR ** 2, None, ALU.max
                                  ).then_inc(pow_asked, 1)

            def normalise(t, p):
                dve.wait_ge(pow_done, t + 1)
                dve.tensor_scalar(H[:], X2[:], mv[:, 0:1], pow_out[p][:, 0:1], ALU.subtract, ALU.mult
                                  ).then_inc(h_ready, 1)

            def read_logits(t, p):
                dve.wait_ge(logits_moved, t + 1)
                n = moves.step()
                his.step()
                dve.scalar_tensor_tensor(out=logit[:], in0=psT[moves.bank()][:, P:P + E], scalar=pow_out[p][:, 1:2],
                                         in1=neg_sig[:], op0=ALU.mult, op1=ALU.add).then_inc(moved_lo, 1)
                dve.wait_ge(moved_lo, n)

            def gates_1():
                link(dve.tensor_reduce(g1[:, 0:1], logit[:], AX.X, ALU.max))
                link(dve.scalar_tensor_tensor(out=rank[:], in0=logit[:], scalar=g1[:, 0:1], in1=rev[:],
                                              op0=ALU.is_equal, op1=ALU.mult))
                link(dve.tensor_reduce(g1[:, 1:2], rank[:], AX.X, ALU.max))
                link(dve.tensor_scalar(pick1[:], rev[:], g1[:, 1:2], None, ALU.is_equal))
                link(dve.scalar_tensor_tensor(out=other[:], in0=pick1[:], scalar=CAUSAL_FILL, in1=logit[:],
                                              op0=ALU.mult, op1=ALU.add))
                link(dve.tensor_reduce(g1[:, 2:3], other[:], AX.X, ALU.max))

            def gates_2(t, p):
                link(dve.scalar_tensor_tensor(out=rank[:], in0=other[:], scalar=g1[:, 2:3], in1=rev[:],
                                              op0=ALU.is_equal, op1=ALU.mult))
                link(dve.tensor_reduce(g1[:, 3:4], rank[:], AX.X, ALU.max))
                dve.tensor_scalar(active[:], logit[:], 0.0, None, ALU.is_gt)
                dve.tensor_scalar(g1[:, 4:5], g1[:, 0:1], 0.0, None, ALU.is_le)
                dve.tensor_scalar(g1[:, 5:6], g1[:, 0:1], -1.0, 0.0, ALU.mult, ALU.min)
                link(dve.scalar_tensor_tensor(out=picks[:], in0=rev[:], scalar=g1[:, 3:4], in1=pick1[:],
                                              op0=ALU.is_equal, op1=ALU.add))
                dve.tensor_scalar(gate_in[:], logit[:], 0.0, g1[:, 5:6], ALU.max, ALU.add).then_inc(gate_in_ready, 1)
                link(dve.scalar_tensor_tensor(out=chosen[:], in0=picks[:], scalar=g1[:, 4:5], in1=active[:],
                                              op0=ALU.mult, op1=ALU.add))

            def gates_3(t, p):
                dve.wait_ge(gate_exp_ready, t + 1)
                link(dve.tensor_tensor(chosen[:], chosen[:], gate_exp[:], ALU.mult))
                link(dve.tensor_reduce(g1[:, 6:7], chosen[:], AX.X, ALU.add))
                link(dve.reciprocal(g1[:, 7:8], g1[:, 6:7]))
                if not isinstance(t, int) or t >= 2:
                    dve.wait_ge(rw_kept, t - 1)
                dve.tensor_scalar(RW[p][:], chosen[:], g1[:, 7:8], None, ALU.mult).then_inc(rw_ready, 1)

            row_stats(0)
            normalise(0, 0)
            lo(hT[0][1][:], slice(0, D), hT[0][0][:])
            read_logits(0, 0)
            gates_1()
            gates_2(0, 0)
            gates_3(0, 0)

            def body(b, qkv, attn, prep):
                for k in range(SLOTS):
                    j, g, prepare = job_lists(k, b, qkv, attn, prep)
                    t = TILES * b + j
                    tp = j % 2
                    if qkv:
                        dve.wait_ge(qkv_summed, SLOTS * b + k + 1)
                        if g == 0:
                            dve.wait_ge(rw_ready, t + 1)
                        for e in range(2):
                            src = psQ[g % 4][:, e * Q3:(e + 1) * Q3]
                            w = RW[tp][:, 2 * g + e:2 * g + e + 1]
                            if g == 0:
                                dve.tensor_scalar(acc[e][:], src, w, None, ALU.mult).then_inc(expert_added, 1)
                            else:
                                dve.wait_ge(expert_added, 2 * (SLOTS * b + k) + e - 1)
                                dve.scalar_tensor_tensor(out=acc[e][:], in0=src, scalar=w, in1=acc[e][:],
                                                         op0=ALU.mult, op1=ALU.add).then_inc(expert_added, 1)
                    if qkv and g == PAIRS - 1:
                        dve.wait_ge(expert_added, 2 * (SLOTS * b + k + 1))
                        dve.tensor_tensor(nat[tp][:], acc[0][:], acc[1][:], ALU.add).then_inc(nat_ready, 1)
                    if attn and k - 1 in PROJECT_AT and PROJECT_AT[k - 1][1] == 1:
                        i = PROJECT_AT[k - 1][0]
                        a = TILES * (b - 1) + i
                        dve.wait_ge(projected, 2 * a + 2)
                        dve.wait_ge(res_in[i % 2], 16 * (2 * (b - 1) + i // 2 + 1))
                        dve.tensor_tensor(resid[i % 2][:], psO[:], resid[i % 2][:], ALU.add).then_inc(y_ready, 1)
                    if prepare and g == NORM_SLOT:
                        normalise(t + 1, 1 - tp)
                    if prepare and g == LOGITS_T_SLOT:
                        read_logits(t + 1, 1 - tp)
                    if prepare and g == H_T_SLOT:
                        lo(hT[1 - tp][1][:], slice(0, D), hT[1 - tp][0][:])
                    if attn and k in PROBS_T_AT:
                        i = PROBS_T_AT[k]
                        lo(keys_of(probsT[i // 2][1], i), None, keys_of(probsT[i // 2][0], i),
                           lambda bank: bank[:, 0:(i + 1) * P].rearrange("p (s l) -> p s l", l=P))
                    n = tile_copies(k, qkv, attn)
                    if n is not None:
                        bt = b - 1 if k == 1 else b
                        lo(qkT[1][:, :, n * P:(n + 1) * P], None, qkT[0][:, :, n * P:(n + 1) * P],
                           lambda bank: bank[0:DH, 0:2 * P].rearrange("p (a s) -> p a s", a=2))
                        dve.wait_ge(v_hi, TILES * bt + n + 1)
                        dve.tensor_tensor(V[1][:, n, :, :], v_twice(n), V[0][:, n, :, :].bitcast(F32),
                                          ALU.subtract).then_inc(v_lo, 1)
                    if attn and k in GATES_T_AT:
                        h = GATES_T_AT[k]
                        where = (slice(32, GK), slice(h * 2 * P, (h + 1) * 2 * P))
                        lo(gatesT[where], None, gatesT[where], lambda bank: bank[32:GK, 0:2 * P])
                    if attn and k in MIX_AT:
                        h, u = MIX_AT[k]
                        m = 8 * (b - 1) + 4 * h + u + 1
                        dve.wait_ge(moved, moves.step())
                        dve.wait_ge(attT_out, 2 * (b - 1) + h + 1)
                        if not isinstance(b, int) or m > 2:
                            dve.wait_ge(mix_lo, m - 2)
                        else:
                            dve.wait_ge(wo_lo, OC)
                        dve.tensor_tensor(mixed_f[u % 2][:],
                                          psT[moves.bank()][:].rearrange("p (c l) -> p c l", c=2),
                                          attT[h][:].unsqueeze(1).broadcast_to([P, 2, 2 * P]), ALU.mult
                                          ).then_inc(moved_lo, 1)
                    if attn and k in SCORES_AT:
                        i = SCORES_AT[k]
                        dve.wait_ge(scored, TILES * (b - 1) + i + 1)
                        link(dve.tensor_reduce(neg_mx[i % 2][:, 0:1], psM[:, 0:(i + 1) * P], AX.X, ALU.max,
                                               negate=True))
                        dve.tensor_scalar(neg_mx[i % 2][:, 1:2], neg_mx[i % 2][:, 0:1], HEAD_SCALE, None, ALU.mult
                                          ).then_inc(neg_max_ready, 1)
                    if attn and k in GATES_AT:
                        i = GATES_AT[k]
                        a = TILES * (b - 1) + i
                        dve.wait_ge(exp_done, a + 1)
                        if not isinstance(b, int) or a >= 2:
                            dve.wait_ge(gates_divided, a - 1)
                        dve.reciprocal(p_inv[i % 2][:], p_sum[i % 2][:]).then_inc(inv_made, 1)
                    if prepare and g == LOGITS_T_SLOT:
                        gates_1()
                    if prepare and g == LOGITS_T_SLOT + 1:
                        gates_2(t + 1, 1 - tp)
                    if prepare and g == LOGITS_T_SLOT + 2:
                        gates_3(t + 1, 1 - tp)
                    if prepare and g == STATS_SLOT:
                        row_stats(t + 1)

            bodies(dve, body, [(own, OWN_STEPS), (moves, MOVES), (his, HIS)])

        @block.tensor
        def _(pe):
            moves, his = Seq(), Seq()

            def next_bank(ready, value, has_high=True):
                n = moves.step()
                if has_high:
                    his.step()
                if not isinstance(n, int) or n >= 3:
                    pe.wait_ge(moved_lo, n - 2)
                pe.wait_ge(ready, value)
                return psT[moves.bank()]

            def move_h(t):
                bank = next_bank(h_ready, t + 1)
                for c in range(KC):
                    last = pe.transpose(bank[:, c * P:(c + 1) * P], H[:, c * P:(c + 1) * P], ident[:])
                last.then_inc(moved, 1)

            def sum_logits(p, h_moved):
                bank = next_bank(moved_lo, h_moved)
                for c in range(KC):
                    for n, (a, b) in enumerate(products(simn, hT[p])):
                        last = pe.matmul(bank[0:E, 0:P], a[:, c, :], b[:, c * P:(c + 1) * P],
                                         start=(c == 0 and n == 0), stop=(c == KC - 1 and n == 2))
                last.then_inc(moved, 1)
                return bank, his.now()

            def move_logits(bank, job):
                pe.wait_ge(moved_hi, job)
                pe.transpose(bank[:, P:2 * P], logitT[:], ident[:]).then_inc(logits_moved, 1)

            move_h(0)
            move_logits(*sum_logits(0, moves.now()))
            Wv = [w[:].rearrange("p (c n) -> p c n", c=KC) for w in Wqkv]

            def body(b, qkv, attn, prep):
                before = moves.now()
                h_moved = logits = qk3_moved = None
                probs_moved, gates_in_place = {}, {}
                for k in range(SLOTS):
                    j, g, prepare = job_lists(k, b, qkv, attn, prep)
                    t = TILES * b + j
                    tp = j % 2
                    if qkv:
                        n = SLOTS * b + k
                        if not isinstance(b, int) or n >= 4:
                            pe.wait_ge(expert_added, 2 * (n - 3))
                        for c in range(KC):
                            for m, (x, w) in enumerate(products(hT[tp], Wv)):
                                last = pe.matmul(psQ[g % 4][:, 0:PW], x[:, c * P:(c + 1) * P],
                                                 w[:, c, g * PW:(g + 1) * PW],
                                                 start=(c == 0 and m == 0), stop=(c == KC - 1 and m == 2))
                        last.then_inc(qkv_summed, 1)
                    if prepare and g == H_T_SLOT:
                        move_h(t + 1)
                        h_moved = moves.now()
                    if prepare and g == LOGITS_T_SLOT:
                        move_logits(*logits)
                    if attn and k in PROBS_T_AT:
                        i = PROBS_T_AT[k]
                        bank = next_bank(exp_done, TILES * (b - 1) + i + 1)
                        for s in range(i + 1):
                            last = pe.transpose(bank[:, s * P:(s + 1) * P], probs[i % 2][:, s * P:(s + 1) * P],
                                                ident[:])
                        last.then_inc(moved, 1)
                        probs_moved[i] = moves.now()
                    i = tile_copies(k, qkv, attn)
                    if i is not None:
                        bank = next_bank(nat_ready, TILES * (b - 1 if k == 1 else b) + i + 1)
                        for s in range(2):
                            last = pe.transpose(bank[:, s * P:(s + 1) * P], nat[i % 2][:, s * DH:s * DH + P],
                                                ident[:])
                        last.then_inc(moved, 1)
                        if k == 1:
                            qk3_moved = moves.now()
                    if attn and k in GATES_T_AT:
                        h = GATES_T_AT[k]
                        bank = next_bank(gates_divided, TILES * (b - 1) + 2 * h + 2)
                        for s in range(2):
                            last = pe.transpose(bank[:, place(s)], gates_q[:, (2 * h + s) * 64:(2 * h + s + 2) * 64],
                                                ident[:])
                        last.then_inc(moved, 1)
                        gates_in_place[h] = moves.now()
                    if attn and k in MIX_AT:
                        h, u = MIX_AT[k]
                        if isinstance(b, int) and b == 1 and (h, u) == (0, 0):
                            pe.wait_ge(spread_made, 17)
                        bank = next_bank(moved_lo, gates_in_place[h], has_high=False)
                        for s in range(2):
                            last = pe.matmul(bank[:, s * 2 * P:(s + 1) * 2 * P], spread[:, 2 * u + s, :],
                                             gatesT[:, h * 2 * P:(h + 1) * 2 * P], start=True, stop=True)
                        last.then_inc(moved, 1)
                    if attn and k in SCORES_AT:
                        i = SCORES_AT[k]
                        if i > 0:
                            pe.wait_ge(exp_done, TILES * (b - 1) + i)
                        elif not isinstance(b, int) or b >= 2:
                            pe.wait_ge(attT_out, 2 * (b - 1))
                        if i == 0:
                            pe.wait_ge(moved_lo, before)
                        if i == TILES - 1:
                            pe.wait_ge(moved_lo, qk3_moved)
                        cols = slice(0, (i + 1) * P)
                        for n, (q, kk) in enumerate(products(qkT, qkT)):
                            last = pe.matmul(psM[:, cols], q[:, 0, i * P:(i + 1) * P], kk[:, 1, cols],
                                             start=(n == 0), stop=(n == 2), skip_group_check=True)
                            if n == 0:
                                pe.matmul(psM[:, i * P:(i + 1) * P], ident_r[:], causal_r[:], start=False,
                                          stop=False, skip_group_check=True)
                        last.then_inc(scored, 1)
                    if attn and k in VALUES_AT:
                        h = VALUES_AT[k]
                        if h == 0:
                            pe.wait_ge(exp_done, TILES * b)
                        else:
                            pe.wait_ge(attT_out, 2 * (b - 1) + 1)
                        pe.wait_ge(moved_lo, probs_moved[2 * h + 1])
                        pe.wait_ge(v_lo, TILES * (b - 1) + 2 * h + 2)
                        last_keys = 2 * h + 1
                        order = [(0, n) for n in range(2)] + [(s, n) for s in range(last_keys, 0, -1) for n in range(3)]
                        order.append((0, 2))
                        for m, (s, n) in enumerate(order):
                            cols = slice(0, P if s == last_keys else 2 * P)
                            v, x = products(V, probsT[h])[n]
                            last = pe.matmul(psM[:, cols], v[:, s, :, :].rearrange("p r d -> p (r d)"), 
                                             x[:, s * 2 * P:s * 2 * P + cols.stop],
                                             start=(m == 0), stop=(m == len(order) - 1), skip_group_check=True)
                        last.then_inc(valued, 1)
                    if prepare and g == LOGITS_SLOT:
                        logits = sum_logits(1 - tp, h_moved)
                    if attn and k in PROJECT_AT:
                        i, part = PROJECT_AT[k]
                        a = TILES * (b - 1) + i
                        pe.wait_ge(mix_lo, 8 * (b - 1) + 4 * (i // 2) + 2 * part + 2)
                        if part == 0 and not (isinstance(b, int) and a == 0):
                            pe.wait_ge(y_ready, a)
                        pe.wait_ge(wo_lo, OC)
                        for c in range(part * HALF, (part + 1) * HALF):
                            for n, (x, w) in enumerate(products(mixedT, Wo)):
                                last = pe.matmul(psO[:], x[:, c, place(i)], w[:, c, :],
                                                 start=(c == 0 and n == 0), stop=(c == OC - 1 and n == 2))
                        last.then_inc(projected, 1)

            bodies(pe, body, [(moves, MOVES), (his, HIS)])


OWN_STEPS = 4 * (4 + 6 + 4 + 3) + 4

_OUTS = [((8, 512, 512), 'float32')]


def kernel(x, ctx_1024, mask_BxSxS2_bk1, L0_xattn_W_merge, L0_xattn_b_merge, L0_ffn_sim_matrix, L0_ffn_gates,
           L0_ffn_q_proj, L0_ffn_k_proj, L0_ffn_v_proj, L0_ffn_o_proj):
    import numpy as _np
    import concourse.bacc as _bacc
    from concourse import mybir as _mybir
    from concourse.bass_utils import run_bass_kernel_spmd as _run

    E, D, DH = L0_ffn_q_proj.shape

    def rows_on_partitions(w):
        return w.reshape(-1, 128, w.shape[-1]).transpose(1, 0, 2)

    merge = _np.asarray(L0_xattn_W_merge)
    qkv = _np.stack([_np.asarray(w) for w in (L0_ffn_q_proj, L0_ffn_k_proj, L0_ffn_v_proj)], 2)
    laid = {
        "x": _np.asarray(x),
        "ctx_in": _np.asarray(ctx_1024),
        "mask": _np.asarray(mask_BxSxS2_bk1),
        "merge_t": rows_on_partitions(merge.T).reshape(128, -1),
        "bias": _np.asarray(L0_xattn_b_merge).reshape(1, -1),
        "sim": _np.asarray(L0_ffn_sim_matrix),
        "gates": _np.asarray(L0_ffn_gates),
        "w_qkv": rows_on_partitions(qkv.transpose(1, 0, 2, 3).reshape(D, E * 3 * DH)),
        "w_o": rows_on_partitions(_np.asarray(L0_ffn_o_proj).reshape(E * DH, D)),
    }
    nc = _bacc.Bacc("TRN2", target_bir_lowering=False, num_devices=1)
    arrays, args = {}, []
    for name, a in laid.items():
        a = _np.ascontiguousarray(a)
        arrays[f"in_{name}"] = a
        args.append(nc.dram_tensor(f"in_{name}", a.shape, _mybir.dt.from_np(a.dtype), kind="ExternalInput").ap())
    for i, (shape, dtype) in enumerate(_OUTS):
        dt = _mybir.dt.from_np(_np.dtype(dtype))
        args.append(nc.dram_tensor(f"out_{i}", shape, dt, kind="ExternalOutput").ap())
    cross_attention_then_experts_kernel(nc, *args)
    r = _run(nc, [arrays], core_ids=[0])
    return r.results[0]["out_0"]
```

```python
from contextlib import ExitStack

import concourse.bass as bass
from concourse import mybir

ALU = mybir.AluOpType
ACT = mybir.ActivationFunctionType
AX = mybir.AxisListType
F32 = mybir.dt.float32
F32R = mybir.dt.float32r
U8 = mybir.dt.uint8

P = 128
NEG_INF = -1.0e9
CAUSAL_FILL = -1.0e30
LN_EPS = 1e-5
NORM_FLOOR = 1e-12
HEAD_SCALE = 0.125

LEAD = 16
QK_T_AT = {12: 0, 16: 1, 28: 2, 0: 3}
SCORES_AT = {16: 0, 18: 1, 29: 2, 2: 3}
GATES_AT = {17: 0, 19: 1, 30: 2, 3: 3}
PROBS_T_AT = {18: 0, 20: 1, 31: 2, 4: 3}
GATES_T_AT = {21: 0, 5: 1}
VALUES_AT = {22: 0, 6: 1}
MIX_AT = {23: (0, 0), 24: (0, 1), 25: (0, 2), 26: (0, 3),
          7: (1, 0), 8: (1, 1), 9: (1, 2), 10: (1, 3)}
PROJECT_AT = {27: [(0, 0)], 28: [(0, 1)], 30: [(1, 0), (1, 1)],
              11: [(2, 0)], 12: [(2, 1)], 14: [(3, 0), (3, 1)]}
Y_AT = {29: 0, 31: 1, 13: 2, 15: 3}
STATS_SLOT, NORM_SLOT, H_T_SLOT, LOGITS_SLOT = 0, 1, 3, 4
LOGITS_T_SLOT = 5


class Seq:

    def __init__(self):
        self.base, self.k, self.static = 0, 0, 0

    def step(self):
        self.k += 1
        return self.base + self.k

    def now(self):
        return self.base + self.k

    def bank(self):
        return (self.static + self.k - 1) % 2

    def enter(self, turn, per):
        assert per % 2 == 0
        self.first = self.base + self.k
        self.base, self.static, self.k = self.first + per * turn, self.first, 0

    def leave(self, per, turns):
        assert self.k == per, (self.k, per)
        self.base = self.static = self.first + per * turns
        self.k = 0


def products(a, b):
    return ((a[0], b[0]), (a[0], b[1]), (a[1], b[0]))


def cross_attention_then_experts_kernel(nc, x, ctx_in, mask, merge_t, bias, sim, gates, w_qkv, w_o, out):
    B, S, D = x.shape
    C = ctx_in.shape[1]
    E = sim.shape[1]
    DH = w_qkv.shape[2] // E // 3
    TILES = S // P
    KC = D // P
    Q3 = 3 * DH
    PAIRS = E // 2
    SLOTS = TILES * PAIRS
    OC = E * DH // P
    HALF = OC // 2
    CP = C + 1
    CE = CP + CP % 2
    assert TILES == 4 and KC == 4 and PAIRS == 8 and DH == 64 and SLOTS == 32 and B == 8
    W_COLS = w_qkv.shape[1] * w_qkv.shape[2]
    W_PIECE = W_COLS // B

    x2_dram = nc.dram_tensor("x2_scratch", (B, S, D), F32, kind="Internal").ap()

    whole = ExitStack()
    with whole:
        def alloc(stack):
            def sb(name, shape, dt=F32):
                return stack.enter_context(nc.sbuf_tensor(name, shape, dt))

            def ps(name):
                return stack.enter_context(nc.psum_tensor(name, [P, 512], F32))

            def sem(name):
                return stack.enter_context(nc.semaphore(name))

            def pair(name, shape):
                return (sb(name + "_hi", shape, F32R), sb(name + "_lo", shape, F32R))
            return sb, ps, sem, pair

        sb, _, sem, pair = alloc(whole)
        Wqkv = pair("Wqkv", [P, W_COLS])
        simn = sb("simn", [P, KC, 2, E], F32R)
        ident = sb("ident", [P, P])
        ident_r = sb("ident_r", [P, P], F32R)
        causal_r = sb("causal_r", [P, P], F32R)
        rev = sb("rev", [P, E])
        neg_sig = sb("neg_sig", [P, E])
        neg_half = sb("neg_half", [P, TILES])
        const_ready = sem("const_ready")
        X2 = sb("X2", [P, D])
        x2_in = sem("x2_in")
        st_x2 = [sem(f"st_x2{p}") for p in range(2)]

        first = ExitStack()
        with first:
            sb, ps, sem, pair = alloc(first)
            X = [sb(f"X{p}", [P, TILES, D]) for p in range(2)]
            XR = [sb(f"XR{p}", [P, TILES, D]) for p in range(2)]
            CTX = [sb(f"CTX{p}", [C, D]) for p in range(2)]
            ctx = [pair(f"ctx{p}", [CP, D]) for p in range(2)]
            MASK = [sb(f"MASK{p}", [P, TILES, C], U8) for p in range(2)]
            ctx_centred = sb("ctx_centred", [C, D])
            ctxT = pair("ctxT", [P, KC, CE])
            xT = [pair(f"xT{p}", [P, S]) for p in range(2)]
            scoresT = sb("scoresT", [CE, S])
            keep = sb("keep", [P, TILES, C])
            fill = sb("fill", [P, TILES, C])
            scores = sb("scores", [P, TILES, C])
            E_un = sb("E_un", [P, TILES, C])
            att_f = sb("att_f", [P, TILES, CE])
            att = pair("att", [P, TILES, CE])
            G = pair("G", [CP, D])
            mergeT = pair("mergeT", [P, KC, D])
            stage = sb("stage", [P, W_PIECE])
            sim_f = sb("sim_f", [P, KC, E])
            sim_sq = sb("sim_sq", [P, KC, E])
            sim_ss = sb("sim_ss", [P, E])
            sim_rn = sb("sim_rn", [P, E])
            half_e = sb("half_e", [P, E])
            ones_f = sb("ones_f", [P, P])
            gate_e = sb("gate_e", [P, E])
            bias_f = sb("bias_f", [1, D])
            bias_p = pair("bias_p", [1, D])
            causal_f = sb("causal_f", [P, P])
            stats = sb("stats", [P, TILES, 6])
            mv = sb("mv", [P, TILES, 2])
            var_in = sb("var_in", [P, TILES])
            row_scale = [sb(f"row_scale{p}", [P, TILES]) for p in range(2)]
            ctx_mean = sb("ctx_mean", [C, 2])
            neg_max = sb("neg_max", [P, TILES])
            row_sum = sb("row_sum", [P, TILES])
            row_inv = sb("row_inv", [P, TILES])

            psXT = [ps(f"psXT{p}") for p in range(2)]
            psCT = ps("psCT")
            psST = ps("psST")
            psS = ps("psS")
            psG = ps("psG")
            psX2 = [ps(f"psX2{p}") for p in range(2)]
            psCT_v = psCT[:, 0:KC * CE].rearrange("p (c k) -> p c k", c=KC)
            psS_v = psS[:, 0:TILES * CE].rearrange("p (t k) -> p t k", t=TILES)

            ld_x = [sem(f"ld_x{p}") for p in range(2)]
            ld_ctx = [sem(f"ld_ctx{p}") for p in range(2)]
            ld_mask = [sem(f"ld_mask{p}") for p in range(2)]
            ld_w = sem("ld_w")
            ld_merge = sem("ld_merge")
            ld_sim = sem("ld_sim")
            ld_gates = sem("ld_gates")
            ld_bias = sem("ld_bias")
            bias_placed = sem("bias_placed")
            pool_init = sem("pool_init")
            dve_init = sem("dve_init")
            act_init = sem("act_init")
            sim_normed = sem("sim_normed")
            sim_summed = sem("sim_summed")
            merge_hi = sem("merge_hi")
            merge_lo = sem("merge_lo")
            w_hi = sem("w_hi")
            w_lo = sem("w_lo")
            ctx_hi = sem("ctx_hi")
            ctx_lo = sem("ctx_lo")
            centred = sem("centred")
            ctx_summed = sem("ctx_summed")
            ctxT_moved = sem("ctxT_moved")
            ctxT_hi = sem("ctxT_hi")
            ctxT_lo = sem("ctxT_lo")
            xT_moved = sem("xT_moved")
            xT_hi = sem("xT_hi")
            xT_lo = sem("xT_lo")
            xT_used = sem("xT_used")
            scoresT_out = sem("scoresT_out")
            scores_moved = sem("scores_moved")
            scores_read = sem("scores_read")
            mask_ready = sem("mask_ready")
            var_ready = sem("var_ready")
            scale_ready = sem("scale_ready")
            max_ready = sem("max_ready")
            exp_done = sem("exp_done")
            inv_ready = sem("inv_ready")
            att_scaled = sem("att_scaled")
            att_hi = sem("att_hi")
            att_lo = sem("att_lo")
            G_summed = sem("G_summed")
            G_hi = sem("G_hi")
            G_lo = sem("G_lo")
            resid_kept = sem("resid_kept")
            x2_summed = sem("x2_summed")
            x2_added = sem("x2_added")
            dve_own = sem("dve_own")

            def steps(eng, step, own=None, per=0):
                step(0, 0, True, True, False, False)
                step(1, 1, True, True, True, False)
                with eng.Fori(0, (B - 4) // 2) as n:
                    if own:
                        own.enter(n, per)
                    for p in range(2):
                        step(2 * n + 2 + p, p, True, True, True, True)
                    if own:
                        own.leave(per, (B - 4) // 2)
                step(B - 2, 0, True, True, True, True)
                step(B - 1, 1, True, False, True, True)
                step(B, 0, False, False, True, True)
                step(B + 1, 1, False, False, False, True)

            def turns(i, p):
                return i // 2 + 1 if isinstance(i, int) else (i - p) // 2 + 1

            FREE = 2

            def from_batch(i, least):
                return not isinstance(i, int) or i >= least

            with nc.Block() as block:
                @block.sync
                def _(sp):
                    def tiles_of(dram, i):
                        return dram[bass.ds(i, 1)].rearrange("b (t p) d -> p (b t) d", p=P)

                    sp.dma_start(CTX[0][:], ctx_in[0]).then_inc(ld_ctx[0], 16)
                    sp.dma_start(X[0][:], tiles_of(x, 0)).then_inc(ld_x[0], 16)
                    sp.dma_start(sim_f[:], sim.rearrange("(c p) e -> p c e", p=P)).then_inc(ld_sim, 16)
                    sp.dma_start(MASK[0][:], tiles_of(mask, 0)).then_inc(ld_mask[0], 16)
                    sp.dma_start(gate_e[:], gates.partition_broadcast(P)).then_inc(ld_gates, 16)
                    sp.dma_start(bias_f[:], bias).then_inc(ld_bias, 16)
                    sp.dma_start(CTX[1][:], ctx_in[1]).then_inc(ld_ctx[1], 16)
                    sp.dma_start(X[1][:], tiles_of(x, 1)).then_inc(ld_x[1], 16)
                    sp.dma_start(MASK[1][:], tiles_of(mask, 1)).then_inc(ld_mask[1], 16)
                    sp.dma_start(XR[1][:].rearrange("p t d -> p (t d)"), merge_t).then_inc(ld_merge, 16)
                    w_flat = w_qkv.rearrange("p c n -> p (c n)")
                    sp.dma_start(stage[:], w_flat[:, 0:W_PIECE]).then_inc(ld_w, 16)
                    sp.wait_ge(act_init, 1)
                    sp.dma_start(G[0][C:CP, :].bitcast(F32), bias_p[0][:].bitcast(F32)).then_inc(bias_placed, 16)
                    sp.wait_ge(dve_init, 2)
                    sp.dma_start(G[1][C:CP, :].bitcast(F32), bias_p[1][:].bitcast(F32)).then_inc(bias_placed, 16)

                    def step(i, p, score, ahead, back, tail):
                        if score and from_batch(i, 1):
                            sp.wait_ge(w_hi, i)
                            sp.wait_ge(w_lo, i)
                            sp.dma_start(stage[:], w_flat[:, bass.ds(i * W_PIECE, W_PIECE)]).then_inc(ld_w, 16)
                        if isinstance(i, int) and i == B:
                            sp.wait_ge(st_x2[0], 32)
                            sp.dma_start(X2[:], x2_dram[0, 0:P, :]).then_inc(x2_in, 16)
                        if tail:
                            for h in range(2):
                                sp.wait_ge(x2_added, FREE + TILES * (i - 2) + 2 * h + 2)
                                dst = x2_dram.rearrange("b (h t p) d -> (b h) p t d", p=P, h=2)
                                sp.dma_start(dst[bass.ds(2 * (i - 2) + h, 1)].rearrange("a p t d -> p (a t) d"),
                                             XR[p][:, 2 * h:2 * h + 2, :]).then_inc(st_x2[p], 16)
                        if ahead and not (isinstance(i, int) and i + 2 >= B):
                            sp.wait_ge(xT_moved, KC * (i + 1))
                            sp.wait_ge(resid_kept, i + 1)
                            sp.wait_ge(var_ready, i + 1)
                            sp.wait_ge(mask_ready, i + 1)
                            sp.wait_ge(centred, i + 1)
                            sp.wait_ge(ctx_lo, i + 1)
                            sp.dma_start(X[p][:], tiles_of(x, i + 2)).then_inc(ld_x[p], 16)
                            sp.dma_start(MASK[p][:], tiles_of(mask, i + 2)).then_inc(ld_mask[p], 16)
                            sp.dma_start(CTX[p][:], ctx_in[bass.ds(i + 2, 1)].rearrange("b c d -> (b c) d")
                                         ).then_inc(ld_ctx[p], 16)

                    steps(sp, step)

                @block.gpsimd
                def _(pool):
                    pool.memset(neg_half[:], -0.5).then_inc(pool_init, 1)
                    pool.memset(half_e[:], -0.5).then_inc(pool_init, 1)
                    pool.memset(ones_f[:], 1.0).then_inc(pool_init, 1)
                    pool.wait_ge(pool_init, 3)
                    pool.affine_select(out=ident[:], in_=ones_f[:], compare_op=ALU.is_equal, fill=0.0, base=0,
                                       pattern=[[-1, P]], channel_multiplier=1).then_inc(pool_init, 1)
                    pool.memset(causal_f[:], 0.0).then_inc(pool_init, 1)
                    pool.wait_ge(pool_init, 5)
                    pool.affine_select(out=causal_f[:], in_=causal_f[:], compare_op=ALU.is_ge, fill=CAUSAL_FILL,
                                       base=0, pattern=[[-1, P]], channel_multiplier=1).then_inc(pool_init, 1)
                    pool.iota(rev[:], pattern=[[-1, E]], base=E, channel_multiplier=0,
                              allow_small_or_imprecise_dtypes=True).then_inc(pool_init, 1)

                    def power(m, p):
                        pool.wait_ge(var_ready, m + 1)
                        pool.tensor_tensor(row_scale[p][:], var_in[:], neg_half[:], ALU.pow).then_inc(scale_ready, 1)

                    def masks(i, p):
                        pool.tensor_scalar(keep[:], MASK[p][:], -1.0, 1.0, ALU.mult, ALU.add)
                        pool.tensor_scalar(fill[:], MASK[p][:], NEG_INF, None, ALU.mult).then_inc(mask_ready, 1)

                    def step(i, p, score, ahead, back, tail):
                        if score:
                            pool.wait_ge(ld_mask[p], 16 * turns(i, p))
                        if back:
                            pool.wait_ge(att_hi, i)
                            pool.tensor_tensor(att[1][:], att_f[:], att[0][:].bitcast(F32), ALU.subtract
                                               ).then_inc(att_lo, 1)
                        if score:
                            masks(i, p)
                            pool.wait_ge(ctx_hi, i + 1)
                            pool.tensor_tensor(ctx[p][1][0:C, :], CTX[p][:], ctx[p][0][0:C, :].bitcast(F32),
                                               ALU.subtract).then_inc(ctx_lo, 1)
                        if isinstance(i, int) and i == 0:
                            pool.wait_ge(merge_hi, 1)
                            pool.tensor_tensor(mergeT[1][:], XR[1][:], mergeT[0][:].bitcast(F32), ALU.subtract
                                               ).then_inc(merge_lo, 1)
                        if ahead:
                            power(i + 1, 1 - p)
                        if score:
                            pool.wait_ge(w_hi, i + 1)
                            dst = bass.ds(i * W_PIECE, W_PIECE)
                            pool.tensor_tensor(Wqkv[1][:, dst], stage[:], Wqkv[0][:, dst].bitcast(F32),
                                               ALU.subtract).then_inc(w_lo, 1)
                        if isinstance(i, int) and i == 1:
                            pool.wait_ge(sim_summed, 2)
                            pool.tensor_tensor(sim_rn[:], sim_ss[:], half_e[:], ALU.pow).then_inc(sim_normed, 1)

                    power(0, 0)
                    steps(pool, step)

                @block.scalar
                def _(act):
                    def split_x(i, c):
                        act.wait_ge(xT_moved, KC * i + c + 1)
                        if from_batch(i, 1) or c >= 2:
                            act.wait_ge(xT_used, KC * i + c - 1)
                        act.activation(xT[c % 2][0][:], psXT[c % 2][:], ACT.Copy).then_inc(xT_hi, 1)

                    def split_ahead(m):
                        act.wait_ge(ctxT_moved, m + 1)
                        if from_batch(m, 1):
                            act.wait_ge(xT_used, KC * m)
                        act.activation(ctxT[0][:, :, 0:C], psCT_v[:, :, 0:C], ACT.Copy).then_inc(ctxT_hi, 1)
                        split_x(m, 0)
                        split_x(m, 1)

                    def centre(m, p):
                        act.wait_ge(ld_ctx[p], 16 * turns(m, p))
                        if from_batch(m, 1):
                            act.wait_ge(ctxT_moved, m)
                        act.activation(ctx_centred[:], CTX[p][:], ACT.Copy, scale=-1.0 / D, accum_out=ctx_mean[:, 0:1]
                                       ).then_inc(ctx_summed, 1)
                        act.wait_ge(ctx_summed, m + 1)
                        act.activation(ctx_centred[:], CTX[p][:], ACT.Identity, bias=ctx_mean[:, 0:1]
                                       ).then_inc(centred, 1)

                    def step(i, p, score, ahead, back, tail):
                        if score:
                            split_x(i, 2)
                        if back:
                            act.wait_ge(max_ready, i)
                            for t in range(TILES):
                                act.activation(E_un[:, t, :], scores[:, t, :], ACT.Exp, bias=neg_max[:, t:t + 1],
                                               accum_out=row_sum[:, t:t + 1]).then_inc(exp_done, 1)
                        if score:
                            split_x(i, 3)
                        if back:
                            act.wait_ge(inv_ready, i)
                            if from_batch(i, 2):
                                act.wait_ge(att_lo, i - 1)
                                act.wait_ge(G_summed, i - 1)
                            for t in range(TILES):
                                last = act.activation(att_f[:, t, 0:C], E_un[:, t, :], ACT.Copy,
                                                      scale=row_inv[:, t:t + 1])
                            last.then_inc(att_scaled, 1)
                            act.wait_ge(att_scaled, i)
                            act.activation(att[0][:], att_f[:], ACT.Copy).then_inc(att_hi, 1)
                        if isinstance(i, int) and i == 0:
                            act.wait_ge(ld_merge, 16)
                            act.activation(mergeT[0][:], XR[1][:], ACT.Copy).then_inc(merge_hi, 1)
                        if score:
                            act.wait_ge(xT_used, KC * (i + 1))
                            if from_batch(i, 1):
                                act.wait_ge(scores_moved, i)
                            act.activation(scoresT[:], psST[0:CE, :], ACT.Copy).then_inc(scoresT_out, 1)
                            if from_batch(i, 2):
                                act.wait_ge(x2_summed, TILES * (i - 1))
                            else:
                                act.wait_ge(dve_init, 1)
                            act.activation(ctx[p][0][0:C, :], CTX[p][:], ACT.Copy).then_inc(ctx_hi, 1)
                        if ahead:
                            centre(i + 1, 1 - p)
                        if back:
                            act.wait_ge(G_summed, i)
                            if from_batch(i, 2):
                                act.wait_ge(x2_summed, TILES * (i - 1))
                            act.activation(G[0][0:C, :], psG[0:C, :], ACT.Copy).then_inc(G_hi, 1)
                        if ahead:
                            split_ahead(i + 1)
                        if score:
                            act.wait_ge(ld_w, 16 * (i + 1))
                            dst = bass.ds(i * W_PIECE, W_PIECE)
                            act.activation(Wqkv[0][:, dst], stage[:], ACT.Copy).then_inc(w_hi, 1)
                            if from_batch(i, 2):
                                act.wait_ge(st_x2[p], 32 * (turns(i, p) - 1))
                            elif i == 1:
                                act.wait_ge(merge_lo, 1)
                            act.activation(XR[p][:], X[p][:], ACT.Copy).then_inc(resid_kept, 1)
                        if isinstance(i, int) and i == B - 2:
                            act.wait_ge(sim_normed, 2)
                            act.activation(simn[:, :, 0, :], sim_f[:], ACT.Copy).then_inc(sim_normed, 1)

                    centre(0, 0)
                    act.wait_ge(dve_init, 1)
                    split_ahead(0)
                    act.wait_ge(ld_bias, 16)
                    act.activation(bias_p[0][:], bias_f[:], ACT.Copy).then_inc(act_init, 1)
                    act.wait_ge(ld_gates, 16)
                    act.activation(gate_e[:], gate_e[:], ACT.Exp, scale=-1.0).then_inc(act_init, 1)
                    act.wait_ge(pool_init, 6)
                    act.activation(ident_r[:], ident[:], ACT.Copy).then_inc(const_ready, 1)
                    act.activation(causal_r[:], causal_f[:], ACT.Copy).then_inc(const_ready, 1)

                    steps(act, step)

                @block.vector
                def _(dve):
                    own = Seq()

                    def link(ins):
                        ins.then_inc(dve_own, 1)
                        dve.wait_ge(dve_own, own.step())

                    def lo(dst, src, hi, signal):
                        dve.tensor_tensor(dst, src, hi.bitcast(F32), ALU.subtract).then_inc(signal, 1)

                    def row_stats(m, p):
                        dve.wait_ge(ld_x[p], 16 * turns(m, p))
                        for t in range(TILES):
                            dve.bn_stats(stats[:, t, :], X[p][:, t, :])
                        dve.drain()
                        for t in range(TILES):
                            last = dve.bn_aggr(mv[:, t, :], stats[:, t, :])
                        link(last)
                        if from_batch(m, 1):
                            dve.wait_ge(scale_ready, m)
                        dve.tensor_scalar(var_in[:], mv[:, :, 1], LN_EPS, float(D), ALU.add, ALU.mult
                                          ).then_inc(var_ready, 1)

                    def split_x(i, c):
                        dve.wait_ge(xT_hi, KC * i + c + 1)
                        lo(xT[c % 2][1][:], psXT[c % 2][:], xT[c % 2][0][:], xT_lo)

                    def split_ahead(m):
                        dve.wait_ge(ctxT_hi, m + 1)
                        lo(ctxT[1][:, :, 0:C], psCT_v[:, :, 0:C], ctxT[0][:, :, 0:C], ctxT_lo)
                        split_x(m, 0)
                        split_x(m, 1)

                    def mask_scores(i, p):
                        dve.wait_ge(scores_moved, i + 1)
                        dve.wait_ge(scale_ready, i + 1)
                        dve.wait_ge(mask_ready, i + 1)
                        if from_batch(i, 1):
                            dve.wait_ge(exp_done, TILES * i)
                        for t in range(TILES):
                            last = dve.scalar_tensor_tensor(
                                out=scores[:, t, :], in0=psS_v[:, t, 0:C], scalar=row_scale[p][:, t:t + 1],
                                in1=keep[:, t, :], op0=ALU.mult, op1=ALU.mult)
                        last.then_inc(scores_read, 1)
                        dve.wait_ge(scores_read, i + 1)
                        link(dve.tensor_tensor(scores[:], scores[:], fill[:], ALU.add))
                        dve.tensor_reduce(neg_max[:], scores[:], AX.X, ALU.max, negate=True).then_inc(max_ready, 1)

                    def add_residual(i, p, t):
                        dve.wait_ge(x2_summed, TILES * (i - 2) + t + 1)
                        dve.wait_ge(resid_kept, i - 1)
                        dve.tensor_tensor(XR[p][:, t, :], psX2[t % 2][:], XR[p][:, t, :], ALU.add
                                          ).then_inc(x2_added, 1)

                    def step(i, p, score, ahead, back, tail):
                        if score:
                            split_x(i, 2)
                        if tail:
                            add_residual(i, p, 0)
                        if back:
                            dve.wait_ge(exp_done, TILES * i)
                            dve.reciprocal(row_inv[:], row_sum[:]).then_inc(inv_ready, 1)
                        if score:
                            split_x(i, 3)
                        if tail:
                            for t in range(1, TILES):
                                add_residual(i, p, t)
                        if isinstance(i, int) and i == 0:
                            dve.wait_ge(ld_sim, 16)
                            dve.tensor_tensor(sim_sq[:], sim_f[:], sim_f[:], ALU.mult).then_inc(dve_init, 1)
                            dve.wait_ge(sim_summed, 1)
                            dve.tensor_scalar(sim_ss[:], psG[:, 0:E], NORM_FLOOR ** 2, None, ALU.max
                                              ).then_inc(sim_summed, 1)
                        if ahead:
                            row_stats(i + 1, 1 - p)
                        if back:
                            dve.wait_ge(G_hi, i)
                            lo(G[1][0:C, :], psG[0:C, :], G[0][0:C, :], G_lo)
                        if ahead:
                            split_ahead(i + 1)
                        if score:
                            mask_scores(i, p)
                        if isinstance(i, int) and i == B - 2:
                            link(dve.tensor_scalar(gate_e[:], gate_e[:], 1.0, None, ALU.add))
                            link(dve.reciprocal(gate_e[:], gate_e[:]))
                            dve.tensor_scalar(neg_sig[:], gate_e[:], -1.0, None, ALU.mult).then_inc(const_ready, 1)
                            dve.wait_ge(sim_normed, 1)
                            for c in range(KC):
                                last = dve.tensor_tensor(sim_f[:, c, :], sim_f[:, c, :], sim_rn[:], ALU.mult)
                            last.then_inc(sim_normed, 1)
                            dve.wait_ge(sim_normed, 3)
                            lo(simn[:, :, 1, :], sim_f[:], simn[:, :, 0, :], const_ready)

                    for part in range(2):
                        dve.memset(ctxT[part][:].bitcast(F32), 0.0)
                    for p in range(2):
                        dve.memset(ctx[p][0][:].bitcast(F32), 1.0)
                        dve.memset(ctx[p][1][:].bitcast(F32), 0.0)
                    dve.memset(att_f[:], 0.0).then_inc(dve_init, 1)
                    dve.memset(row_sum[:], 1.0).then_inc(x2_added, FREE)
                    split_ahead(0)
                    row_stats(0, 0)
                    dve.wait_ge(act_init, 2)
                    lo(bias_p[1][:], bias_f[:], bias_p[0][:], dve_init)
                    steps(dve, step, own, 2 * 2)

                @block.tensor
                def _(pe):
                    def move_ctx(m):
                        pe.wait_ge(centred, m + 1)
                        if from_batch(m, 1):
                            pe.wait_ge(ctxT_lo, m)
                        for c in range(KC):
                            last = pe.transpose(psCT_v[:, c, 0:C], ctx_centred[:, c * P:(c + 1) * P],
                                                ident[0:C, 0:C])
                        last.then_inc(ctxT_moved, 1)

                    def move_x(m, p, c):
                        if c == 0:
                            pe.wait_ge(ld_x[p], 16 * turns(m, p))
                        if from_batch(m, 1) or c >= 2:
                            pe.wait_ge(xT_lo, KC * m + c - 1)
                        for t in range(TILES):
                            last = pe.transpose(psXT[c % 2][:, t * P:(t + 1) * P], X[p][:, t, c * P:(c + 1) * P],
                                                ident[:])
                        last.then_inc(xT_moved, 1)

                    def sum_scores(i, c):
                        pe.wait_ge(xT_lo, KC * i + c + 1)
                        if c == 0:
                            pe.wait_ge(ctxT_lo, i + 1)
                            if from_batch(i, 1):
                                pe.wait_ge(scoresT_out, i)
                        for n, (a, b) in enumerate(products(ctxT, xT[c % 2])):
                            last = pe.matmul(psST[0:CE, :], a[:, c, :], b[:],
                                             start=(c == 0 and n == 0), stop=(c == KC - 1 and n == 2))
                        last.then_inc(xT_used, 1)

                    def sum_x2(i, p, t):
                        if t == 0:
                            pe.wait_ge(G_lo, i - 1)
                            pe.wait_ge(ctx_lo, i - 1)
                        pe.wait_ge(x2_added, FREE + TILES * (i - 2) + t - 1)
                        for k, (a, b) in enumerate(products(ctx[p], G)):
                            last = pe.matmul(psX2[t % 2][:], a[:, t * P:(t + 1) * P], b[:],
                                             start=(k == 0), stop=(k == 2))
                        last.then_inc(x2_summed, 1)

                    def step(i, p, score, ahead, back, tail):
                        if score:
                            sum_scores(i, 0)
                            move_x(i, p, 2)
                        if tail:
                            sum_x2(i, p, 0)
                        if score:
                            sum_scores(i, 1)
                            move_x(i, p, 3)
                        if tail:
                            sum_x2(i, p, 1)
                        if score:
                            sum_scores(i, 2)
                        if tail:
                            sum_x2(i, p, 2)
                        if score:
                            sum_scores(i, 3)
                        if tail:
                            sum_x2(i, p, 3)
                        if isinstance(i, int) and i == 0:
                            pe.wait_ge(dve_init, 3)
                            for c in range(KC):
                                last = pe.matmul(psG[:, 0:E], ones_f[:], sim_sq[:, c, :], start=(c == 0),
                                                 stop=(c == KC - 1))
                            last.then_inc(sim_summed, 1)
                        if back:
                            pe.wait_ge(att_lo, i)
                            if isinstance(i, int) and i == 1:
                                pe.wait_ge(merge_lo, 1)
                                pe.wait_ge(bias_placed, 32)
                                pe.wait_ge(sim_summed, 2)
                            else:
                                pe.wait_ge(G_lo, i - 1)
                            for t in range(TILES):
                                for n, (a, b) in enumerate(products(att, mergeT)):
                                    last = pe.matmul(psG[0:CE, :], a[:, t, :], b[:, t, :],
                                                     start=(t == 0 and n == 0), stop=(t == TILES - 1 and n == 2))
                            last.then_inc(G_summed, 1)
                        if score:
                            pe.wait_ge(scoresT_out, i + 1)
                            if from_batch(i, 1):
                                pe.wait_ge(scores_read, i)
                            for t in range(TILES):
                                last = pe.transpose(psS_v[:, t, 0:C], scoresT[0:C, t * P:(t + 1) * P],
                                                    ident[0:C, 0:C])
                            last.then_inc(scores_moved, 1)
                        if ahead:
                            move_ctx(i + 1)
                            move_x(i + 1, 1 - p, 0)
                            move_x(i + 1, 1 - p, 1)

                    pe.wait_ge(pool_init, 4)
                    move_ctx(0)
                    move_x(0, 0, 0)
                    move_x(0, 0, 1)
                    steps(pe, step)

        experts_block(nc, whole, alloc, x2_dram, w_o, out, Wqkv, simn, ident, ident_r, causal_r, rev, neg_sig,
                      neg_half, const_ready, X2, x2_in, st_x2, (B, S, D, E, DH, TILES, KC, Q3, PAIRS, SLOTS, OC, HALF))


def experts_block(nc, whole, alloc, x2_dram, w_o, out, Wqkv, simn, ident, ident_r, causal_r, rev, neg_sig,
                  neg_half, const_ready, X2, x2_in, st_x2, sizes):
    B, S, D, E, DH, TILES, KC, Q3, PAIRS, SLOTS, OC, HALF = sizes
    N_TILES = B * TILES
    PW = 2 * Q3
    GK = 32 + E
    sb, ps, sem, pair = alloc(whole)
    Wo = pair("Wo", [P, OC, D])
    H = sb("H", [P, D])
    hT = [pair(f"hT{p}", [P, D]) for p in range(2)]
    acc = [sb(f"acc{k}", [P, Q3]) for k in range(2)]
    nat = [sb(f"nat{p}", [P, Q3]) for p in range(2)]
    qkT = pair("qkT", [DH, 2, S])
    V = pair("V", [P, TILES, 2, DH])
    probs = [sb(f"probs{p}", [P, S]) for p in range(2)]
    probsT = [pair(f"probsT{h}", [P, (4 * h + 3) * P]) for h in range(2)]
    attT = [sb(f"attT{h}", [P, 2 * P]) for h in range(2)]
    gates_q = sb("gates_q", [P, (TILES + 1) * 64])
    gatesT = sb("gatesT", [GK, S], F32R)
    spread = sb("spread", [GK, OC, P], F32R)
    mixed_f = [sb(f"mixed_f{p}", [P, 2, 2 * P]) for p in range(2)]
    mixedT = pair("mixedT", [P, OC, 2 * P])
    resid = [sb(f"resid{p}", [P, D]) for p in range(2)]
    RW = sb("RW", [P, TILES, E])
    stats = sb("b_stats", [P, 6])
    mv = sb("b_mv", [P, 2])
    pow_tmp = sb("pow_tmp", [P, 2])
    eps = sb("eps", [P, 1])
    pow_out = [sb(f"pow_out{p}", [P, 2]) for p in range(2)]
    neg_mx = [sb(f"neg_mx{p}", [P, 2]) for p in range(2)]
    p_sum = [sb(f"p_sum{p}", [P, 1]) for p in range(2)]
    p_inv = [sb(f"p_inv{p}", [P, 1]) for p in range(2)]
    logitT = sb("logitT", [P, P])
    logit = sb("logit", [P, E])
    logit_lo = sb("logit_lo", [P, E])
    rank = sb("rank", [P, E])
    pick1 = sb("pick1", [P, E])
    picks = sb("picks", [P, E])
    other = sb("other", [P, E])
    active = sb("active", [P, E])
    chosen = picks
    gate_in, gate_exp = other, rank
    g1 = sb("g1", [P, 8])

    psQ = [ps(f"psQ{k}") for k in range(4)]
    psT = [ps(f"psT{k}") for k in range(2)]
    psM = ps("psM")
    psO = ps("psO")

    ld_wo = [sem(f"ld_wo{p}") for p in range(2)]
    wo_hi, wo_lo = sem("wo_hi"), sem("wo_lo")
    res_in = [sem(f"res_in{p}") for p in range(2)]
    y_out = [sem(f"y_out{p}") for p in range(2)]
    stats_ready, eps_made = sem("stats_ready"), sem("eps_made")
    pow_done, norm_done = sem("pow_done"), sem("norm_done")
    h_ready = sem("h_ready")
    moved = sem("moved")
    moved_hi = sem("moved_hi")
    moved_lo = sem("moved_lo")
    logits_moved, logitT_zero = sem("logits_moved"), sem("logitT_zero")
    qkv_summed = sem("qkv_summed")
    expert_added = sem("expert_added")
    nat_ready = sem("nat_ready")
    v_hi, v_lo = sem("v_hi"), sem("v_lo")
    scored = sem("scored")
    neg_max_ready = sem("neg_max_ready")
    exp_done = sem("b_exp_done")
    valued = sem("valued")
    inv_made = sem("inv_made")
    gates_divided = sem("gates_divided")
    attT_out = sem("attT_out")
    mix_hi, mix_lo = sem("mix_hi"), sem("mix_lo")
    spread_made = sem("spread_made")
    projected = sem("projected")
    y_ready = sem("y_ready")
    gate_in_ready, gate_exp_ready = sem("gate_in_ready"), sem("gate_exp_ready")
    rw_ready = sem("rw_ready")
    own2 = sem("own2")

    MOVES, HIS = 26, 18
    WO_EVERY = 2
    LOOP = B - 3

    def bodies(eng, body, seqs):
        body(0, True, False, True)
        body(1, True, True, True)
        with eng.Fori(0, LOOP) as n:
            for s, per in seqs:
                s.enter(n, per)
            body(n + 2, True, True, True)
            for s, per in seqs:
                s.leave(per, LOOP)
        body(B - 1, True, True, False)
        body(B, False, True, False)

    def job_lists(k, b, qkv, lead, last_prep):
        j, g = divmod(k, PAIRS)
        prepare = qkv and (last_prep or j < TILES - 1)
        own = k >= LEAD
        return j, g, prepare, (qkv if own else lead), (b if own else b - 1)

    def tile_copies(k, qkv, lead):
        if k in QK_T_AT and (lead if k == 0 else qkv):
            return QK_T_AT[k]
        return None

    def place(i):
        return slice((1 - i % 2) * P, (2 - i % 2) * P)

    def keys_of(half, i):
        blocks = 2 * (i - i % 2) + 3
        return half[:].rearrange("p (s l) -> p s l", l=P)[:, 1 - i % 2:blocks:2, :]

    def y_bank(i, qkv):
        return psO if qkv or i < TILES - 1 else psQ[0]

    def v_twice(i):
        return nat[i % 2][:, 2 * DH:Q3].unsqueeze(1).broadcast_to([P, 2, DH])

    with nc.Block() as block:
        @block.sync
        def _(sp):
            for p in range(2):
                sp.wait_ge(st_x2[p], 16 * B)

            def load_wo(n):
                if n >= 2:
                    sp.wait_ge(wo_lo, n - 1)
                sp.dma_start(mixed_f[n % 2][:].rearrange("p a l -> p (a l)"), w_o[:, n, :]).then_inc(ld_wo[n % 2], 16)

            def row(dram, b, t):
                return dram.rearrange("b (t p) d -> (b t) p d", p=P)[bass.ds(TILES * b + t, 1)].rearrange(
                    "a p d -> p (a d)")

            def store_y(b, i):
                sp.wait_ge(y_ready, TILES * b + i + 1)
                sp.dma_start(row(out, b, i), resid[i % 2][:]).then_inc(y_out[i % 2], 16)

            def load_resid(b, i):
                if not isinstance(b, int) or TILES * b + i >= 2:
                    sp.wait_ge(y_out[i % 2], 16 * (2 * b + i // 2))
                sp.dma_start(resid[i % 2][:], row(x2_dram, b, i)).then_inc(res_in[i % 2], 16)

            def body(b, qkv, lead, prep):
                for j in range(TILES):
                    if qkv and (prep or j < TILES - 1):
                        sp.wait_ge(h_ready, TILES * b + j + 1)
                        sp.dma_start(X2[:], row(x2_dram, b, j + 1)).then_inc(x2_in, 16)
                    if not lead and j < 2:
                        for n in range(OC // 2):
                            load_wo(j * OC // 2 + n)
                    if lead and j == 0:
                        load_resid(b - 1, 2)
                        load_resid(b - 1, 3)
                    if lead and j == 1:
                        store_y(b - 1, 2)
                        store_y(b - 1, 3)
                    if qkv and j == 2:
                        load_resid(b, 0)
                        load_resid(b, 1)
                    if qkv and j == 3:
                        store_y(b, 0)
                        store_y(b, 1)

            bodies(sp, body, [])
            for p in range(2):
                sp.wait_ge(y_out[p], 16 * (N_TILES // 2))

        @block.gpsimd
        def _(pool):
            def powers(t, p):
                pool.wait_ge(stats_ready, t + 1)
                pool.tensor_tensor(pow_tmp[:, 0:1], mv[:, 1:2], eps[:], ALU.add)
                pool.tensor_scalar(pow_tmp[:, 1:2], mv[:, 1:2], float(D), None, ALU.mult)
                pool.drain()
                pool.tensor_tensor(pow_out[p][:, 0:1], pow_tmp[:, 0:1], neg_half[:, 0:1], ALU.pow
                                   ).then_inc(pow_done, 1)
                pool.drain()
                for _ in range(2):
                    pool.tensor_tensor(pow_tmp[:, 1:2], pow_tmp[:, 1:2], pow_out[p][:, 0:1], ALU.mult)
                    pool.drain()
                pool.tensor_scalar(pow_tmp[:, 1:2], pow_tmp[:, 1:2], NORM_FLOOR ** 2, None, ALU.max)
                pool.drain()
                pool.tensor_tensor(pow_out[p][:, 1:2], pow_tmp[:, 1:2], neg_half[:, 0:1], ALU.pow
                                   ).then_inc(norm_done, 1)

            pool.memset(eps[:], LN_EPS).then_inc(eps_made, 1)
            pool.wait_ge(eps_made, 1)
            pool.memset(gates_q[:], 0.0).then_inc(spread_made, 1)
            pool.memset(logitT[:], 0.0).then_inc(logitT_zero, 1)
            powers(0, 0)
            done = 1
            for p in range(2):
                pool.memset(probs[p][:], 0.0).then_inc(spread_made, 1)
                done += 1
            pool.wait_ge(spread_made, done)
            for sign, base in (None, None), (1, 0), (-1, DH - 1):
                for p in range(2):
                    for row in (0, 32):
                        rows = probs[p][row:row + E, :].rearrange("k (c m) -> k c m", m=P)
                        if sign is None:
                            pool.memset(rows, 1.0).then_inc(spread_made, 1)
                        else:
                            shift = sign * 2 * DH * p * OC // 2
                            pool.affine_select(out=rows, in_=rows, compare_op=ALU.is_ge, fill=0.0, base=base + shift,
                                               pattern=[[sign * 2 * DH, OC // 2], [sign, P]],
                                               channel_multiplier=-sign * DH).then_inc(spread_made, 1)
                        done += 1
                pool.wait_ge(spread_made, done)
            for p in range(2):
                pool.tensor_copy(spread[:, p * OC // 2:(p + 1) * OC // 2, :],
                                 probs[p][0:GK, :].rearrange("k (c m) -> k c m", m=P)).then_inc(spread_made, 1)

            def body(b, qkv, lead, prep):
                for k in range(SLOTS):
                    j, g, prepare, attn, ab = job_lists(k, b, qkv, lead, prep)
                    t = TILES * b + j
                    if prepare and g == STATS_SLOT:
                        powers(t + 1, (j + 1) % 2)
                    if not lead and k % WO_EVERY == 0 and k < WO_EVERY * OC:
                        n = k // WO_EVERY
                        pool.wait_ge(wo_hi, n + 1)
                        pool.tensor_tensor(Wo[1][:, n, :], mixed_f[n % 2][:].rearrange("p a l -> p (a l)"),
                                           Wo[0][:, n, :].bitcast(F32), ALU.subtract).then_inc(wo_lo, 1)
                    if attn and k in GATES_AT:
                        i = GATES_AT[k]
                        a = TILES * ab + i
                        pool.wait_ge(inv_made, a + 1)
                        pool.wait_ge(rw_ready, a + 1)
                        twice = gates_q[:, i * 64:(i + 1) * 64].rearrange("p (r e) -> p r e", r=2)[:, :, 0:E]
                        rw = RW[:, i, :].unsqueeze(1).broadcast_to([P, 2, E])
                        inv = p_inv[i % 2][:].unsqueeze(2).broadcast_to([P, 2, E])
                        pool.tensor_tensor(twice, rw, inv, ALU.mult).then_inc(gates_divided, 1)
                    if attn and k in MIX_AT:
                        h, u = MIX_AT[k]
                        pool.wait_ge(mix_hi, 2 * TILES * ab + 4 * h + u + 1)
                        pair_of = slice(2 * u, 2 * u + 2)
                        pool.tensor_tensor(mixedT[1][:, pair_of, :], mixed_f[u % 2][:],
                                           mixedT[0][:, pair_of, :].bitcast(F32), ALU.subtract).then_inc(mix_lo, 1)

            bodies(pool, body, [])

        @block.scalar
        def _(act):
            moves = Seq()

            def copy_h(t, p):
                if not isinstance(t, int) or t >= 2:
                    act.wait_ge(qkv_summed, PAIRS * (t - 1))
                act.wait_ge(moved, moves.step())
                act.activation(hT[p][0][:], psT[moves.bank()][:], ACT.Copy).then_inc(moved_hi, 1)

            def gate(t):
                act.wait_ge(gate_in_ready, t + 1)
                act.activation(gate_exp[:], gate_in[:], ACT.Exp).then_inc(gate_exp_ready, 1)

            def copy_logits():
                act.wait_ge(moved, moves.step())
                act.activation(logitT[0:2 * E, :], psT[moves.bank()][0:2 * E, 0:P], ACT.Copy).then_inc(moved_hi, 1)

            copy_h(0, 0)
            act.wait_ge(logitT_zero, 1)
            copy_logits()
            gate(0)
            def body(b, qkv, lead, prep):
                for k in range(SLOTS):
                    j, g, prepare, attn, ab = job_lists(k, b, qkv, lead, prep)
                    t = TILES * b + j
                    if prepare and g == H_T_SLOT:
                        copy_h(t + 1, (j + 1) % 2)
                    if not lead and k % WO_EVERY == 0 and k < WO_EVERY * OC:
                        n = k // WO_EVERY
                        act.wait_ge(ld_wo[n % 2], 16 * (n // 2 + 1))
                        act.activation(Wo[0][:, n, :], mixed_f[n % 2][:].rearrange("p a l -> p (a l)"), ACT.Copy
                                       ).then_inc(wo_hi, 1)
                    if attn and k in PROBS_T_AT:
                        i = PROBS_T_AT[k]
                        n = moves.step()
                        act.wait_ge(moved, n)
                        if not isinstance(ab, int) or ab >= 1:
                            act.wait_ge(valued, 2 * (ab - 1) + i // 2 + 1)
                        act.activation(keys_of(probsT[i // 2][0], i),
                                       psT[moves.bank()][:, 0:(i + 1) * P].rearrange("p (s l) -> p s l", l=P),
                                       ACT.Copy).then_inc(moved_hi, 1)
                    i = tile_copies(k, qkv, lead)
                    if i is not None:
                        bt = b - 1 if k == 0 else b
                        n = moves.step()
                        act.wait_ge(moved, n)
                        if not isinstance(b, int) or bt >= 1:
                            act.wait_ge(scored, TILES * bt)
                            act.wait_ge(valued, 2 * bt)
                        src = psT[moves.bank()][0:DH, 0:2 * P].rearrange("p (a s) -> p a s", a=2)
                        act.activation(qkT[0][:, :, i * P:(i + 1) * P], src, ACT.Copy).then_inc(moved_hi, 1)
                        act.activation(V[0][:, i, :, :], v_twice(i), ACT.Copy).then_inc(v_hi, 1)
                    if attn and k in GATES_T_AT:
                        h = GATES_T_AT[k]
                        n = moves.step()
                        act.wait_ge(moved, n)
                        act.activation(gatesT[:, h * 2 * P:(h + 1) * 2 * P], psT[moves.bank()][0:GK, 0:2 * P], ACT.Copy
                                       ).then_inc(moved_hi, 1)
                    if attn and k in MIX_AT:
                        h, u = MIX_AT[k]
                        act.wait_ge(moved_lo, moves.step())
                        if h == 1:
                            act.wait_ge(projected, 8 * ab + 3 + u // 2)
                        elif not isinstance(ab, int) or ab >= 1:
                            act.wait_ge(projected, 8 * (ab - 1) + 7 + u // 2)
                        act.activation(mixedT[0][:, 2 * u:2 * u + 2, :], mixed_f[u % 2][:], ACT.Copy
                                       ).then_inc(mix_hi, 1)
                    if prepare and g == LOGITS_SLOT:
                        copy_logits()
                    if attn and k in SCORES_AT:
                        i = SCORES_AT[k]
                        act.wait_ge(neg_max_ready, TILES * ab + i + 1)
                        if isinstance(ab, int) and ab == 0 and i < 2:
                            act.wait_ge(spread_made, 17)
                        act.activation(probs[i % 2][:, 0:(i + 1) * P], psM[:, 0:(i + 1) * P], ACT.Exp,
                                       bias=neg_mx[i % 2][:, 1:2], scale=HEAD_SCALE,
                                       accum_out=p_sum[i % 2][:]).then_inc(exp_done, 1)
                    if attn and k in VALUES_AT:
                        h = VALUES_AT[k]
                        act.wait_ge(valued, 2 * ab + h + 1)
                        act.activation(attT[h][:], psM[:, 0:2 * P], ACT.Copy).then_inc(attT_out, 1)
                    if prepare and g == LOGITS_SLOT + 2:
                        gate(t + 1)

            bodies(act, body, [(moves, MOVES)])

        @block.vector
        def _(dve):
            own, moves, his = Seq(), Seq(), Seq()

            def link(ins):
                ins.then_inc(own2, 1)
                dve.wait_ge(own2, own.step())

            def lo(dst, cols, dst_hi, view=None):
                moves.step()
                bank = psT[moves.bank()]
                src = bank[:, cols] if view is None else view(bank)
                dve.wait_ge(moved_hi, his.step())
                dve.tensor_tensor(dst, src, dst_hi.bitcast(F32), ALU.subtract).then_inc(moved_lo, 1)

            def row_stats(t):
                dve.wait_ge(x2_in, 16 * (t + 1))
                dve.bn_stats(stats[:], X2[:])
                dve.drain()
                dve.bn_aggr(mv[:], stats[:]).then_inc(stats_ready, 1)

            def normalise(t, p):
                dve.wait_ge(pow_done, t + 1)
                dve.tensor_scalar(H[:], X2[:], mv[:, 0:1], pow_out[p][:, 0:1], ALU.subtract, ALU.mult
                                  ).then_inc(h_ready, 1)

            def read_logits(t, p):
                dve.wait_ge(logits_moved, t + 1)
                dve.wait_ge(norm_done, t + 1)
                n = moves.step()
                his.step()
                bank = psT[moves.bank()]
                link(dve.scalar_tensor_tensor(out=logit_lo[:], in0=bank[:, P + E:P + 2 * E],
                                              scalar=pow_out[p][:, 1:2], in1=neg_sig[:], op0=ALU.mult, op1=ALU.add))
                dve.scalar_tensor_tensor(out=logit[:], in0=bank[:, P:P + E], scalar=pow_out[p][:, 1:2],
                                         in1=logit_lo[:], op0=ALU.mult, op1=ALU.add).then_inc(moved_lo, 1)
                dve.wait_ge(moved_lo, n)

            def gates_1():
                link(dve.tensor_reduce(g1[:, 0:1], logit[:], AX.X, ALU.max))
                link(dve.scalar_tensor_tensor(out=rank[:], in0=logit[:], scalar=g1[:, 0:1], in1=rev[:],
                                              op0=ALU.is_equal, op1=ALU.mult))
                link(dve.tensor_reduce(g1[:, 1:2], rank[:], AX.X, ALU.max))
                link(dve.tensor_scalar(pick1[:], rev[:], g1[:, 1:2], None, ALU.is_equal))
                link(dve.scalar_tensor_tensor(out=other[:], in0=pick1[:], scalar=CAUSAL_FILL, in1=logit[:],
                                              op0=ALU.mult, op1=ALU.add))
                link(dve.tensor_reduce(g1[:, 2:3], other[:], AX.X, ALU.max))

            def gates_2(t, p):
                link(dve.scalar_tensor_tensor(out=rank[:], in0=other[:], scalar=g1[:, 2:3], in1=rev[:],
                                              op0=ALU.is_equal, op1=ALU.mult))
                link(dve.tensor_reduce(g1[:, 3:4], rank[:], AX.X, ALU.max))
                dve.tensor_scalar(active[:], logit[:], 0.0, None, ALU.is_gt)
                dve.tensor_scalar(g1[:, 4:5], g1[:, 0:1], 0.0, None, ALU.is_le)
                dve.tensor_scalar(g1[:, 5:6], g1[:, 0:1], -1.0, 0.0, ALU.mult, ALU.min)
                link(dve.scalar_tensor_tensor(out=picks[:], in0=rev[:], scalar=g1[:, 3:4], in1=pick1[:],
                                              op0=ALU.is_equal, op1=ALU.add))
                dve.tensor_scalar(gate_in[:], logit[:], 0.0, g1[:, 5:6], ALU.max, ALU.add).then_inc(gate_in_ready, 1)
                link(dve.scalar_tensor_tensor(out=chosen[:], in0=picks[:], scalar=g1[:, 4:5], in1=active[:],
                                              op0=ALU.mult, op1=ALU.add))

            def gates_3(t, j):
                dve.wait_ge(gate_exp_ready, t + 1)
                link(dve.tensor_tensor(chosen[:], chosen[:], gate_exp[:], ALU.mult))
                link(dve.tensor_reduce(g1[:, 6:7], chosen[:], AX.X, ALU.add))
                link(dve.reciprocal(g1[:, 7:8], g1[:, 6:7]))
                if not isinstance(t, int) or t >= TILES:
                    dve.wait_ge(gates_divided, t - TILES + 1)
                dve.tensor_scalar(RW[:, j, :], chosen[:], g1[:, 7:8], None, ALU.mult).then_inc(rw_ready, 1)

            row_stats(0)
            normalise(0, 0)
            lo(hT[0][1][:], slice(0, D), hT[0][0][:])
            read_logits(0, 0)
            gates_1()
            gates_2(0, 0)
            gates_3(0, 0)

            def body(b, qkv, lead, prep):
                for k in range(SLOTS):
                    j, g, prepare, attn, ab = job_lists(k, b, qkv, lead, prep)
                    t = TILES * b + j
                    tp = j % 2
                    if qkv:
                        dve.wait_ge(qkv_summed, SLOTS * b + k + 1)
                        if g == 0:
                            dve.wait_ge(rw_ready, t + 1)
                        for e in range(2):
                            src = psQ[g % 4][:, e * Q3:(e + 1) * Q3]
                            w = RW[:, j, 2 * g + e:2 * g + e + 1]
                            if g == 0:
                                dve.tensor_scalar(acc[e][:], src, w, None, ALU.mult).then_inc(expert_added, 1)
                            else:
                                dve.wait_ge(expert_added, 2 * (SLOTS * b + k) + e - 1)
                                dve.scalar_tensor_tensor(out=acc[e][:], in0=src, scalar=w, in1=acc[e][:],
                                                         op0=ALU.mult, op1=ALU.add).then_inc(expert_added, 1)
                    if qkv and g == PAIRS - 1:
                        dve.wait_ge(expert_added, 2 * (SLOTS * b + k + 1))
                        dve.tensor_tensor(nat[tp][:], acc[0][:], acc[1][:], ALU.add).then_inc(nat_ready, 1)
                    if attn and k in Y_AT:
                        i = Y_AT[k]
                        a = TILES * ab + i
                        dve.wait_ge(projected, 2 * a + 2)
                        dve.wait_ge(res_in[i % 2], 16 * (2 * ab + i // 2 + 1))
                        dve.tensor_tensor(resid[i % 2][:], y_bank(i, qkv)[:], resid[i % 2][:], ALU.add).then_inc(y_ready, 1)
                    if attn and k in SCORES_AT:
                        i = SCORES_AT[k]
                        dve.wait_ge(scored, TILES * ab + i + 1)
                        link(dve.tensor_reduce(neg_mx[i % 2][:, 0:1], psM[:, 0:(i + 1) * P], AX.X, ALU.max,
                                               negate=True))
                        dve.tensor_scalar(neg_mx[i % 2][:, 1:2], neg_mx[i % 2][:, 0:1], HEAD_SCALE, None, ALU.mult
                                          ).then_inc(neg_max_ready, 1)
                    if prepare and g == LOGITS_T_SLOT:
                        read_logits(t + 1, 1 - tp)
                    if prepare and g == H_T_SLOT:
                        lo(hT[1 - tp][1][:], slice(0, D), hT[1 - tp][0][:])
                    if attn and k in PROBS_T_AT:
                        i = PROBS_T_AT[k]
                        lo(keys_of(probsT[i // 2][1], i), None, keys_of(probsT[i // 2][0], i),
                           lambda bank: bank[:, 0:(i + 1) * P].rearrange("p (s l) -> p s l", l=P))
                    n = tile_copies(k, qkv, lead)
                    if n is not None:
                        bt = b - 1 if k == 0 else b
                        lo(qkT[1][:, :, n * P:(n + 1) * P], None, qkT[0][:, :, n * P:(n + 1) * P],
                           lambda bank: bank[0:DH, 0:2 * P].rearrange("p (a s) -> p a s", a=2))
                        dve.wait_ge(v_hi, TILES * bt + n + 1)
                        dve.tensor_tensor(V[1][:, n, :, :], v_twice(n), V[0][:, n, :, :].bitcast(F32),
                                          ALU.subtract).then_inc(v_lo, 1)
                    if attn and k in GATES_T_AT:
                        h = GATES_T_AT[k]
                        where = (slice(32, GK), slice(h * 2 * P, (h + 1) * 2 * P))
                        lo(gatesT[where], None, gatesT[where], lambda bank: bank[32:GK, 0:2 * P])
                    if attn and k in MIX_AT:
                        h, u = MIX_AT[k]
                        m = 8 * ab + 4 * h + u + 1
                        dve.wait_ge(moved, moves.step())
                        dve.wait_ge(attT_out, 2 * ab + h + 1)
                        if not isinstance(b, int) or m > 2:
                            dve.wait_ge(mix_lo, m - 2)
                        else:
                            dve.wait_ge(wo_lo, OC)
                        dve.tensor_tensor(mixed_f[u % 2][:],
                                          psT[moves.bank()][:].rearrange("p (c l) -> p c l", c=2),
                                          attT[h][:].unsqueeze(1).broadcast_to([P, 2, 2 * P]), ALU.mult
                                          ).then_inc(moved_lo, 1)
                    if prepare and g == NORM_SLOT:
                        normalise(t + 1, 1 - tp)
                    if attn and k in GATES_AT:
                        i = GATES_AT[k]
                        a = TILES * ab + i
                        dve.wait_ge(exp_done, a + 1)
                        if not isinstance(b, int) or a >= 2:
                            dve.wait_ge(gates_divided, a - 1)
                        dve.reciprocal(p_inv[i % 2][:], p_sum[i % 2][:]).then_inc(inv_made, 1)
                    if prepare and g == LOGITS_T_SLOT:
                        gates_1()
                    if prepare and g == LOGITS_T_SLOT + 1:
                        gates_2(t + 1, 1 - tp)
                    if prepare and g == LOGITS_T_SLOT + 2:
                        gates_3(t + 1, (j + 1) % TILES)
                    if prepare and g == STATS_SLOT:
                        row_stats(t + 1)

            bodies(dve, body, [(own, OWN_STEPS), (moves, MOVES), (his, HIS)])

        @block.tensor
        def _(pe):
            moves, his = Seq(), Seq()

            def next_bank(ready, value, has_high=True):
                n = moves.step()
                if has_high:
                    his.step()
                if not isinstance(n, int) or n >= 3:
                    pe.wait_ge(moved_lo, n - 2)
                pe.wait_ge(ready, value)
                return psT[moves.bank()]

            def move_h(t):
                bank = next_bank(h_ready, t + 1)
                for c in range(KC):
                    last = pe.transpose(bank[:, c * P:(c + 1) * P], H[:, c * P:(c + 1) * P], ident[:])
                last.then_inc(moved, 1)

            def sum_logits(p, h_moved):
                bank = next_bank(moved_lo, h_moved)
                order = [(0, c) for c in range(KC - 1)] + [(1, c) for c in range(KC)] + [(0, KC - 1)]
                for n, (part, c) in enumerate(order):
                    rows = (2 - part) * E
                    last = pe.matmul(bank[0:rows, 0:P], simn[:, c, 0:2 - part, :].rearrange("p r e -> p (r e)"),
                                     hT[p][part][:, c * P:(c + 1) * P], start=(n == 0), stop=(n == len(order) - 1),
                                     skip_group_check=True)
                last.then_inc(moved, 1)
                return bank, his.now()

            def move_logits(bank, job):
                pe.wait_ge(moved_hi, job)
                pe.transpose(bank[:, P:2 * P], logitT[:], ident[:]).then_inc(logits_moved, 1)

            move_h(0)
            first_logits = sum_logits(0, moves.now())
            Wv = [w[:].rearrange("p (c n) -> p c n", c=KC) for w in Wqkv]

            def body(b, qkv, lead, prep):
                qk_moved = {}
                h_moved = logits = None
                probs_moved, gates_in_place = {}, {}
                for k in range(SLOTS):
                    j, g, prepare, attn, ab = job_lists(k, b, qkv, lead, prep)
                    t = TILES * b + j
                    tp = j % 2
                    if qkv:
                        n = SLOTS * b + k
                        if not isinstance(b, int) or n >= 4:
                            pe.wait_ge(expert_added, 2 * (n - 3))
                        for c in range(KC):
                            for m, (x, w) in enumerate(products(hT[tp], Wv)):
                                last = pe.matmul(psQ[g % 4][:, 0:PW], x[:, c * P:(c + 1) * P],
                                                 w[:, c, g * PW:(g + 1) * PW],
                                                 start=(c == 0 and m == 0), stop=(c == KC - 1 and m == 2))
                        last.then_inc(qkv_summed, 1)
                    if k == 0 and not lead:
                        move_logits(*first_logits)
                    if prepare and g == H_T_SLOT:
                        move_h(t + 1)
                        h_moved = moves.now()
                    if prepare and g == LOGITS_T_SLOT:
                        move_logits(*logits)
                    if attn and k in PROBS_T_AT:
                        i = PROBS_T_AT[k]
                        bank = next_bank(exp_done, TILES * ab + i + 1)
                        for s in range(i + 1):
                            last = pe.transpose(bank[:, s * P:(s + 1) * P], probs[i % 2][:, s * P:(s + 1) * P],
                                                ident[:])
                        last.then_inc(moved, 1)
                        probs_moved[i] = moves.now()
                    i = tile_copies(k, qkv, lead)
                    if i is not None:
                        bank = next_bank(nat_ready, TILES * (b - 1 if k == 0 else b) + i + 1)
                        for s in range(2):
                            last = pe.transpose(bank[:, s * P:(s + 1) * P], nat[i % 2][:, s * DH:s * DH + P],
                                                ident[:])
                        last.then_inc(moved, 1)
                        qk_moved[i] = moves.now()
                    if attn and k in GATES_T_AT:
                        h = GATES_T_AT[k]
                        bank = next_bank(gates_divided, TILES * ab + 2 * h + 2)
                        for s in range(2):
                            last = pe.transpose(bank[:, place(s)], gates_q[:, (2 * h + s) * 64:(2 * h + s + 2) * 64],
                                                ident[:])
                        last.then_inc(moved, 1)
                        gates_in_place[h] = moves.now()
                    if attn and k in MIX_AT:
                        h, u = MIX_AT[k]
                        if isinstance(ab, int) and ab == 0 and (h, u) == (0, 0):
                            pe.wait_ge(spread_made, 17)
                        bank = next_bank(moved_lo, gates_in_place[h], has_high=False)
                        for s in range(2):
                            last = pe.matmul(bank[:, s * 2 * P:(s + 1) * 2 * P], spread[:, 2 * u + s, :],
                                             gatesT[:, h * 2 * P:(h + 1) * 2 * P], start=True, stop=True)
                        last.then_inc(moved, 1)
                    if attn and k in SCORES_AT:
                        i = SCORES_AT[k]
                        if i % 2 == 1:
                            pe.wait_ge(exp_done, TILES * ab + i)
                        elif i == 2:
                            pe.wait_ge(attT_out, 2 * ab + 1)
                        elif not isinstance(ab, int) or ab >= 1:
                            pe.wait_ge(attT_out, 2 * ab)
                        pe.wait_ge(moved_lo, qk_moved[i])
                        cols = slice(0, (i + 1) * P)
                        for n, (q, kk) in enumerate(products(qkT, qkT)):
                            last = pe.matmul(psM[:, cols], q[:, 0, i * P:(i + 1) * P], kk[:, 1, cols],
                                             start=(n == 0), stop=(n == 2), skip_group_check=True)
                            if n == 0:
                                pe.matmul(psM[:, i * P:(i + 1) * P], ident_r[:], causal_r[:], start=False,
                                          stop=False, skip_group_check=True)
                        last.then_inc(scored, 1)
                    if attn and k in VALUES_AT:
                        h = VALUES_AT[k]
                        pe.wait_ge(exp_done, TILES * ab + 2 * h + 2)
                        pe.wait_ge(moved_lo, probs_moved[2 * h + 1])
                        pe.wait_ge(v_lo, TILES * ab + 2 * h + 2)
                        last_keys = 2 * h + 1
                        order = [(0, n) for n in range(2)] + [(s, n) for s in range(last_keys, 0, -1) for n in range(3)]
                        order.append((0, 2))
                        for m, (s, n) in enumerate(order):
                            cols = slice(0, P if s == last_keys else 2 * P)
                            v, x = products(V, probsT[h])[n]
                            last = pe.matmul(psM[:, cols], v[:, s, :, :].rearrange("p r d -> p (r d)"), 
                                             x[:, s * 2 * P:s * 2 * P + cols.stop],
                                             start=(m == 0), stop=(m == len(order) - 1), skip_group_check=True)
                        last.then_inc(valued, 1)
                    if prepare and g == LOGITS_SLOT:
                        logits = sum_logits(1 - tp, h_moved)
                    for i, part in PROJECT_AT.get(k, []) if attn else []:
                        a = TILES * ab + i
                        pe.wait_ge(mix_lo, 8 * ab + 4 * (i // 2) + 2 * part + 2)
                        bank = y_bank(i, qkv)
                        if part == 0 and bank is psO and not (isinstance(ab, int) and a == 0):
                            pe.wait_ge(y_ready, a)
                        pe.wait_ge(wo_lo, OC)
                        for c in range(part * HALF, (part + 1) * HALF):
                            for n, (x, w) in enumerate(products(mixedT, Wo)):
                                last = pe.matmul(bank[:], x[:, c, place(i)], w[:, c, :],
                                                 start=(c == 0 and n == 0), stop=(c == OC - 1 and n == 2))
                        last.then_inc(projected, 1)

            bodies(pe, body, [(moves, MOVES), (his, HIS)])


OWN_STEPS = 4 * (7 + 4 + 3) + 4

_OUTS = [((8, 512, 512), 'float32')]


def kernel(x, ctx_1024, mask_BxSxS2_bk1, L0_xattn_W_merge, L0_xattn_b_merge, L0_ffn_sim_matrix, L0_ffn_gates,
           L0_ffn_q_proj, L0_ffn_k_proj, L0_ffn_v_proj, L0_ffn_o_proj):
    import numpy as _np
    import concourse.bacc as _bacc
    from concourse import mybir as _mybir
    from concourse.bass_utils import run_bass_kernel_spmd as _run

    E, D, DH = L0_ffn_q_proj.shape

    def rows_on_partitions(w):
        return w.reshape(-1, 128, w.shape[-1]).transpose(1, 0, 2)

    merge = _np.asarray(L0_xattn_W_merge)
    qkv = _np.stack([_np.asarray(w) for w in (L0_ffn_q_proj, L0_ffn_k_proj, L0_ffn_v_proj)], 2)
    laid = {
        "x": _np.asarray(x),
        "ctx_in": _np.asarray(ctx_1024),
        "mask": _np.asarray(mask_BxSxS2_bk1),
        "merge_t": rows_on_partitions(merge.T).reshape(128, -1),
        "bias": _np.asarray(L0_xattn_b_merge).reshape(1, -1),
        "sim": _np.asarray(L0_ffn_sim_matrix),
        "gates": _np.asarray(L0_ffn_gates),
        "w_qkv": rows_on_partitions(qkv.transpose(1, 0, 2, 3).reshape(D, E * 3 * DH)),
        "w_o": rows_on_partitions(_np.asarray(L0_ffn_o_proj).reshape(E * DH, D)),
    }
    nc = _bacc.Bacc("TRN2", target_bir_lowering=False, num_devices=1)
    arrays, args = {}, []
    for name, a in laid.items():
        a = _np.ascontiguousarray(a)
        arrays[f"in_{name}"] = a
        args.append(nc.dram_tensor(f"in_{name}", a.shape, _mybir.dt.from_np(a.dtype), kind="ExternalInput").ap())
    for i, (shape, dtype) in enumerate(_OUTS):
        dt = _mybir.dt.from_np(_np.dtype(dtype))
        args.append(nc.dram_tensor(f"out_{i}", shape, dt, kind="ExternalOutput").ap())
    cross_attention_then_experts_kernel(nc, *args)
    r = _run(nc, [arrays], core_ids=[0])
    return r.results[0]["out_0"]
```
